# Optimizing a Trainium2 kernel written in Bass

```python
import numpy as np
import jax
import jax.numpy as jnp

def _softmax(x, axis=-1):
    return jax.nn.softmax(x, axis=axis)

def _gelu(x):
    return jax.nn.gelu(x, approximate=True)

def _silu(x):
    return jax.nn.silu(x)

def _sigmoid(x):
    return jax.nn.sigmoid(x)

def _layernorm(x, axis=-1, eps=1e-05):
    m = jnp.mean(x, axis=axis, keepdims=True)
    v = jnp.var(x, axis=axis, keepdims=True)
    return (x - m) / jnp.sqrt(v + eps)

def _scatter_add(tgt, idx, src, axis=0):
    return tgt.at[idx].add(src)

def _segment_sum(src, seg, n):
    return jax.ops.segment_sum(src, seg, n)
kernel_name = 'mk_prb_d2_jaxref_r8_be938a'

def setup_inputs(seed: int=0):
    np.random.seed(seed)
    _w = jnp.asarray

    def _L0_attn_setup():
        import jax, jax.numpy as jnp
        import numpy as np

        def _rope_cos_sin(m, d, dtype=jnp.float32):
            i = jnp.arange(d // 2, dtype=dtype)
            theta = jnp.power(jnp.asarray(10000.0, dtype), -2.0 * (i - 1.0) / d)
            pos = jnp.arange(m, dtype=dtype)
            ang = pos[:, None] * theta[None, :]
            return (jnp.cos(ang), jnp.sin(ang))

        def _rotate(t, cos, sin):
            te = t[..., 0::2]
            to = t[..., 1::2]
            re = te * cos + to * sin
            ro = -te * sin + to * cos
            return jnp.stack((re, ro), axis=-1).reshape(t.shape)
        key = jax.random.key(seed)
        k1, k2, k3, k4 = jax.random.split(key, 4)
        b, m, d = (4, 256, 128)
        scale = 1.0 / np.sqrt(d)
        return {'x': jax.random.normal(k1, (b, m, d), dtype=jnp.float32), 'w_q': jax.random.normal(k2, (d, d), dtype=jnp.float32) * scale, 'w_k': jax.random.normal(k3, (d, d), dtype=jnp.float32) * scale, 'w_v': jax.random.normal(k4, (d, d), dtype=jnp.float32) * scale}
    _L0_attn_in = _L0_attn_setup()

    def _L0_ffn_setup():
        import jax, jax.numpy as jnp
        import numpy as np
        H = 128
        E = 8
        B, S = (4, 256)
        key = jax.random.key(seed)
        k1, k2, k3, k4 = jax.random.split(key, 4)
        x = jax.random.normal(k1, (B, S, H), dtype=jnp.float32)
        wg = jax.random.normal(k2, (H, E), dtype=jnp.float32) * 0.02
        W = jax.random.normal(k3, (E, H, H), dtype=jnp.float32) * 0.02
        b = jax.random.normal(k4, (E, H), dtype=jnp.float32) * 0.02
        return {'x': x, 'wg': wg, 'W': W, 'b': b}
    _L0_ffn_in = _L0_ffn_setup()

    def _L1_attn_setup():
        import jax, jax.numpy as jnp
        import numpy as np
        B, L, D = (2, 1024, 128)
        FILTER_ORDER = 64
        FILTER_HIDDEN = 64

        def positional_embedding(seq_len, emb_dim):
            positions = jnp.arange(seq_len, dtype=jnp.float32)[:, None]
            div_term = jnp.exp(jnp.arange(0, emb_dim, 2, dtype=jnp.float32) * -(jnp.log(10000.0) / emb_dim))
            pe = jnp.zeros((seq_len, emb_dim), jnp.float32)
            pe = pe.at[:, 0::2].set(jnp.sin(positions * div_term))
            pe = pe.at[:, 1::2].set(jnp.cos(positions * div_term))
            return pe

        def causal_fft_conv(v, h):
            seq_len = v.shape[1]
            n = 2 * seq_len
            v_f = jnp.fft.rfft(v, n=n, axis=1)
            h_f = jnp.fft.rfft(h, n=n, axis=0)[None]
            y = jnp.fft.irfft(v_f * h_f, n=n, axis=1)[:, :seq_len, :]
            return y.astype(v.dtype)
        key = jax.random.key(seed)
        ks = jax.random.split(key, 12)
        s = lambda fan_in: 1.0 / np.sqrt(fan_in)
        return {'x': jax.random.normal(ks[0], (B, L, D), dtype=jnp.float32), 'Wu': jax.random.normal(ks[1], (D, D), dtype=jnp.float32) * s(D), 'bu': jnp.zeros((D,), jnp.float32), 'Wv': jax.random.normal(ks[2], (D, D), dtype=jnp.float32) * s(D), 'bv': jnp.zeros((D,), jnp.float32), 'W1': jax.random.normal(ks[3], (FILTER_ORDER, FILTER_HIDDEN), dtype=jnp.float32) * s(FILTER_ORDER), 'b1': jnp.zeros((FILTER_HIDDEN,), jnp.float32), 'W2': jax.random.normal(ks[4], (FILTER_HIDDEN, FILTER_HIDDEN), dtype=jnp.float32) * s(FILTER_HIDDEN), 'b2': jnp.zeros((FILTER_HIDDEN,), jnp.float32), 'W3': jax.random.normal(ks[5], (FILTER_HIDDEN, D), dtype=jnp.float32) * s(FILTER_HIDDEN), 'b3': jnp.zeros((D,), jnp.float32), 'Wo': jax.random.normal(ks[6], (D, D), dtype=jnp.float32) * s(D), 'bo': jnp.zeros((D,), jnp.float32)}
    _L1_attn_in = _L1_attn_setup()

    def _L1_ffn_setup():
        import jax, jax.numpy as jnp
        import numpy as np
        NUM_EXPERTS = 8
        TOP_K = 2
        key = jax.random.key(seed)
        ks = jax.random.split(key, 6)
        B, S, D, H, E = (4, 128, 128, 256, NUM_EXPERTS)
        x = jax.random.normal(ks[0], (B, S, D), dtype=jnp.float32)
        Wg = jax.random.normal(ks[1], (D, E), dtype=jnp.float32) * 0.02
        W1 = jax.random.normal(ks[2], (E, D, H), dtype=jnp.float32) * 0.02
        b1 = jax.random.normal(ks[3], (E, H), dtype=jnp.float32) * 0.02
        W2 = jax.random.normal(ks[4], (E, H, D), dtype=jnp.float32) * 0.02
        b2 = jax.random.normal(ks[5], (E, D), dtype=jnp.float32) * 0.02
        return {'x': x, 'Wg': Wg, 'W1': W1, 'b1': b1, 'W2': W2, 'b2': b2}
    _L1_ffn_in = _L1_ffn_setup()
    _d = {'L0_attn_x': _L0_attn_in['x'], 'L0_attn_w_q': _L0_attn_in['w_q'], 'L0_attn_w_k': _L0_attn_in['w_k'], 'L0_attn_w_v': _L0_attn_in['w_v'], 'L0_ffn_wg': _L0_ffn_in['wg'], 'L0_ffn_W': _L0_ffn_in['W'], 'L0_ffn_b': _L0_ffn_in['b'], 'L1_attn_Wu': _L1_attn_in['Wu'], 'L1_attn_bu': _L1_attn_in['bu'], 'L1_attn_Wv': _L1_attn_in['Wv'], 'L1_attn_bv': _L1_attn_in['bv'], 'L1_attn_W1': _L1_attn_in['W1'], 'L1_attn_b1': _L1_attn_in['b1'], 'L1_attn_W2': _L1_attn_in['W2'], 'L1_attn_b2': _L1_attn_in['b2'], 'L1_attn_W3': _L1_attn_in['W3'], 'L1_attn_b3': _L1_attn_in['b3'], 'L1_attn_Wo': _L1_attn_in['Wo'], 'L1_attn_bo': _L1_attn_in['bo'], 'L1_ffn_Wg': _L1_ffn_in['Wg'], 'L1_ffn_W1': _L1_ffn_in['W1'], 'L1_ffn_b1': _L1_ffn_in['b1'], 'L1_ffn_W2': _L1_ffn_in['W2'], 'L1_ffn_b2': _L1_ffn_in['b2']}
    _x0 = _d['L0_attn_x']
    _d['L0_attn_x'] = jax.random.normal(jax.random.fold_in(jax.random.key(seed), 1), (4, 1024, 128), dtype=_x0.dtype)
    del _x0
    return _d

def reference(L0_attn_x, L0_attn_w_q, L0_attn_w_k, L0_attn_w_v, L0_ffn_wg, L0_ffn_W, L0_ffn_b, L1_attn_Wu, L1_attn_bu, L1_attn_Wv, L1_attn_bv, L1_attn_W1, L1_attn_b1, L1_attn_W2, L1_attn_b2, L1_attn_W3, L1_attn_b3, L1_attn_Wo, L1_attn_bo, L1_ffn_Wg, L1_ffn_W1, L1_ffn_b1, L1_ffn_W2, L1_ffn_b2):

    def _L0_attn_ref(x, w_q, w_k, w_v):
        import jax, jax.numpy as jnp
        import numpy as np

        def _rope_cos_sin(m, d, dtype=jnp.float32):
            i = jnp.arange(d // 2, dtype=dtype)
            theta = jnp.power(jnp.asarray(10000.0, dtype), -2.0 * (i - 1.0) / d)
            pos = jnp.arange(m, dtype=dtype)
            ang = pos[:, None] * theta[None, :]
            return (jnp.cos(ang), jnp.sin(ang))

        def _rotate(t, cos, sin):
            te = t[..., 0::2]
            to = t[..., 1::2]
            re = te * cos + to * sin
            ro = -te * sin + to * cos
            return jnp.stack((re, ro), axis=-1).reshape(t.shape)
        b, m, d = x.shape
        q = jnp.einsum('bmd,ed->bme', x, w_q)
        k = jnp.einsum('bmd,ed->bme', x, w_k)
        v = jnp.einsum('bmd,ed->bme', x, w_v)
        cos, sin = _rope_cos_sin(m, d, x.dtype)
        q_rot = _rotate(q, cos, sin)
        k_rot = _rotate(k, cos, sin)
        scores = jnp.einsum('bqd,bkd->bqk', q_rot, k_rot) / jnp.sqrt(jnp.asarray(d, x.dtype))
        causal = jnp.tril(jnp.ones((m, m), dtype=bool))
        scores = jnp.where(causal[None], scores, jnp.asarray(-jnp.inf, scores.dtype))
        attn = jax.nn.softmax(scores, axis=-1)
        return jnp.einsum('bqk,bkd->bqd', attn, v)

    def _L0_ffn_ref(x, wg, W, b):
        import jax, jax.numpy as jnp
        import numpy as np
        H = 128
        E = 8
        B, S = (4, 256)
        Bb, Ss, Hh = x.shape
        Ee = wg.shape[1]
        T = Bb * Ss
        C = T // Ee
        xt = x.reshape(T, Hh)
        logits = xt @ wg
        probs = jax.nn.softmax(logits, axis=-1)
        idx = jnp.argmax(probs, axis=-1)
        mask = jax.nn.one_hot(idx, Ee, dtype=xt.dtype)
        locations = jnp.cumsum(mask, axis=0) - mask
        mask = mask * (locations < C).astype(xt.dtype)
        gate = jnp.sum(probs * mask, axis=-1)
        loc_s = jnp.sum(locations * mask, axis=-1).astype(jnp.int32)
        loc_oh = jax.nn.one_hot(loc_s, C, dtype=xt.dtype)
        dispatch = mask[:, :, None] * loc_oh[:, None, :]
        combine = gate[:, None, None] * dispatch
        exp_in = jnp.einsum('tec,th->ech', dispatch, xt)
        exp_out = jnp.einsum('ech,efh->ecf', exp_in, W) + b[:, None, :]
        out = jnp.einsum('tec,ecf->tf', combine, exp_out)
        return out.reshape(Bb, Ss, Hh)

    def _L1_attn_ref(x, Wu, bu, Wv, bv, W1, b1, W2, b2, W3, b3, Wo, bo):
        import jax, jax.numpy as jnp
        import numpy as np
        B, L, D = (2, 1024, 128)
        FILTER_ORDER = 64
        FILTER_HIDDEN = 64

        def positional_embedding(seq_len, emb_dim):
            positions = jnp.arange(seq_len, dtype=jnp.float32)[:, None]
            div_term = jnp.exp(jnp.arange(0, emb_dim, 2, dtype=jnp.float32) * -(jnp.log(10000.0) / emb_dim))
            pe = jnp.zeros((seq_len, emb_dim), jnp.float32)
            pe = pe.at[:, 0::2].set(jnp.sin(positions * div_term))
            pe = pe.at[:, 1::2].set(jnp.cos(positions * div_term))
            return pe

        def causal_fft_conv(v, h):
            seq_len = v.shape[1]
            n = 2 * seq_len
            v_f = jnp.fft.rfft(v, n=n, axis=1)
            h_f = jnp.fft.rfft(h, n=n, axis=0)[None]
            y = jnp.fft.irfft(v_f * h_f, n=n, axis=1)[:, :seq_len, :]
            return y.astype(v.dtype)
        seq_len = x.shape[1]
        u = x @ Wu + bu
        v = x @ Wv + bv
        pos_emb = positional_embedding(seq_len, FILTER_ORDER)
        h = jax.nn.gelu(pos_emb @ W1 + b1)
        h = jax.nn.gelu(h @ W2 + b2)
        h = h @ W3 + b3
        t = jnp.arange(seq_len, dtype=jnp.float32)
        decay = jnp.exp(-0.01 * t)[:, None]
        h = h * decay
        v_conv = causal_fft_conv(v, h)
        y = u * v_conv
        y = y @ Wo + bo
        return y

    def _L1_ffn_ref(x, Wg, W1, b1, W2, b2):
        import jax, jax.numpy as jnp
        import numpy as np
        NUM_EXPERTS = 8
        TOP_K = 2
        B, S, D = x.shape
        E, _, H = W1.shape
        OUT = W2.shape[2]
        xm = x.reshape(-1, D)
        logits = xm @ Wg
        probs = jax.nn.softmax(logits, axis=-1)
        topk_p, topk_i = jax.lax.top_k(probs, TOP_K)
        flat_e = topk_i.reshape(-1)
        flat_p = topk_p.reshape(-1)
        order = jnp.argsort(flat_e)
        tok_idx = order // TOP_K
        e_sorted = flat_e[order]
        p_sorted = flat_p[order]
        xs = xm[tok_idx]
        y = jnp.zeros((xs.shape[0], OUT), dtype=xs.dtype)
        for e in range(E):
            h = jax.nn.relu(xs @ W1[e] + b1[e])
            ye = h @ W2[e] + b2[e]
            m = (e_sorted == e)[:, None].astype(xs.dtype)
            y = y + m * ye
        y = y * p_sorted[:, None]
        out = jnp.zeros((B * S, OUT), dtype=y.dtype).at[tok_idx].add(y)
        return out.reshape(B, S, OUT)
    x = L0_attn_x
    xn = _layernorm(x, axis=-1)
    x = x + _L0_attn_ref(xn, L0_attn_w_q, L0_attn_w_k, L0_attn_w_v) + _L0_ffn_ref(xn, L0_ffn_wg, L0_ffn_W, L0_ffn_b)
    xn = _layernorm(x, axis=-1)
    x = x + _L1_attn_ref(xn, L1_attn_Wu, L1_attn_bu, L1_attn_Wv, L1_attn_bv, L1_attn_W1, L1_attn_b1, L1_attn_W2, L1_attn_b2, L1_attn_W3, L1_attn_b3, L1_attn_Wo, L1_attn_bo) + _L1_ffn_ref(xn, L1_ffn_Wg, L1_ffn_W1, L1_ffn_b1, L1_ffn_W2, L1_ffn_b2)
    return x

_drawn_inputs = setup_inputs


def setup_inputs(seed=0):
    import zlib

    import numpy as np

    out = dict(_drawn_inputs(seed))
    spreads = {'L1_attn_bu': (0.0, 0.1),
     'L1_attn_bv': (0.0, 0.1),
     'L1_attn_b1': (0.0, 0.1),
     'L1_attn_b2': (0.0, 0.1),
     'L1_attn_b3': (0.0, 0.1),
     'L1_attn_bo': (0.0, 0.317)}
    factors = {'L0_ffn_b': 7.783,
     'L1_ffn_Wg': 8.0,
     'L1_ffn_W1': 8.0,
     'L1_ffn_b1': 8.0,
     'L1_ffn_W2': 8.0,
     'L1_ffn_b2': 8.0}
    for name, (base, spread) in spreads.items():
        noise = np.random.default_rng([zlib.crc32(name.encode()), seed]).standard_normal(out[name].shape)
        drawn = base * np.exp(spread * noise) if base else spread * noise
        out[name] = jnp.asarray(drawn.astype(out[name].dtype))
    for name, factor in factors.items():
        out[name] = (out[name] * factor).astype(out[name].dtype)
    return out
```

```python
from contextlib import ExitStack

import numpy as np

import concourse.bass as bass
from concourse import mybir

F32 = mybir.dt.float32
BF16 = mybir.dt.bfloat16
I32 = mybir.dt.int32
ALU = mybir.AluOpType
ACT = mybir.ActivationFunctionType
X = mybir.AxisListType.X

P = 128
D = 128
B, L = 4, 1024
T = B * L
NT = T // P
J = L // P
E = 8
CAP = T // E
H1 = 256
ROWW = D + 1
SLOTS0 = E * CAP
TILES0 = SLOTS0 // P
UNROLL = 8
TILES1 = -(-(2 * T // P + E - 1) // UNROLL) * UNROLL
SLOTS1 = TILES1 * P
FAR = 65536.0
FO = 64
KS = (0, 4, 2, 10, 1, 9, 5, 13)
NC = len(KS)
NFFT = 2 * L
RC = float(np.sqrt(0.5))
TC = float(np.cos(np.pi / 8))
TAU = float(np.tan(np.pi / 8))
HALF = 2
W = (B // HALF) * D
VGW = D + E
SCALE = float(D) ** -0.5

CONST = {}


def _const_columns():
    at = 0
    for name, n in (("ident", P), ("before", P), ("mask", P), ("rank", E * NT), ("e_cap", E * NT),
                    ("carry", E * NT), ("decay", J), ("minus_half", J), ("tile_no", TILES1 * E),
                    ("token", NT), ("token2", NT), ("token2b", NT)):
        CONST[name] = (at, at + n)
        at += n
    return at


NCONST = _const_columns()


def dft_matrices():
    t = np.arange(P)
    fw = np.zeros((NC, 4, P, P))
    iv = np.zeros((NC, 4, P, P))
    for c, k1 in enumerate(KS):
        if c == 0:
            continue
        th = 2 * np.pi * ((t[:, None] * (k1 + 16 * t[None, :])) % NFFT) / NFFT
        co, si = np.cos(th), np.sin(th)
        fw[c] = co, -si, si, co
        iv[c] = co.T, si.T, -si.T, co.T
        iv[c] *= 2 / NFFT
    h = np.arange(P // 2)
    th0 = 2 * np.pi * ((t[:, None] * 16 * h[None, :]) % NFFT) / NFFT
    th8 = 2 * np.pi * ((t[:, None] * (8 + 16 * h[None, :])) % NFFT) / NFFT
    fw[0, 0, :, :64] = np.cos(th0)
    fw[0, 1, :, 64:] = np.cos(th8)
    fw[0, 2, :, :64] = np.sin(th0)
    fw[0, 2, :, 0] = (-1.0) ** t
    fw[0, 3, :, 64:] = np.sin(th8)
    iv[0, 0, :64] = 2 * np.cos(th0).T
    iv[0, 0, 0] = 1
    iv[0, 1, :64] = 2 * np.sin(th0).T
    iv[0, 1, 0] = (-1.0) ** t
    iv[0, 2, 64:] = 2 * np.cos(th8).T
    iv[0, 3, 64:] = 2 * np.sin(th8).T
    iv[0] /= NFFT
    lay = lambda m: np.ascontiguousarray(m.transpose(2, 0, 1, 3).reshape(P, -1), np.float32)
    return lay(fw), lay(iv)


def rope_tables():
    theta = np.float32(10000.0 ** (-2.0 * (np.arange(D // 2) - 1.0) / D))
    ang = np.arange(L, dtype=np.float32)[:, None] * theta.astype(np.float32)[None, :]
    ang = ang.astype(np.float64)
    co = np.repeat(np.cos(ang), 2, axis=1).T
    si = np.repeat(np.sin(ang), 2, axis=1).T * np.where(np.arange(D) % 2, -1.0, 1.0)[:, None]
    return np.ascontiguousarray(np.stack([co, si], 1).reshape(P, -1), np.float32)


def position_table():
    pos = np.arange(L, dtype=np.float32)[:, None]
    div = np.exp(np.arange(0, FO, 2, dtype=np.float32) * np.float32(-(np.log(np.float32(10000.0)) / np.float32(FO))),
                 dtype=np.float64).astype(np.float32)
    ang = (pos * div.astype(np.float32)).astype(np.float32).astype(np.float64)
    pe = np.zeros((L, FO), np.float32)
    pe[:, 0::2] = np.sin(ang)
    pe[:, 1::2] = np.cos(ang)
    return np.ascontiguousarray(pe.T)


def constants():
    c = np.zeros((P, NCONST), np.float32)
    p = np.arange(P)
    put = lambda name, v: c.__setitem__((slice(None), slice(*CONST[name])), np.broadcast_to(v, (P, CONST[name][1] - CONST[name][0])))
    put("ident", np.eye(P))
    put("before", (p[:, None] < p[None, :]))
    put("mask", np.where(p[None, :] > p[:, None], -1e38, 0.0))
    e = np.arange(E)
    put("rank", np.repeat(E - e, NT))
    put("e_cap", np.repeat(e * CAP, NT))
    put("carry", np.tile(np.arange(NT) > 0, E))
    t = np.arange(L, dtype=np.float32).reshape(J, P).T
    put("decay", 0.5 * np.exp(np.float32(-0.01) * t))
    put("minus_half", -0.5)
    put("tile_no", np.repeat(np.arange(TILES1), E))
    token = np.arange(T).reshape(NT, P).T
    c = c.view(np.int32)
    for name, v in (("token", token), ("token2", 2 * token), ("token2b", 2 * token + 1)):
        c[:, slice(*CONST[name])] = v
    return c.view(np.float32)


R0_REL, R0_OH, R0_CUM = 2, 6, 11
R1_REL, R1_M2, R1_OH, R1_CUM = 17, 22, 27, 33
RAD_F = 22
N_FILL = (TILES0 + TILES1 + NT) // 8
N_L1W = 2 + E + 7
MOE0_AT = 2 * J - 1


def two_layer_kernel(nc, x_in, cst_in, rope_in, fw_in, iv_in, pe_in, wqk_in, wvg_in, w0_in, b0_in,
                     f1w_in, f1b_in, f2w_in, f2b_in, f3_in, wv_in, wu_in, wg1_in, bu_in, bv_in, wo_in,
                     bo_in, w1_in, b1_in, w2_in, b2_in, out):
    ctx = ExitStack()
    with ctx:
        def sb(name, shape, dt=F32):
            return ctx.enter_context(nc.sbuf_tensor(name, shape, dt))

        def ps(name, shape):
            return ctx.enter_context(nc.psum_tensor(name, shape, F32))

        def sem(name):
            return ctx.enter_context(nc.semaphore(name))

        slots0 = nc.dram_tensor("slots0", (SLOTS0, ROWW), F32, kind="Internal").ap()
        slots1 = nc.dram_tensor("slots1", (SLOTS1, ROWW), F32, kind="Internal").ap()
        moe0 = nc.dram_tensor("moe0", (T, D), F32, kind="Internal").ap()
        moe1 = nc.dram_tensor("moe1", (2 * T, D), F32, kind="Internal").ap()

        xres = sb("xres", [P, NT, D])
        row = sb("row", [P, NT, ROWW])
        xT = sb("xT", [P, T])
        cst = sb("cst", [P, NCONST])
        identb = sb("identb", [P, P], BF16)
        beforeb = sb("beforeb", [P, P], BF16)
        maskb = sb("maskb", [P, P], BF16)
        onesb = sb("onesb", [P, P], BF16)
        w0 = sb("w0", [P, E, D])
        bmoe = sb("bmoe", [P, E, D])
        w1 = sb("w1", [P, E, H1 + 2])
        w2 = sb("w2", [P, E, 2 * D])
        wv = sb("wv", [P, D])
        wu = sb("wu", [P, D])
        wg1 = sb("wg1", [P, E])
        wo = sb("wo", [P, D])
        bu = sb("bu", [P, D])
        bv = sb("bv", [P, D])
        bo = sb("bo", [P, D])
        mats = sb("mats", [P, NC, 4, P])
        hspec = sb("hspec", [P, NC, 2, D])
        hspec0 = sb("hspec0", [P, 2, 2, D])
        stats = sb("stats", [P, NT, 6])
        mv = sb("mv", [P, NT, 2])
        rstd = sb("rstd", [P, NT])
        veps = sb("veps", [P, NT])
        xs = sb("xs", [P, UNROLL, ROWW])
        ys = sb("ys", [P, UNROLL, D])
        xsT = sb("xsT", [P, 2, P])
        hT = sb("hT", [P, 2, 2, P])
        w1r = sb("w1r", [P, 2, H1 + 2])
        lg = sb("lg", [P, E, NT])
        rel = sb("rel", [P, E, NT])
        score = sb("score", [P, E, NT])
        expl = sb("expl", [P, E, NT])
        oh1 = sb("oh1", [P, E, NT])
        oh2 = sb("oh2", [P, E, NT])
        ohb = sb("ohb", [P, E, NT], BF16)
        cum = sb("cum", [P, E, NT])
        m1 = sb("m1", [P, NT])
        m2 = sb("m2", [P, NT])
        best = sb("best", [P, NT])
        gate0 = sb("gate0", [P, NT])
        gate1 = sb("gate1", [P, NT])
        gate2 = sb("gate2", [P, NT])
        em2 = sb("em2", [P, NT])
        slot0 = sb("slot0", [P, NT], I32)
        slot1 = sb("slot1", [P, NT], I32)
        slot2 = sb("slot2", [P, NT], I32)
        cnt_i = sb("cnt_i", [P, E], I32)
        cnt_t = sb("cnt_t", [P, E], I32)
        ntile = sb("ntile", [P, E])
        ctile = sb("ctile", [P, E])
        base = sb("base", [P, E])
        ones8 = sb("ones8", [P, E])
        ecmp = sb("ecmp", [1, TILES1, E])
        ecnt = sb("ecnt", [1, TILES1])
        expert = sb("expert", [1, TILES1], I32)

        WORK = 17200
        work = sb("work", [P, WORK])
        place = [0]

        def part(n, shape=None, **kw):
            a = work[:, place[0]:place[0] + n]
            place[0] += n
            assert place[0] <= WORK
            return a.rearrange(shape, **kw) if shape else a

        rope = part(2 * L, "p (a m) -> p a m", a=2)
        wqk = part(4 * D, "p (a e) -> p a e", a=4)
        wvg = part(VGW)
        vsb = part(NT * D, "p (i d) -> p i d", d=D)
        negmax = part(NT)
        rsum = part(NT)
        rrec = part(NT)
        y0 = part(J * D, "p (j d) -> p j d", d=D)
        shared = place[0]
        qk = [part(2 * L, "p (a m) -> p a m", a=2) for _ in range(2)]
        rtmp = part(2 * 512, "p (a m) -> p a m", a=2)
        prob = [part(L) for _ in range(2)]
        pT = [part(L, "p (j q) -> p j q", q=P) for _ in range(2)]
        place[0] = shared
        hx = part(L)
        ht = part(L)
        hg = part(L)
        pe_sb = part(L)
        fw_small = part(2 * FO + D + 2)
        filt_v = part(J * D, "p (j w) -> p j w", w=D)
        filt_spec = part(NC * 2 * D, "p (c a w) -> p c a w", a=2, w=D)
        filt_pm = hx.rearrange("p (a j w) -> p a j w", a=2, w=D)
        filt_ej = ht[:, 0:4 * D].rearrange("p (s x w) -> p s x w", s=2, w=D)
        filt_uv = hg[:, 0:4 * D].rearrange("p (s a w) -> p s a w", s=2, w=D)
        f1w, f2w = fw_small[0:FO, 0:FO], fw_small[0:FO, FO:2 * FO]
        f3w = fw_small[0:FO + 1, 2 * FO:2 * FO + D]
        f1b, f2b = fw_small[0:FO, 2 * FO + D:2 * FO + D + 1], fw_small[0:FO, 2 * FO + D + 1:2 * FO + D + 2]
        place[0] = 0
        uu = part(NT * D, "p (i d) -> p i d", d=D)
        vv = [part(J * W, "p (j w) -> p j w", w=W) for _ in range(HALF)]
        spec0 = part(NC * 2 * W)
        spec = [a.rearrange("p (c a w) -> p c a w", a=2, w=W) for a in (spec0, xT[:, :])]
        moe_back = [spec0[:, n * 1024:(n + 1) * 1024].rearrange("p (i k d) -> p i k d", k=2, d=D) for n in range(4)]
        pmf = part(8 * W)
        pm = pmf.rearrange("p (a j w) -> p a j w", a=2, w=W)
        prod = pmf.rearrange("p (n a w) -> p n a w", n=4, w=W)
        ej = part(4 * W, "p (s x w) -> p s x w", s=2, w=W)
        uv = part(4 * W, "p (s a w) -> p s a w", s=2, w=W)

        S = [ps(f"psS{n}", [P, 2, 512]) for n in range(2)]
        TP = [ps(f"psT{n}", [P, 512]) for n in range(2)]
        O = [ps(f"psO{n}", [P, 512]) for n in range(2)]
        SB = [S[0][:, 0, :], S[0][:, 1, :], S[1][:, 0, :], S[1][:, 1, :]]
        TO = [TP[0][:, :], TP[1][:, :], O[0][:, :], O[1][:, :]]

        def col(name, shape=None, **kw):
            a = cst[:, CONST[name][0]:CONST[name][1]]
            return a.rearrange(shape, **kw) if shape else a

        def ei(a):
            return a[:, :, :].rearrange("p e i -> p i e")

        def flat(a):
            return a[:, :, :].rearrange("p e i -> p (e i)")

        def over_e(a):
            return a[:, :].unsqueeze(1).to_broadcast([P, E, NT])

        ident = col("ident")

        x_loaded = [sem(f"x_loaded{g}") for g in range(B)]
        cst_loaded = sem("cst_loaded")
        w_a_loaded = sem("w_a_loaded")
        filt_loaded = sem("filt_loaded")
        fw_loaded = sem("fw_loaded")
        rope_loaded = sem("rope_loaded")
        moe0_w_loaded = sem("moe0_w_loaded")
        l1_w_loaded = sem("l1_w_loaded")
        b2_loaded = sem("b2_loaded")
        iv_loaded = [sem(f"iv_loaded{c}") for c in range(NC)]
        fill_ready = sem("fill_ready")
        prefilled = sem("prefilled")
        casts_done = sem("casts_done")
        ones_done = sem("ones_done")
        ids_done = sem("ids_done")
        stats_done = sem("stats_done")
        aggr_done = sem("aggr_done")
        veps_done = sem("veps_done")
        rstd_done = sem("rstd_done")
        xn_done = sem("xn_done")
        tr_full = sem("tr_full")
        tr_free = sem("tr_free")
        vg_full = sem("vg_full")
        vg_free = sem("vg_free")
        f_full = sem("f_full")
        f_act = sem("f_act")
        f_dve = sem("f_dve")
        fs_full = sem("fs_full")
        fs_free = sem("fs_free")
        hspec_done = sem("hspec_done")
        rt = sem("rt")
        rt_exp = sem("rt_exp")
        rt_mm = sem("rt_mm")
        slot0_ready = sem("slot0_ready")
        sent0 = sem("sent0")
        pr_full = sem("pr_full")
        rope_mul = sem("rope_mul")
        rope_done = sem("rope_done")
        s_full = sem("s_full")
        max_done = sem("max_done")
        exp_done = sem("exp_done")
        bias_done = sem("bias_done")
        pt_full = sem("pt_full")
        pt_act = sem("pt_act")
        pt_dve = sem("pt_dve")
        o_full = sem("o_full")
        rrec_done = sem("rrec_done")
        o_done = sem("o_done")
        xs_loaded = [[sem(f"xs_loaded{l}_{m}") for m in range(UNROLL)] for l in range(2)]
        sent_back = [[sem(f"sent_back{l}_{m}") for m in range(UNROLL)] for l in range(2)]
        e_t = [sem(f"e_t{l}") for l in range(2)]
        e_xT = [sem(f"e_xT{l}") for l in range(2)]
        e_y = [sem(f"e_y{l}") for l in range(2)]
        e_ys = [sem(f"e_ys{l}") for l in range(2)]
        e_w1 = sem("e_w1")
        e_h = sem("e_h")
        e_ha = sem("e_ha")
        e_hd = sem("e_hd")
        y0_loaded = sem("y0_loaded")
        y0_used = sem("y0_used")
        uvg_full = sem("uvg_full")
        v_done = sem("v_done")
        u_done = sem("u_done")
        lg1_done = sem("lg1_done")
        bo_done = sem("bo_done")
        slot1_ready = sem("slot1_ready")
        expert_ready = sem("expert_ready")
        sent1 = sem("sent1")
        ids2_done = sem("ids2_done")
        rad = sem("rad")
        x_full = sem("x_full")
        pmul = sem("pmul")
        x_free = sem("x_free")
        y_ready = sem("y_ready")
        b_full = sem("b_full")
        b_free = sem("b_free")
        conv_done = sem("conv_done")
        yt_full = sem("yt_full")
        yt_free = sem("yt_free")
        wo_full = sem("wo_full")
        wo_done = sem("wo_done")
        back_loaded = [sem(f"back_loaded{n}") for n in range(4)]
        out_a = sem("out_a")
        out_ready = sem("out_ready")
        stored = sem("stored")

        NPT = sum((i + 4) // 4 for i in range(J))

        def pt_uses():
            return [(n, c, min(4, n % J + 1 - 4 * c)) for n in range(NT) for c in range((n % J + 4) // 4)]

        PT = pt_uses()
        PT_OF = {(n, c): u for u, (n, c, _) in enumerate(PT)}
        PT_ACT = {u: k for k, u in enumerate(u for u, (_, c, _) in enumerate(PT) if c == 0)}
        PT_DVE = {u: k for k, u in enumerate(u for u, (_, c, _) in enumerate(PT) if c == 1)}

        def wait_pt_free(eng, u):
            if u >= 2:
                if u - 2 in PT_ACT:
                    eng.wait_ge(pt_act, PT_ACT[u - 2] + 1)
                else:
                    eng.wait_ge(pt_dve, PT_DVE[u - 2] + 1)

        S_USES = [("pr", u) for u in range(4)] + [("s", 0)]
        for n in range(NT):
            if n % J == 4 and n // J + 1 < B:
                S_USES += [("pr", 4 * (n // J + 1) + u) for u in range(4)]
            if n + 1 < NT:
                S_USES.append(("s", n + 1))
        LAST_S, seen = {}, {}
        for use in S_USES:
            slot = use[1] % 2 if use[0] == "s" else (use[1] + 1) % 2
            LAST_S[use] = seen.get(slot)
            seen[slot] = use

        block = ctx.enter_context(nc.Block())

        @block.sync
        def _(sp):
            xv = x_in.rearrange("b (j p) d -> b p j d", p=P)
            for g in range(B):
                sp.dma_start(xres[:, J * g:J * (g + 1), :], xv[g]).then_inc(x_loaded[g], 16)
                if g == 0:
                    sp.dma_start(cst[:, :], cst_in).then_inc(cst_loaded, 16)
                    sp.dma_start(wvg, wvg_in).then_inc(w_a_loaded, 16)
            for a, b in ((pe_sb[0:FO, :], pe_in), (f1w, f1w_in), (f1b, f1b_in), (f2w, f2w_in),
                         (f2b, f2b_in), (f3w, f3_in)):
                sp.dma_start(a, b).then_inc(filt_loaded, 16)
            sp.dma_start(mats[:, :, :, :], fw_in).then_inc(fw_loaded, 16)
            sp.dma_start(wqk, wqk_in).then_inc(rope_loaded, 16)
            sp.dma_start(rope, rope_in).then_inc(rope_loaded, 16)
            sp.dma_start(w0[:, :, :], w0_in).then_inc(moe0_w_loaded, 16)
            sp.dma_start(bmoe[:, :, :], b0_in.rearrange("e d -> (e d)").partition_broadcast(P)).then_inc(moe0_w_loaded, 16)
            sp.wait_ge(fill_ready, 2)
            for dst, n in ((slots0, TILES0), (slots1, TILES1)):
                for i in range(0, n, 8):
                    sp.dma_start(dst[i * P:(i + 8) * P, :].rearrange("(i p) w -> p i w", p=P),
                                 xs[:, :, :]).then_inc(prefilled, 16)
            for i in range(0, NT, 8):
                sp.dma_start(moe0[i * P:(i + 8) * P, :].rearrange("(i p) w -> p i w", p=P),
                             xs[:, :, 0:D]).then_inc(prefilled, 16)
            for a, b in ((w1[:, :, 0:H1], w1_in.rearrange("e d h -> d e h")), (w1[:, :, H1:H1 + 2], b1_in),
                         (w2[:, :, :].rearrange("p e (f o) -> p e f o", f=2), w2_in.rearrange("e (f p) o -> p e f o", p=P)),
                         (wv[:, :], wv_in), (wu[:, :], wu_in), (wg1[:, :], wg1_in), (wo[:, :], wo_in),
                         (bu[:, :], bu_in.partition_broadcast(P)), (bv[:, :], bv_in.partition_broadcast(P)),
                         (bo[:, :], bo_in.partition_broadcast(P))):
                for e in (range(E) if b.ndim == 4 else [None]):
                    sp.dma_start(a if e is None else a[:, e], b if e is None else b[:, e]).then_inc(l1_w_loaded, 16)

            def expert_rows(l, src, n_iter):
                for m in range(UNROLL):
                    sp.dma_start(xs[:, m, :], src[m * P:(m + 1) * P, :]).then_inc(xs_loaded[l][m], 16)
                with sp.Fori(1, n_iter) as it:
                    for m in range(UNROLL):
                        sp.wait_ge(sent_back[l][m], it * 16)
                        n = it * UNROLL + m
                        sp.dma_start(xs[:, m, :], src[bass.ds(n * P, P), :]).then_inc(xs_loaded[l][m], 16)

            sp.wait_ge(prefilled, 16 * N_FILL)
            sp.wait_ge(sent0, 16 * NT)
            expert_rows(0, slots0, TILES0 // UNROLL)
            for m in range(UNROLL):
                sp.wait_ge(sent_back[0][m], 16 * (TILES0 // UNROLL))
            sp.dma_start(bmoe[:, :, :], b2_in.rearrange("e d -> (e d)").partition_broadcast(P)).then_inc(b2_loaded, 16)
            for g in range(B):
                if g:
                    sp.wait_ge(y0_used, g)
                sp.dma_start(y0, moe0[g * L:(g + 1) * L, :].rearrange("(j p) d -> p j d", p=P)).then_inc(y0_loaded, 16)
            for c in range(NC):
                sp.wait_ge(x_full, NC + c + 1)
                sp.dma_start(mats[:, c, :, :], iv_in[:, c * 4 * P:(c + 1) * 4 * P]).then_inc(iv_loaded[c], 16)
            sp.wait_ge(sent1, 2 * 16 * NT)
            expert_rows(1, slots1, TILES1 // UNROLL)
            for m in range(UNROLL):
                sp.wait_ge(sent_back[1][m], 16 * (TILES1 // UNROLL))
            for q in range(NT // 4):
                if q >= 4:
                    sp.wait_ge(out_ready, q - 3)
                sp.dma_start(moe_back[q % 4], moe1[q * 1024:(q + 1) * 1024, :].rearrange(
                    "(i p k) d -> p i k d", p=P, k=2)).then_inc(back_loaded[q % 4], 16)
            ov = out.rearrange("b (j p) d -> p (b j) d", p=P)
            for q in range(NT // 4):
                sp.wait_ge(out_ready, q + 1)
                sp.dma_start(ov[:, 4 * q:4 * q + 4, :], xres[:, 4 * q:4 * q + 4, :]).then_inc(stored, 16)
            sp.wait_ge(stored, 16 * (NT // 4))

        @block.gpsimd
        def _(pool):
            pool.memset(xs[:, :, 0:D], 0.0).then_inc(fill_ready, 1)
            pool.memset(xs[:, :, D:ROWW].bitcast(I32), 1 << 24).then_inc(fill_ready, 1)
            pool.memset(onesb[:, :], 1.0).then_inc(ones_done, 1)
            pool.memset(ones8[:, :], 1.0).then_inc(ones_done, 1)
            pool.wait_ge(cst_loaded, 16)
            ids = row[:, :, D:ROWW].rearrange("p i w -> p (i w)").bitcast(I32)
            pool.tensor_copy(ids, col("token").bitcast(I32)).then_inc(ids_done, 1)

            def inverse_std(k):
                g = slice(J * (k % B), J * (k % B) + J)
                pool.wait_ge(aggr_done, J * (k + 1))
                pool.tensor_scalar(veps[:, g], mv[:, g, 1], 1e-5, None, ALU.add).then_inc(veps_done, 1)
                pool.wait_ge(veps_done, k + 1)
                pool.tensor_tensor(rstd[:, g], veps[:, g], col("minus_half"), ALU.pow).then_inc(rstd_done, 1)

            def scatter_rows(dst, slots, bound, done, tiles=range(NT)):
                for i in tiles:
                    pool.indirect_dma_start(dst[:, :], bass.IndirectOffsetOnAxis(ap=slots[:, i:i + 1], axis=0),
                                            row[:, i, :], None, bounds_check=bound,
                                            oob_is_err=False).then_inc(done, 16)

            def rope_add(b):
                for u in range(4):
                    n = 4 * b + u
                    pool.wait_ge(rope_mul, 2 * (n + 1))
                    o = qk[b % 2][:, u % 2, 512 * (u // 2):512 * (u // 2) + 512]
                    pool.tensor_tensor(o, o, rtmp[:, n % 2, :], ALU.add).then_inc(rope_done, 1)

            def expert_back(l, dst, bound, n_iter):
                for n in range(UNROLL * n_iter):
                    m = n % UNROLL
                    pool.wait_ge(e_ys[l], n + 1)
                    pool.wait_ge(xs_loaded[l][m], (n // UNROLL) * 16 + 16)
                    pool.indirect_dma_start(
                        dst[:, :], bass.IndirectOffsetOnAxis(ap=xs[:, m, D:ROWW].bitcast(I32), axis=0),
                        ys[:, m, :], None, bounds_check=bound, oob_is_err=False).then_inc(sent_back[l][m], 16)

            for k in range(B):
                inverse_std(k)
            pool.wait_ge(xn_done, NT)
            pool.wait_ge(ids_done, 1)
            pool.wait_ge(prefilled, 16 * N_FILL)
            pool.wait_ge(slot0_ready, 1)
            rope_add(0)
            scatter_rows(slots0, slot0, SLOTS0 - 1, sent0, range(NT // 2))
            rope_add(1)
            scatter_rows(slots0, slot0, SLOTS0 - 1, sent0, range(NT // 2, NT))
            rope_add(2)
            expert_back(0, moe0, T - 1, TILES0 // UNROLL)
            rope_add(3)

            pool.wait_ge(sent0, 16 * NT)
            for k in range(B, 2 * B):
                inverse_std(k)
            pool.tensor_copy(ids, col("token2").bitcast(I32)).then_inc(ids_done, 1)
            pool.wait_ge(xn_done, 2 * NT)
            pool.wait_ge(l1_w_loaded, 16 * N_L1W)
            pool.tensor_tensor(xres[:, :, :], xres[:, :, :],
                               bo[:, :].unsqueeze(1).to_broadcast([P, NT, D]), ALU.add).then_inc(bo_done, 1)
            pool.wait_ge(ids_done, 2)
            pool.wait_ge(slot1_ready, 2)
            scatter_rows(slots1, slot1, SLOTS1 - 1, sent1)
            pool.wait_ge(sent1, 16 * NT)
            pool.tensor_copy(ids, col("token2b").bitcast(I32)).then_inc(ids_done, 1)
            pool.wait_ge(ids_done, 3)
            scatter_rows(slots1, slot2, SLOTS1 - 1, sent1)
            expert_back(1, moe1, 2 * T - 1, TILES1 // UNROLL)

        @block.scalar
        def _(act):
            act.wait_ge(cst_loaded, 16)
            for o, name in ((identb, "ident"), (beforeb, "before"), (maskb, "mask")):
                act.activation(o[:, :], col(name), ACT.Copy).then_inc(casts_done, 1)

            def take_transposes(k0):
                for u in range(2):
                    act.wait_ge(tr_full, k0 + u + 1)
                    act.activation(xT[:, 512 * ((k0 + u) % 8):512 * ((k0 + u) % 8) + 512], TP[u][:, :],
                                   ACT.Copy).then_inc(tr_free, 1)

            for g in range(B):
                take_transposes(2 * g)
                for u in range(4):
                    n = 4 * g + u
                    i = 2 * n
                    act.wait_ge(vg_full, n + 1)
                    pv = O[n % 2][:, 0:2 * VGW].rearrange("p (i w) -> p i w", w=VGW)
                    act.activation(vsb[:, i:i + 2, :], pv[:, :, 0:D], ACT.Copy)
                    act.activation(lg[:, :, i:i + 2].rearrange("p e i -> p i e"), pv[:, :, D:VGW],
                                   ACT.Copy).then_inc(vg_free, 1)

            for k, (fb, sc) in enumerate(((f1b, 1.0), (f2b, 0.5))):
                act.wait_ge(filt_loaded, 96)
                act.wait_ge(f_full, k + 1)
                act.activation(hx[0:FO, :], S[k][0:FO, :, :].rearrange("p a m -> p (a m)"), ACT.Identity,
                               bias=fb, scale=sc).then_inc(f_act, 1)
                act.wait_ge(f_dve, 4 * k + 3)
                act.activation(hg[0:FO, :], ht[0:FO, :], ACT.Tanh, scale=float(np.sqrt(2 / np.pi))).then_inc(f_act, 1)
                if k == 0:
                    act.wait_ge(rt, R0_REL)
                    act.activation(flat(expl), flat(rel), ACT.Exp).then_inc(rt_exp, 1)
            for u in range(4):
                act.wait_ge(fs_full, u + 1)
                act.activation(hspec[:, 2 * u:2 * u + 2, :, :].rearrange("p c a d -> p (c a d)"),
                               TO[u][:, :], ACT.Copy).then_inc(fs_free, 1)
            act.wait_ge(fs_free, 4)
            for a in range(2):
                act.activation(hspec0[:, a, :, :], hspec[:, 0, a, :].unsqueeze(1).to_broadcast([P, 2, D]),
                               ACT.Copy).then_inc(hspec_done, 1)
            act.wait_ge(hspec_done, 2)
            act.activation(hspec0[0:1, 0, 1, :], hspec[0:1, 0, 1, :], ACT.Copy).then_inc(hspec_done, 1)

            def exp_rows(n):
                i = n % J
                act.wait_ge(bias_done, n + 1)
                if n >= 2:
                    act.wait_ge(pt_full, PT_OF[(n - 2, (i - 2) % J // 4)] + 1)
                act.activation(prob[n % 2][:, 0:(i + 1) * P],
                               S[n % 2][:, :, :].rearrange("p a m -> p (a m)")[:, 0:(i + 1) * P], ACT.Exp,
                               bias=negmax[:, n:n + 1], scale=SCALE,
                               accum_out=rsum[:, n:n + 1]).then_inc(exp_done, 1)

            def take_pt(n):
                u = PT_OF[(n, 0)]
                act.wait_ge(pt_full, u + 1)
                if n >= 2:
                    act.wait_ge(o_full, n - 1)
                k = min(4, n % J + 1)
                act.activation(pT[n % 2][:, 0:k, :].rearrange("p j q -> p (j q)"), TP[u % 2][:, 0:k * P],
                               ACT.Copy).then_inc(pt_act, 1)

            def expert_act(l, n_iter):
                with act.Fori(0, n_iter) as it:
                    for m in range(UNROLL):
                        n = it * UNROLL + m
                        act.wait_ge(e_t[l], n + 1)
                        act.activation(xsT[:, m % 2, :], TP[m % 2][:, 0:P], ACT.Copy).then_inc(e_xT[l], 1)
                        if l == 1:
                            act.wait_ge(e_h, n + 1)
                            act.activation(hT[:, m % 2, 0, :], S[m % 2][:, 0, 0:P], ACT.Relu,
                                           bias=w1r[:, m % 2, H1:H1 + 1]).then_inc(e_ha, 1)

            exp_rows(0)
            for n in range(NT):
                take_pt(n)
                if n == MOE0_AT:
                    expert_act(0, TILES0 // UNROLL)
                if n + 1 < NT:
                    exp_rows(n + 1)

            for g in range(B):
                take_transposes(2 * B + 2 * g)
            for q in range(NT // 4):
                act.wait_ge(uvg_full, q + 1)
                act.activation(lg[:, :, 4 * q:4 * q + 4].rearrange("p e i -> p i e"),
                               O[q % 2][:, 0:4 * E].rearrange("p (i e) -> p i e", e=E), ACT.Copy).then_inc(lg1_done, 1)
            act.wait_ge(rt, R1_REL)
            act.activation(flat(expl), flat(rel), ACT.Exp).then_inc(rt_exp, 1)
            act.wait_ge(rt, R1_M2)
            act.activation(em2[:, :], m2[:, :], ACT.Exp).then_inc(rt_exp, 1)
            for u in range(2 * NC):
                act.wait_ge(b_full, u + 1)
                act.activation(spec[u // NC][:, u % NC, :, :].rearrange("p a w -> p (a w)"), TO[u % 4],
                               ACT.Copy).then_inc(b_free, 1)
            for q in range(NT // 4):
                act.wait_ge(yt_full, q + 1)
                act.activation(xT[:, 512 * q:512 * q + 512], TP[q % 2][:, :], ACT.Copy).then_inc(yt_free, 1)
            expert_act(1, TILES1 // UNROLL)

        @block.tensor
        def _(pe):
            def mm(o, lhsT, rhs, start=True, stop=True):
                return pe.matmul(o, lhsT, rhs, start=start, stop=stop)

            def transpose_tokens(k):
                for u in range(2):
                    n = 2 * k + u
                    if n >= 2:
                        pe.wait_ge(tr_free, n - 1)
                    for q in range(4):
                        i = 4 * (n % 8) + q
                        pe.wait_ge(xn_done, NT * (k // B) + i + 1)
                        last = pe.transpose(TP[u][:, q * P:(q + 1) * P], row[:, i, 0:D], ident)
                    last.then_inc(tr_full, 1)

            def values_and_gates(g):
                for u in range(4):
                    n = 4 * g + u
                    pe.wait_ge(tr_free, 2 * g + u // 2 + 1)
                    if n >= 2:
                        pe.wait_ge(vg_free, n - 1)
                    for q in range(2):
                        i = 2 * n + q
                        last = mm(O[n % 2][:, q * VGW:(q + 1) * VGW], xT[:, i * P:(i + 1) * P], wvg)
                    last.then_inc(vg_full, 1)

            def routing_counts(k):
                pe.wait_ge(rt, (R0_OH, R1_OH)[k])
                oh = ohb[:, :, :].rearrange("p e i -> p (e i)")
                mm(O[0][:, 0:E * NT], beforeb[:, :], oh)
                mm(O[0][:, E * NT:2 * E * NT], onesb[:, :], oh).then_inc(rt_mm, 1)

            def filter_network():
                pe.wait_ge(filt_loaded, 96)
                for k in range(2):
                    if k:
                        pe.wait_ge(f_dve, 4)
                    for h in range(2):
                        r = (pe_sb[0:FO, :], hg[0:FO, :])[k][:, 512 * h:512 * h + 512]
                        last = mm(S[k][0:FO, h, :], (f1w, f2w)[k], r)
                    last.then_inc(f_full, 1)
                    if k == 0:
                        routing_counts(0)
                pe.wait_ge(f_dve, 9)
                for j in range(J):
                    last = mm(S[0][:, j // 4, (j % 4) * P:(j % 4) * P + P], hg[0:FO + 1, j * P:(j + 1) * P], f3w)
                last.then_inc(f_full, 1)

            def dft(o, a, c, s):
                for n in range(2):
                    mm(o[n], mats[:, c, 2 * n, :], a[:, 0, :], stop=False)
                    last = mm(o[n], mats[:, c, 2 * n + 1, :], a[:, 1, :], start=False)
                last.then_inc(s, 1) if s else None

            def filter_spectrum():
                pe.wait_ge(fw_loaded, 16)
                pe.wait_ge(rad, RAD_F)
                for c in range(NC):
                    o = TO[c // 2][:, 256 * (c % 2):256 * (c % 2) + 256].rearrange("p (a w) -> p a w", a=2)
                    dft([o[:, 0, :], o[:, 1, :]], filt_spec[:, c, :, :], c, fs_full if c % 2 else None)

            def project(b):
                for u in range(4):
                    n = 4 * b + u
                    slot = S[(n + 1) % 2]
                    wait_scores_bank(("pr", n))
                    for a in range(2):
                        last = mm(slot[:, a, :], wqk[:, 2 * (u % 2) + a, :],
                                  xT[:, b * L + 512 * (u // 2):b * L + 512 * (u // 2) + 512])
                    last.then_inc(pr_full, 1)

            def scores(n):
                b, i = n // J, n % J
                wait_scores_bank(("s", n))
                pe.wait_ge(rope_done, 4 * b + (2 if i < 4 else 4))
                q = qk[b % 2][:, 0, i * P:(i + 1) * P]
                for c in range((i + 4) // 4):
                    w = min(512, (i + 1) * P - 512 * c)
                    diagonal = c == i // 4
                    last = mm(S[n % 2][:, c, 0:w], q, qk[b % 2][:, 1, 512 * c:512 * c + w], stop=not diagonal)
                    if diagonal:
                        last = mm(S[n % 2][:, c, w - P:w], identb[:, :], maskb[:, :], start=False)
                last.then_inc(s_full, 1)

            def wait_scores_bank(use):
                before = LAST_S[use]
                if before is not None:
                    kind, n = before
                    pe.wait_ge(*((rope_mul, 2 * n + 2) if kind == "pr" else (exp_done, n + 1)))

            def transpose_probs(n):
                i = n % J
                pe.wait_ge(exp_done, n + 1)
                for c in range((i + 4) // 4):
                    u = PT_OF[(n, c)]
                    wait_pt_free(pe, u)
                    for j in range(4 * c, min(4 * c + 4, i + 1)):
                        last = pe.transpose(TP[u % 2][:, (j - 4 * c) * P:(j - 4 * c + 1) * P],
                                            prob[n % 2][:, j * P:(j + 1) * P], ident)
                    last.then_inc(pt_full, 1)

            def weigh_values(n):
                b, i = n // J, n % J
                if n >= 2:
                    pe.wait_ge(o_done, n - 1)
                pe.wait_ge(pt_act, n + 1)
                for j in range(i + 1):
                    if j == 4:
                        pe.wait_ge(pt_dve, PT_DVE[PT_OF[(n, 1)]] + 1)
                    last = mm(O[n % 2][:, 0:D], pT[n % 2][:, j, :], vsb[:, b * J + j, :], start=j == 0, stop=j == i)
                last.then_inc(o_full, 1)

            def expert_pe(l, n_iter):
                def T_(it, m):
                    n = it * UNROLL + m
                    pe.wait_ge(xs_loaded[l][m], it * 16 + 16)
                    if not (isinstance(it, int) and n < 2):
                        pe.wait_ge(e_xT[l], n - 1)
                    pe.transpose(TP[m % 2][:, 0:P], xs[:, m, 0:D], ident).then_inc(e_t[l], 1)

                def H_(it, m):
                    n = it * UNROLL + m
                    pe.wait_ge(e_xT[1], n + 1)
                    pe.wait_ge(e_w1, n + 1)
                    if not (isinstance(it, int) and n < 2):
                        pe.wait_ge(e_ha, n - 1)
                        pe.wait_ge(e_hd, n - 1)
                    for f in range(2):
                        last = mm(S[m % 2][:, f, 0:P], w1r[:, m % 2, f * P:(f + 1) * P], xsT[:, m % 2, :])
                    last.then_inc(e_h, 1)

                def Y_(it, m):
                    n = it * UNROLL + m
                    if not (isinstance(it, int) and n < 2):
                        pe.wait_ge(e_ys[l], n - 1)
                    if l == 0:
                        pe.wait_ge(e_xT[0], n + 1)
                        e = it * 2 + m // 4
                        mm(O[m % 2][:, 0:D], xsT[:, m % 2, :], w0[:, e, :] if isinstance(e, int) else
                           w0[:, bass.ds(e, 1), :].rearrange("p e d -> p (e d)")).then_inc(e_y[0], 1)
                    else:
                        e = pe.value_load(expert[0:1, n:n + 1] if isinstance(n, int) else expert[0:1, bass.ds(n, 1)],
                                          min_val=0, max_val=E - 1)
                        we = w2[:, bass.ds(e, 1), :].rearrange("p e d -> p (e d)")
                        pe.wait_ge(e_ha, n + 1)
                        mm(O[m % 2][:, 0:D], hT[:, m % 2, 0, :], we[:, 0:D], stop=False)
                        pe.wait_ge(e_hd, n + 1)
                        mm(O[m % 2][:, 0:D], hT[:, m % 2, 1, :], we[:, D:2 * D], start=False).then_inc(e_y[1], 1)

                def step(it, m, last):
                    for stage, d in ((T_, 1 + l), (H_, 1)):
                        if stage is H_ and l == 0:
                            continue
                        mm_, up = (m + d) % UNROLL, (m + d) // UNROLL
                        if not (last and up):
                            stage(it + up, mm_)
                    Y_(it, m)

                for d in range(1 + l):
                    T_(0, d)
                if l == 1:
                    H_(0, 0)
                for m in range(UNROLL):
                    step(0, m, False)
                with pe.Fori(1, n_iter - 1) as it:
                    for m in range(UNROLL):
                        step(it, m, False)
                for m in range(UNROLL):
                    step(n_iter - 1, m, True)

            pe.wait_ge(cst_loaded, 16)
            pe.wait_ge(w_a_loaded, 16)
            for g in range(B):
                transpose_tokens(g)
                values_and_gates(g)
            pe.wait_ge(casts_done, 3)
            pe.wait_ge(ones_done, 2)
            pe.wait_ge(vg_free, 16)
            filter_network()
            pe.wait_ge(rt, R0_CUM)
            filter_spectrum()
            pe.wait_ge(fs_free, 4)
            pe.wait_ge(f_dve, 11)
            pe.wait_ge(rope_loaded, 32)
            project(0)
            scores(0)
            for n in range(NT):
                if n % J == 4 and n // J + 1 < B:
                    project(n // J + 1)
                if n + 1 < NT:
                    scores(n + 1)
                transpose_probs(n)
                if n:
                    weigh_values(n - 1)
                if n == MOE0_AT:
                    pe.wait_ge(pt_act, n + 1)
                    pe.wait_ge(pt_dve, sum(m <= n for m, c, _ in PT if c == 1))
                    pe.wait_ge(o_done, n)
                    pe.wait_ge(moe0_w_loaded, 32)
                    expert_pe(0, TILES0 // UNROLL)
                    pe.wait_ge(e_ys[0], TILES0)
            weigh_values(NT - 1)

            for g in range(B):
                if g == 0:
                    pe.wait_ge(pt_act, NT)
                    pe.wait_ge(pt_dve, len(PT_DVE))
                transpose_tokens(B + g)
            pe.wait_ge(l1_w_loaded, 16 * N_L1W)
            pe.wait_ge(o_done, NT)
            for q in range(NT // 4):
                pe.wait_ge(tr_free, 2 * B + q + 1)
                if q >= 2:
                    pe.wait_ge(v_done, q - 1)
                    pe.wait_ge(u_done, q - 1)
                    pe.wait_ge(lg1_done, q - 1)
                for t in range(4):
                    i = 4 * q + t
                    xt = xT[:, i * P:(i + 1) * P]
                    mm(S[q % 2][:, 0, t * D:(t + 1) * D], xt, wv[:, :])
                    mm(S[q % 2][:, 1, t * D:(t + 1) * D], xt, wu[:, :])
                    last = mm(O[q % 2][:, t * E:(t + 1) * E], xt, wg1[:, :])
                last.then_inc(uvg_full, 1)
            pe.wait_ge(lg1_done, NT // 4)
            routing_counts(1)
            pe.wait_ge(v_done, NT // 4)
            pe.wait_ge(u_done, NT // 4)
            for u in range(2 * NC):
                hf, c = divmod(u, NC)
                if c == 0:
                    pe.wait_ge(rad, RAD_F * (hf + 2))
                if u >= 4:
                    pe.wait_ge(x_free, u - 3)
                dft([SB[u % 4][:, 0:W], SB[u % 4][:, W:2 * W]], spec[hf][:, c, :, :], c, x_full)
            pe.wait_ge(rt, R1_CUM)
            for u in range(2 * NC):
                hf, c = divmod(u, NC)
                pe.wait_ge(y_ready, u + 1)
                if hf == 0:
                    pe.wait_ge(iv_loaded[c], 16)
                if u >= 4:
                    pe.wait_ge(b_free, u - 3)
                dft([TO[u % 4][:, 0:W], TO[u % 4][:, W:2 * W]], spec[hf][:, c, :, :], c, b_full)
            pe.wait_ge(b_free, 2 * NC)
            pe.wait_ge(conv_done, B)
            for q in range(NT // 4 + 1):
                if q < NT // 4:
                    if q >= 2:
                        pe.wait_ge(yt_free, q - 1)
                    for t in range(4):
                        b, j = divmod(4 * q + t, J)
                        last = pe.transpose(TP[q % 2][:, t * P:(t + 1) * P],
                                            vv[b // 2][:, j, (b % 2) * D:(b % 2 + 1) * D], ident)
                    last.then_inc(yt_full, 1)
                if q >= 1:
                    r = q - 1
                    pe.wait_ge(yt_free, r + 1)
                    if r >= 2:
                        pe.wait_ge(wo_done, r - 1)
                    for t in range(4):
                        i = 4 * r + t
                        last = mm(O[r % 2][:, t * D:(t + 1) * D], xT[:, i * P:(i + 1) * P], wo[:, :])
                    last.then_inc(wo_full, 1)
            pe.wait_ge(wo_done, NT // 4)
            pe.wait_ge(expert_ready, 1)
            expert_pe(1, TILES1 // UNROLL)

        @block.vector
        def _(dve):
            tt, stt, ts = dve.tensor_tensor, dve.scalar_tensor_tensor, dve.tensor_scalar

            def norm_stats(k):
                g = k % B
                if k < B:
                    dve.wait_ge(x_loaded[g], 16)
                for i in range(J * g, J * g + J):
                    dve.bn_stats(stats[:, i, :], xres[:, i, :]).then_inc(stats_done, 1)
                dve.wait_ge(stats_done, J * (k + 1))
                for i in range(J * g, J * g + J):
                    dve.bn_aggr(mv[:, i, :], stats[:, i, :]).then_inc(aggr_done, 1)

            def norm_rows(k):
                g = k % B
                dve.wait_ge(rstd_done, k + 1)
                for i in range(J * g, J * g + J):
                    ts(row[:, i, 0:D], xres[:, i, :], mv[:, i, 0:1], rstd[:, i:i + 1], ALU.subtract,
                       ALU.mult).then_inc(xn_done, 1)

            def norms(k0):
                norm_stats(k0)
                for k in range(k0 + 1, k0 + B):
                    norm_stats(k)
                    norm_rows(k - 1)
                norm_rows(k0 + B - 1)

            n_rt = [0]

            def rstep(ins):
                ins.then_inc(rt, 1)
                n_rt[0] += 1
                dve.wait_ge(rt, n_rt[0])

            def best_expert(src, rel_out, top, onehot):
                rstep(dve.tensor_reduce(top[:, :], ei(src), X, ALU.max))
                rstep(tt(rel_out[:, :, :], src[:, :, :], over_e(top), ALU.subtract))
                rstep(stt(flat(score), flat(rel_out), 0.0, col("rank"), ALU.is_ge, ALU.mult))
                rstep(dve.tensor_reduce(best[:, :], ei(score), X, ALU.max))
                rstep(tt(onehot[:, :, :], score[:, :, :], over_e(best), ALU.is_equal))

            def inverse_sum(gate):
                rstep(dve.tensor_reduce(best[:, :], ei(expl), X, ALU.add))
                rstep(dve.reciprocal(gate[:, :], best[:, :]))

            def earlier_tokens(k):
                dve.wait_ge(rt_mm, k + 1)
                before, total = O[0][:, 0:E * NT], O[0][:, E * NT:2 * E * NT]
                rstep(dve.tensor_tensor_scan(flat(cum), col("carry"), total, 0.0, ALU.mult, ALU.add))
                rstep(tt(flat(score), flat(cum), total, ALU.subtract))
                rstep(tt(flat(score), flat(score), before, ALU.add))

            def filter_poly(k):
                dve.wait_ge(f_act, 2 * k + 1)
                h, t = hx[0:FO, :], ht[0:FO, :]
                tt(t, h, h, ALU.mult).then_inc(f_dve, 1)
                dve.wait_ge(f_dve, 4 * k + 1)
                ts(t, t, 0.044715, 1.0, ALU.mult, ALU.add).then_inc(f_dve, 1)
                dve.wait_ge(f_dve, 4 * k + 2)
                tt(t, t, h, ALU.mult).then_inc(f_dve, 1)

            def filter_gelu(k):
                dve.wait_ge(f_act, 2 * k + 2)
                stt(hg[0:FO, :], hg[0:FO, :], 1.0, hx[0:FO, :], ALU.add, ALU.mult).then_inc(f_dve, 1)

            n_rad = [0]

            def did(ins):
                ins.then_inc(rad, 1)
                n_rad[0] += 1
                return n_rad[0]

            def after(*steps):
                dve.wait_ge(rad, max(steps))

            def radix_forward(v, a, pm_, ej_, uv_):
                p_, m_ = pm_[:, 0], pm_[:, 1]
                after(n_rad[0])
                s1 = did(tt(p_, v[:, 0:4], v[:, 4:8], ALU.add))
                s2 = did(tt(m_, v[:, 0:4], v[:, 4:8], ALU.subtract))
                after(s1)
                did(tt(a[:, 1], p_[:, 0:2], p_[:, 2:4], ALU.subtract))
                s4 = did(tt(uv_[:, 0], p_[:, 0:2], p_[:, 2:4], ALU.add))
                after(s2)
                did(tt(uv_[:, 1, 0], m_[:, 1], m_[:, 3], ALU.subtract))
                s8 = did(tt(uv_[:, 1, 1], m_[:, 1], m_[:, 3], ALU.add))
                after(s4)
                did(tt(a[:, 0, 0], uv_[:, 0, 0], uv_[:, 0, 1], ALU.add))
                did(tt(a[:, 0, 1], uv_[:, 0, 0], uv_[:, 0, 1], ALU.subtract))
                s11 = did(stt(ej_[:, 0], m_[:, 2:4], RC, v[:, 0:2], ALU.mult, ALU.add))
                s12 = did(stt(ej_[:, 1], p_[:, 2:4], RC, v[:, 4:6], ALU.mult, ALU.add))
                after(s8)
                did(stt(a[:, 2], uv_[:, 1], RC, m_[:, 0:3:2], ALU.mult, ALU.add))
                s10 = did(stt(a[:, 3], uv_[:, 1], -RC, m_[:, 0:3:2], ALU.mult, ALU.add))
                after(s12)
                did(stt(v[:, 0:2], m_[:, 2:4], -RC, v[:, 0:2], ALU.mult, ALU.add))
                s14 = did(stt(v[:, 4:6], p_[:, 2:4], -RC, v[:, 4:6], ALU.mult, ALU.add))
                after(s10)
                did(stt(uv_[:, 0, 0], ej_[:, 1, 1], -TAU, ej_[:, 0, 1], ALU.mult, ALU.add))
                s16 = did(stt(uv_[:, 0, 1], ej_[:, 0, 1], TAU, ej_[:, 1, 1], ALU.mult, ALU.add))
                after(s14)
                did(stt(uv_[:, 1, 0], v[:, 1], -TAU, v[:, 5], ALU.mult, ALU.subtract))
                s18 = did(stt(uv_[:, 1, 1], v[:, 5], -TAU, v[:, 1], ALU.mult, ALU.add))
                after(s16)
                did(stt(a[:, 4], uv_[:, 0], TC, ej_[:, :, 0], ALU.mult, ALU.add))
                did(stt(a[:, 5], uv_[:, 0], -TC, ej_[:, :, 0], ALU.mult, ALU.add))
                after(s18)
                did(stt(a[:, 6], uv_[:, 1], TC, v[:, 0:5:4], ALU.mult, ALU.add))
                did(stt(a[:, 7], uv_[:, 1], -TC, v[:, 0:5:4], ALU.mult, ALU.add))

            def radix_inverse(a, v):
                p_, m_ = pm[:, 0], pm[:, 1]
                v01_45 = v.rearrange("p (s h x) w -> p s h x w", s=2, h=2)[:, :, 0]
                did(tt(ej[:, :, 0], a[:, 4], a[:, 5], ALU.add))
                s2 = did(tt(uv[:, :, 0], a[:, 6], a[:, 7], ALU.add))
                after(s2)
                did(tt(a[:, 5], a[:, 4], a[:, 5], ALU.subtract))
                s4 = did(tt(a[:, 7], a[:, 6], a[:, 7], ALU.subtract))
                after(s4)
                did(ts(a[:, 5], a[:, 5], TC, None, ALU.mult))
                s6 = did(ts(a[:, 7], a[:, 7], TC, None, ALU.mult))
                did(tt(m_[:, 0:3:2], a[:, 2], a[:, 3], ALU.add))
                s8 = did(tt(a[:, 3], a[:, 2], a[:, 3], ALU.subtract))
                after(s6)
                did(stt(ej[:, 0, 1], a[:, 5, 1], TAU, a[:, 5, 0], ALU.mult, ALU.add))
                did(stt(ej[:, 1, 1], a[:, 5, 0], -TAU, a[:, 5, 1], ALU.mult, ALU.add))
                did(stt(uv[:, 0, 1], a[:, 7, 0], -TAU, a[:, 7, 1], ALU.mult, ALU.add))
                s12 = did(stt(uv[:, 1, 1], a[:, 7, 1], -TAU, a[:, 7, 0], ALU.mult, ALU.subtract))
                did(tt(p_[:, 0], a[:, 0, 0], a[:, 0, 1], ALU.add))
                s14 = did(tt(p_[:, 1], a[:, 0, 0], a[:, 0, 1], ALU.subtract))
                after(s14)
                did(tt(v01_45, ej[:, :, :], uv[:, :, :], ALU.add))
                s16 = did(tt(ej[:, :, :], ej[:, :, :], uv[:, :, :], ALU.subtract))
                did(tt(m_[:, 1], a[:, 3, 0], a[:, 3, 1], ALU.add))
                s18 = did(tt(m_[:, 3], a[:, 3, 1], a[:, 3, 0], ALU.subtract))
                s19 = did(tt(p_[:, 2:4], p_[:, 0:2], a[:, 1], ALU.subtract))
                after(s19)
                did(tt(p_[:, 0:2], p_[:, 0:2], a[:, 1], ALU.add))
                s21 = did(tt(m_[:, 3], m_[:, 3], ej[:, 0, 1], ALU.add))
                did(stt(m_[:, 2], ej[:, 0, 0], RC, m_[:, 2], ALU.mult, ALU.add))
                s23 = did(stt(p_[:, 2:4], ej[:, 1], RC, p_[:, 2:4], ALU.mult, ALU.add))
                after(s21)
                s24 = did(ts(m_[:, 1:4:2], m_[:, 1:4:2], RC, None, ALU.mult))
                after(s24)
                did(tt(ej[:, 0], p_[:, 0:2], m_[:, 0:2], ALU.add))
                s26 = did(tt(ej[:, 1], p_[:, 0:2], m_[:, 0:2], ALU.subtract))
                did(tt(v[:, 2:4], p_[:, 2:4], m_[:, 2:4], ALU.add))
                did(tt(v[:, 6:8], p_[:, 2:4], m_[:, 2:4], ALU.subtract))
                after(s26)
                after(did(tt(v01_45, v01_45, ej[:, :, :], ALU.add)))

            norms(0)
            filter_poly(0)
            dve.wait_ge(vg_free, 16)
            dve.wait_ge(cst_loaded, 16)
            best_expert(lg, rel, m1, oh1)
            rstep(dve.tensor_copy(flat(ohb), flat(oh1)))
            assert n_rt[0] == R0_OH
            filter_gelu(0)
            dve.wait_ge(rt_exp, 1)
            inverse_sum(gate0)
            filter_poly(1)
            earlier_tokens(0)
            assert n_rt[0] == R0_CUM
            rstep(stt(flat(oh2), flat(score), float(CAP), flat(oh1), ALU.is_lt, ALU.mult))
            rstep(tt(flat(score), flat(score), col("e_cap"), ALU.add))
            rstep(stt(flat(score), flat(score), -FAR, flat(oh2), ALU.add, ALU.mult))
            rstep(dve.tensor_reduce(best[:, :], ei(score), X, ALU.add))
            ts(slot0[:, :], best[:, :], FAR, None, ALU.add).then_inc(slot0_ready, 1)
            filter_gelu(1)
            dve.memset(hg[FO:FO + 1, :], 2.0).then_inc(f_dve, 1)
            dve.wait_ge(f_full, 3)
            for h in range(2):
                tt(filt_v[:, 4 * h:4 * h + 4, :], S[0][:, h, :].rearrange("p (j w) -> p j w", w=D),
                   col("decay")[:, 4 * h:4 * h + 4].unsqueeze(2).to_broadcast([P, 4, D]), ALU.mult).then_inc(f_dve, 1)
            dve.wait_ge(f_dve, 11)
            radix_forward(filt_v, filt_spec, filt_pm, filt_ej, filt_uv)
            assert n_rad[0] == RAD_F
            dve.wait_ge(hspec_done, 2)
            dve.memset(hspec0[0:1, 1, :, :], 0.0).then_inc(hspec_done, 1)

            def rope_products(b):
                for u in range(4):
                    n = 4 * b + u
                    c = slice(512 * (u // 2), 512 * (u // 2) + 512)
                    if n >= 2:
                        dve.wait_ge(rope_done, n - 1)
                    dve.wait_ge(pr_full, n + 1)
                    slot = S[(n + 1) % 2]
                    tt(qk[b % 2][:, u % 2, c], slot[:, 0, :], rope[:, 0, c], ALU.mult).then_inc(rope_mul, 1)
                    tt(rtmp[:, n % 2, :], slot[:, 1, :], rope[:, 1, c], ALU.mult).then_inc(rope_mul, 1)

            def row_max(n):
                dve.wait_ge(s_full, n + 1)
                dve.tensor_reduce(negmax[:, n:n + 1],
                                  S[n % 2][:, :, :].rearrange("p a m -> p (a m)")[:, 0:(n % J + 1) * P], X, ALU.max,
                                  negate=True).then_inc(max_done, 1)
                dve.wait_ge(max_done, n + 1)
                ts(negmax[:, n:n + 1], negmax[:, n:n + 1], SCALE, None, ALU.mult).then_inc(bias_done, 1)

            def take_pt(n):
                if (n, 1) not in PT_OF:
                    return
                u = PT_OF[(n, 1)]
                dve.wait_ge(pt_full, u + 1)
                dve.wait_ge(o_full, n - 1)
                k = n % J + 1 - 4
                dve.tensor_copy(pT[n % 2][:, 4:4 + k, :].rearrange("p j q -> p (j q)"),
                                TP[u % 2][:, 0:k * P]).then_inc(pt_dve, 1)

            def attention_row(n):
                dve.wait_ge(o_full, n + 1)
                dve.wait_ge(rrec_done, n + 1)
                stt(xres[:, n, :], O[n % 2][:, 0:D], rrec[:, n:n + 1], xres[:, n, :], ALU.mult,
                    ALU.add).then_inc(o_done, 1)

            def expert_dve(l, n_iter):
                def bias_of(it, m, n):
                    if l == 0:
                        e = it * 2 + m // 4
                    else:
                        e = load_expert(n)
                    return bmoe[:, bass.ds(e, 1), :].rearrange("p e d -> p (e d)")

                def load_expert(n):
                    return dve.value_load(expert[0:1, n:n + 1] if isinstance(n, int) else expert[0:1, bass.ds(n, 1)],
                                          min_val=0, max_val=E - 1)

                def W1_(it, m):
                    n = it * UNROLL + m
                    e = load_expert(n)
                    if not (isinstance(it, int) and n < 2):
                        dve.wait_ge(e_h, n - 1)
                        dve.wait_ge(e_ha, n - 1)
                        dve.wait_ge(e_hd, n - 1)
                    dve.tensor_copy(w1r[:, m % 2, :], w1[:, bass.ds(e, 1), :].rearrange("p e h -> p (e h)")).then_inc(e_w1, 1)

                def R_(it, m):
                    n = it * UNROLL + m
                    dve.wait_ge(e_h, n + 1)
                    ts(hT[:, m % 2, 1, :], S[m % 2][:, 1, 0:P], w1r[:, m % 2, H1 + 1:H1 + 2], 0.0, ALU.add,
                       ALU.max).then_inc(e_hd, 1)

                def step(it, m, last):
                    n = it * UNROLL + m
                    if l == 1:
                        for stage, d in ((R_, 1), (W1_, 2)):
                            mm_, up = (m + d) % UNROLL, (m + d) // UNROLL
                            if not (last and up):
                                stage(it + up, mm_)
                    b = bias_of(it, m, n)
                    if not (isinstance(it, int) and it == 0):
                        dve.wait_ge(sent_back[l][m], it * 16)
                    dve.wait_ge(e_y[l], n + 1)
                    tt(ys[:, m, :], O[m % 2][:, 0:D], b, ALU.add).then_inc(e_ys[l], 1)

                if l == 1:
                    W1_(0, 0)
                    W1_(0, 1)
                    R_(0, 0)
                for m in range(UNROLL):
                    step(0, m, False)
                with dve.Fori(1, n_iter - 1) as it:
                    for m in range(UNROLL):
                        step(it, m, False)
                for m in range(UNROLL):
                    step(n_iter - 1, m, True)

            dve.wait_ge(rope_loaded, 32)
            rope_products(0)
            row_max(0)
            for n in range(NT):
                if n % J == 4 and n // J + 1 < B:
                    rope_products(n // J + 1)
                if n + 1 < NT:
                    row_max(n + 1)
                dve.wait_ge(exp_done, n + 1)
                dve.reciprocal(rrec[:, n:n + 1], rsum[:, n:n + 1]).then_inc(rrec_done, 1)
                take_pt(n)
                if n:
                    attention_row(n - 1)
                if n == MOE0_AT:
                    dve.wait_ge(moe0_w_loaded, 32)
                    expert_dve(0, TILES0 // UNROLL)
            attention_row(NT - 1)
            dve.wait_ge(o_done, NT)
            for g in range(B):
                dve.wait_ge(y0_loaded, 16 * (g + 1))
                for j in range(J):
                    i = J * g + j
                    last = stt(xres[:, i, :], y0[:, j, :], gate0[:, i:i + 1], xres[:, i, :], ALU.mult, ALU.add)
                last.then_inc(y0_used, 1)

            dve.wait_ge(y0_used, B)
            norms(B)
            dve.wait_ge(l1_w_loaded, 16 * N_L1W)
            for q in range(NT // 4):
                b, j = divmod(4 * q, J)
                dve.wait_ge(uvg_full, q + 1)
                tt(vv[b // 2][:, j:j + 4, (b % 2) * D:(b % 2 + 1) * D],
                   S[q % 2][:, 0, :].rearrange("p (t d) -> p t d", d=D),
                   bv[:, :].unsqueeze(1).to_broadcast([P, 4, D]), ALU.add).then_inc(v_done, 1)
                tt(uu[:, 4 * q:4 * q + 4, :], S[q % 2][:, 1, :].rearrange("p (t d) -> p t d", d=D),
                   bu[:, :].unsqueeze(1).to_broadcast([P, 4, D]), ALU.add).then_inc(u_done, 1)
            dve.wait_ge(lg1_done, NT // 4)
            n_rt[0] = 15
            best_expert(lg, rel, m1, oh1)
            rstep(stt(flat(score), flat(oh1), -1e30, flat(rel), ALU.mult, ALU.add))
            rstep(dve.tensor_reduce(m2[:, :], ei(score), X, ALU.max))
            rstep(tt(score[:, :, :], score[:, :, :], over_e(m2), ALU.subtract))
            rstep(stt(flat(score), flat(score), 0.0, col("rank"), ALU.is_ge, ALU.mult))
            rstep(dve.tensor_reduce(best[:, :], ei(score), X, ALU.max))
            rstep(tt(oh2[:, :, :], score[:, :, :], over_e(best), ALU.is_equal))
            rstep(tt(flat(ohb), flat(oh1), flat(oh2), ALU.add))
            assert n_rt[0] == R1_OH, n_rt
            dve.wait_ge(rt_exp, 3)
            inverse_sum(gate1)
            rstep(tt(gate2[:, :], em2[:, :], gate1[:, :], ALU.mult))
            earlier_tokens(1)
            assert n_rt[0] == R1_CUM, n_rt
            rstep(ts(cnt_i[:, :], cum[:, :, NT - 1], float(P - 1), None, ALU.add))
            rstep(ts(cnt_t[:, :], cnt_i[:, :], 7, None, ALU.arith_shift_right))
            rstep(dve.tensor_copy(ntile[:, :], cnt_t[:, :]))
            dve.wait_ge(ones_done, 2)
            rstep(dve.tensor_tensor_scan(ctile[:, :], ones8[:, :], ntile[:, :], 0.0, ALU.mult, ALU.add))
            rstep(tt(base[:, :], ctile[:, :], ntile[:, :], ALU.subtract))
            rstep(stt(score[:, :, :], base[:, :].unsqueeze(2).to_broadcast([P, E, NT]), float(P), score[:, :, :],
                      ALU.mult, ALU.add))
            for o, onehot, m in ((slot1, oh1, m1), (slot2, oh2, m2)):
                rstep(tt(flat(rel), flat(score), flat(onehot), ALU.mult))
                rstep(dve.tensor_reduce(m[:, :], ei(rel), X, ALU.add))
                dve.tensor_copy(o[:, :], m[:, :]).then_inc(slot1_ready, 1)
            rstep(tt(ecmp[:, :, :], ctile[0:1, :].unsqueeze(1).to_broadcast([1, TILES1, E]),
                     cst[0:1, CONST["tile_no"][0]:CONST["tile_no"][1]].rearrange("p (n e) -> p n e", e=E), ALU.is_le))
            rstep(dve.tensor_reduce(ecnt[:, :], ecmp[:, :, :], X, ALU.add))
            ts(expert[:, :], ecnt[:, :], float(E - 1), None, ALU.min).then_inc(expert_ready, 1)

            for hf in range(HALF):
                radix_forward(vv[hf], spec[hf], pm, ej, uv)
            dve.wait_ge(hspec_done, 4)
            for u in range(2 * NC):
                hf, c = divmod(u, NC)
                dve.wait_ge(x_full, u + 1)
                if u >= 2:
                    dve.wait_ge(y_ready, u - 1)
                t_ = [prod[:, 2 * (u % 2) + a] for a in range(2)]
                for a in range(2):
                    shape, x_ = ([P, 2, 2, D], "p (a b d) -> p a b d") if c == 0 else ([P, 4, D], "p (a d) -> p a d")
                    kw = dict(a=2, d=D) if c == 0 else dict(d=D)
                    h_ = hspec0[:, a, :, :].unsqueeze(2) if c == 0 else hspec[:, c, a, :].unsqueeze(1)
                    o_ = t_[a].rearrange("p a w -> p (a w)").rearrange(x_, **kw)
                    tt(o_, SB[u % 4].rearrange(x_, **kw), h_.to_broadcast(shape), ALU.mult).then_inc((pmul, x_free)[a], 1)
                dve.wait_ge(pmul, u + 1)
                dve.wait_ge(x_free, u + 1)
                y = spec[hf][:, c]
                tt(y[:, 0], t_[0][:, 0], t_[1][:, 1], ALU.subtract)
                tt(y[:, 1], t_[0][:, 1], t_[1][:, 0], ALU.add).then_inc(y_ready, 1)
            dve.wait_ge(y_ready, 2 * NC)
            for hf in range(HALF):
                dve.wait_ge(b_free, NC * (hf + 1))
                radix_inverse(spec[hf], vv[hf])
                for b in range(2 * hf, 2 * hf + 2):
                    v_ = vv[hf][:, :, (b % 2) * D:(b % 2 + 1) * D]
                    tt(v_, v_, uu[:, J * b:J * b + J, :], ALU.mult).then_inc(conv_done, 1)
            dve.wait_ge(bo_done, 1)
            for q in range(NT // 4):
                dve.wait_ge(wo_full, q + 1)
                r_ = xres[:, 4 * q:4 * q + 4, :]
                tt(r_, O[q % 2][:, :].rearrange("p (t d) -> p t d", d=D), r_, ALU.add).then_inc(wo_done, 1)
            dve.wait_ge(expert_ready, 1)
            dve.wait_ge(b2_loaded, 16)
            expert_dve(1, TILES1 // UNROLL)
            for q in range(NT // 4):
                dve.wait_ge(back_loaded[q % 4], 16 * (q // 4 + 1))
                for k, gate in ((0, gate1), (1, gate2)):
                    for t in range(4):
                        i = 4 * q + t
                        last = stt(xres[:, i, :], moe_back[q % 4][:, t, k, :], gate[:, i:i + 1], xres[:, i, :],
                                   ALU.mult, ALU.add)
                    if k == 0:
                        last.then_inc(out_a, 1)
                        dve.wait_ge(out_a, q + 1)
                last.then_inc(out_ready, 1)


def kernel(**inputs):
    import concourse.bacc as bacc
    from concourse.bass_utils import run_bass_kernel_spmd

    a = {k: np.asarray(v) for k, v in inputs.items()}
    fw, iv = dft_matrices()
    wq, wk = a["L0_attn_w_q"], a["L0_attn_w_k"]
    swap = np.arange(D) ^ 1
    args = {
        "x": a["L0_attn_x"],
        "cst": constants(),
        "rope": rope_tables(),
        "fw": fw,
        "iv": iv,
        "pe": position_table(),
        "wqk": np.concatenate([wq.T, wq[swap].T, wk.T, wk[swap].T], 1),
        "wvg": np.concatenate([a["L0_attn_w_v"].T, a["L0_ffn_wg"]], 1),
        "w0": a["L0_ffn_W"].transpose(2, 0, 1),
        "b0": a["L0_ffn_b"],
        "f1w": a["L1_attn_W1"],
        "f1b": a["L1_attn_b1"].reshape(FO, 1),
        "f2w": a["L1_attn_W2"],
        "f2b": a["L1_attn_b2"].reshape(FO, 1),
        "f3": np.concatenate([a["L1_attn_W3"], a["L1_attn_b3"][None]], 0),
        "wv": a["L1_attn_Wv"],
        "wu": a["L1_attn_Wu"],
        "wg1": a["L1_ffn_Wg"],
        "bu": a["L1_attn_bu"],
        "bv": a["L1_attn_bv"],
        "wo": a["L1_attn_Wo"],
        "bo": a["L1_attn_bo"],
        "w1": a["L1_ffn_W1"],
        "b1": a["L1_ffn_b1"].reshape(E, 2, P).transpose(2, 0, 1),
        "w2": a["L1_ffn_W2"],
        "b2": a["L1_ffn_b2"],
    }
    nc = bacc.Bacc("TRN2", target_bir_lowering=False, num_devices=1)
    arrays, aps = {}, []
    for name, v in args.items():
        v = np.ascontiguousarray(v)
        arrays[f"in_{name}"] = v
        aps.append(nc.dram_tensor(f"in_{name}", v.shape, mybir.dt.from_np(v.dtype), kind="ExternalInput").ap())
    aps.append(nc.dram_tensor("out", (B, L, D), F32, kind="ExternalOutput").ap())
    two_layer_kernel(nc, *aps)
    return run_bass_kernel_spmd(nc, [arrays], core_ids=[0]).results[0]["out"]
```

```python
from contextlib import ExitStack

import numpy as np

import concourse.bass as bass
from concourse import mybir

F32 = mybir.dt.float32
BF16 = mybir.dt.bfloat16
I32 = mybir.dt.int32
ALU = mybir.AluOpType
ACT = mybir.ActivationFunctionType
X = mybir.AxisListType.X

P = 128
D = 128
B, L = 4, 1024
T = B * L
NT = T // P
J = L // P
E = 8
CAP = T // E
H1 = 256
ROWW = D + 1
SLOTS0 = E * CAP
TILES0 = SLOTS0 // P
UNROLL = 8
TILES1 = -(-(2 * T // P + E - 1) // UNROLL) * UNROLL
SLOTS1 = TILES1 * P
FAR = 65536.0
FO = 64
KS = (0, 4, 2, 10, 1, 9, 5, 13)
NC = len(KS)
NFFT = 2 * L
RC = float(np.sqrt(0.5))
TC = float(np.cos(np.pi / 8))
TAU = float(np.tan(np.pi / 8))
HALF = 2
W = (B // HALF) * D
VGW = D + E
SCALE = float(D) ** -0.5

CONST = {}


def _const_columns():
    at = 0
    for name, n in (("ident", P), ("before", P), ("mask", P), ("rank", E * NT), ("e_cap", E * NT),
                    ("carry", E * NT), ("decay", J), ("minus_half", J), ("tile_no", TILES1 * E),
                    ("token", NT), ("token2", NT), ("token2b", NT)):
        CONST[name] = (at, at + n)
        at += n
    return at


NCONST = _const_columns()


def dft_matrices():
    t = np.arange(P)
    fw = np.zeros((NC, 4, P, P))
    iv = np.zeros((NC, 4, P, P))
    for c, k1 in enumerate(KS):
        if c == 0:
            continue
        th = 2 * np.pi * ((t[:, None] * (k1 + 16 * t[None, :])) % NFFT) / NFFT
        co, si = np.cos(th), np.sin(th)
        fw[c] = co, -si, si, co
        iv[c] = co.T, si.T, -si.T, co.T
        iv[c] *= 2 / NFFT
    h = np.arange(P // 2)
    th0 = 2 * np.pi * ((t[:, None] * 16 * h[None, :]) % NFFT) / NFFT
    th8 = 2 * np.pi * ((t[:, None] * (8 + 16 * h[None, :])) % NFFT) / NFFT
    fw[0, 0, :, :64] = np.cos(th0)
    fw[0, 1, :, 64:] = np.cos(th8)
    fw[0, 2, :, :64] = np.sin(th0)
    fw[0, 2, :, 0] = (-1.0) ** t
    fw[0, 3, :, 64:] = np.sin(th8)
    iv[0, 0, :64] = 2 * np.cos(th0).T
    iv[0, 0, 0] = 1
    iv[0, 1, :64] = 2 * np.sin(th0).T
    iv[0, 1, 0] = (-1.0) ** t
    iv[0, 2, 64:] = 2 * np.cos(th8).T
    iv[0, 3, 64:] = 2 * np.sin(th8).T
    iv[0] /= NFFT
    lay = lambda m: np.ascontiguousarray(m.transpose(2, 0, 1, 3).reshape(P, -1), np.float32)
    return lay(fw), lay(iv)


def rope_tables():
    theta = np.float32(10000.0 ** (-2.0 * (np.arange(D // 2) - 1.0) / D))
    ang = np.arange(L, dtype=np.float32)[:, None] * theta.astype(np.float32)[None, :]
    ang = ang.astype(np.float64)
    co = np.repeat(np.cos(ang), 2, axis=1).T
    si = np.repeat(np.sin(ang), 2, axis=1).T * np.where(np.arange(D) % 2, -1.0, 1.0)[:, None]
    return np.ascontiguousarray(np.stack([co, si], 1).reshape(P, -1), np.float32)


def position_table():
    pos = np.arange(L, dtype=np.float32)[:, None]
    div = np.exp(np.arange(0, FO, 2, dtype=np.float32) * np.float32(-(np.log(np.float32(10000.0)) / np.float32(FO))),
                 dtype=np.float64).astype(np.float32)
    ang = (pos * div.astype(np.float32)).astype(np.float32).astype(np.float64)
    pe = np.zeros((L, FO), np.float32)
    pe[:, 0::2] = np.sin(ang)
    pe[:, 1::2] = np.cos(ang)
    return np.ascontiguousarray(pe.T)


def constants():
    c = np.zeros((P, NCONST), np.float32)
    p = np.arange(P)
    put = lambda name, v: c.__setitem__((slice(None), slice(*CONST[name])), np.broadcast_to(v, (P, CONST[name][1] - CONST[name][0])))
    put("ident", np.eye(P))
    put("before", (p[:, None] < p[None, :]))
    put("mask", np.where(p[None, :] > p[:, None], -1e38, 0.0))
    e = np.arange(E)
    put("rank", np.repeat(E - e, NT))
    put("e_cap", np.repeat(e * CAP, NT))
    put("carry", np.tile(np.arange(NT) > 0, E))
    t = np.arange(L, dtype=np.float32).reshape(J, P).T
    put("decay", 0.5 * np.exp(np.float32(-0.01) * t))
    put("minus_half", -0.5)
    put("tile_no", np.repeat(np.arange(TILES1), E))
    token = np.arange(T).reshape(NT, P).T
    c = c.view(np.int32)
    for name, v in (("token", token), ("token2", 2 * token), ("token2b", 2 * token + 1)):
        c[:, slice(*CONST[name])] = v
    return c.view(np.float32)


R0_REL, R0_OH, R0_CUM = 2, 6, 11
R1_REL, R1_M2, R1_OH, R1_CUM = 17, 22, 27, 33
RAD_F = 22
N_FILL = (TILES0 + TILES1 + NT) // 8
N_L1W = 2 + E + 7
MOE0_FROM, MOE0_STEP = 12, 4
ADD_AT = 21
W1_RING = 4


def moe0_tiles(n):
    return [k for k in range(MOE0_STEP * (n - MOE0_FROM), MOE0_STEP * (n - MOE0_FROM + 1)) if 0 <= k < TILES0]


N_BACK = 31


def conv_dve_at(n):
    return 1 if 0 <= n < HALF * N_BACK else 0


def conv_pe_at(n):
    if 0 <= n < NC:
        return [("inv", NC + n)]
    for h in range(HALF):
        k = n - (N_BACK * (h + 1) + 1)
        if 0 <= k <= 4:
            return ([("yt", 4 * h + k)] if k < 4 else []) + ([("wo", 4 * h + k - 1)] if k else [])
    return []


def two_layer_kernel(nc, x_in, cst_in, rope_in, fw_in, iv_in, pe_in, wqk_in, wvg_in, w0_in, b0_in,
                     f1w_in, f1b_in, f2w_in, f2b_in, f3_in, wv_in, wu_in, wg1_in, bu_in, bv_in, wo_in,
                     bo_in, w1_in, b1_in, w2_in, b2_in, out):
    ctx = ExitStack()
    with ctx:
        def sb(name, shape, dt=F32):
            return ctx.enter_context(nc.sbuf_tensor(name, shape, dt))

        def ps(name, shape):
            return ctx.enter_context(nc.psum_tensor(name, shape, F32))

        def sem(name):
            return ctx.enter_context(nc.semaphore(name))

        slots0 = nc.dram_tensor("slots0", (SLOTS0, ROWW), F32, kind="Internal").ap()
        slots1 = nc.dram_tensor("slots1", (SLOTS1, ROWW), F32, kind="Internal").ap()
        moe0 = nc.dram_tensor("moe0", (T, D), F32, kind="Internal").ap()
        moe1 = nc.dram_tensor("moe1", (2 * T, D), F32, kind="Internal").ap()

        xres = sb("xres", [P, NT, D])
        row = sb("row", [P, NT, ROWW])
        xT = sb("xT", [P, T])
        cst = sb("cst", [P, NCONST])
        identb = sb("identb", [P, P], BF16)
        beforeb = sb("beforeb", [P, P], BF16)
        maskb = sb("maskb", [P, P], BF16)
        onesb = sb("onesb", [P, P], BF16)
        w0 = sb("w0", [P, E, D])
        bmoe = sb("bmoe", [P, E, D])
        w1 = sb("w1", [P, E, H1 + 2])
        w2 = sb("w2", [P, E, 2 * D])
        wv = sb("wv", [P, D])
        wu = sb("wu", [P, D])
        wg1 = sb("wg1", [P, E])
        wo = sb("wo", [P, D])
        bu = sb("bu", [P, D])
        bv = sb("bv", [P, D])
        bo = sb("bo", [P, D])
        mats = sb("mats", [P, NC, 4, P])
        hspec = sb("hspec", [P, NC, 2, D])
        hspec0 = sb("hspec0", [P, 2, 2, D])
        stats = sb("stats", [P, NT, 6])
        mv = sb("mv", [P, NT, 2])
        rstd = sb("rstd", [P, NT])
        veps = sb("veps", [P, NT])
        xs = sb("xs", [P, UNROLL, ROWW])
        ys = sb("ys", [P, UNROLL, D])
        xsT = sb("xsT", [P, 2, P])
        hT = sb("hT", [P, 2, 2, P])
        w1r = sb("w1r", [P, W1_RING, H1 + 2])
        lg = sb("lg", [P, E, NT])
        rel = sb("rel", [P, E, NT])
        score = sb("score", [P, E, NT])
        expl = sb("expl", [P, E, NT])
        oh1 = sb("oh1", [P, E, NT])
        oh2 = sb("oh2", [P, E, NT])
        ohb = sb("ohb", [P, E, NT], BF16)
        cum = sb("cum", [P, E, NT])
        m1 = sb("m1", [P, NT])
        m2 = sb("m2", [P, NT])
        best = sb("best", [P, NT])
        gate0 = sb("gate0", [P, NT])
        gate1 = sb("gate1", [P, NT])
        gate2 = sb("gate2", [P, NT])
        em2 = sb("em2", [P, NT])
        slot0 = sb("slot0", [P, NT], I32)
        slot1 = sb("slot1", [P, NT], I32)
        slot2 = sb("slot2", [P, NT], I32)
        cnt_i = sb("cnt_i", [P, E], I32)
        cnt_t = sb("cnt_t", [P, E], I32)
        ntile = sb("ntile", [P, E])
        ctile = sb("ctile", [P, E])
        base = sb("base", [P, E])
        ones8 = sb("ones8", [P, E])
        ecmp = sb("ecmp", [1, TILES1, E])
        ecnt = sb("ecnt", [1, TILES1])
        expert = sb("expert", [1, TILES1], I32)

        WORK = 17200
        work = sb("work", [P, WORK])
        place = [0]

        def part(n, shape=None, **kw):
            a = work[:, place[0]:place[0] + n]
            place[0] += n
            assert place[0] <= WORK
            return a.rearrange(shape, **kw) if shape else a

        rope = part(2 * L, "p (a m) -> p a m", a=2)
        wqk = part(4 * D, "p (a e) -> p a e", a=4)
        wvg = part(VGW)
        vsb = part(NT * D, "p (i d) -> p i d", d=D)
        negmax = part(NT)
        rsum = part(NT)
        rrec = part(NT)
        y0 = part(J * D, "p (j d) -> p j d", d=D)
        shared = place[0]
        qk = [part(2 * L, "p (a m) -> p a m", a=2) for _ in range(2)]
        rtmp = part(2 * 512, "p (a m) -> p a m", a=2)
        prob = [part(L) for _ in range(2)]
        pT = [part(L, "p (j q) -> p j q", q=P) for _ in range(2)]
        place[0] = shared
        hx = part(L)
        ht = part(L)
        hg = part(L)
        pe_sb = part(L)
        fw_small = part(2 * FO + D + 2)
        filt_v = part(J * D, "p (j w) -> p j w", w=D)
        filt_spec = part(NC * 2 * D, "p (c a w) -> p c a w", a=2, w=D)
        filt_pm = hx.rearrange("p (a j w) -> p a j w", a=2, w=D)
        filt_ej = ht[:, 0:4 * D].rearrange("p (s x w) -> p s x w", s=2, w=D)
        filt_uv = hg[:, 0:4 * D].rearrange("p (s a w) -> p s a w", s=2, w=D)
        f1w, f2w = fw_small[0:FO, 0:FO], fw_small[0:FO, FO:2 * FO]
        f3w = fw_small[0:FO + 1, 2 * FO:2 * FO + D]
        f1b, f2b = fw_small[0:FO, 2 * FO + D:2 * FO + D + 1], fw_small[0:FO, 2 * FO + D + 1:2 * FO + D + 2]
        place[0] = 0
        uu = part(NT * D, "p (i d) -> p i d", d=D)
        vv = [part(J * W, "p (j w) -> p j w", w=W) for _ in range(HALF)]
        spec0 = part(NC * 2 * W)
        spec = [a.rearrange("p (c a w) -> p c a w", a=2, w=W) for a in (spec0, xT[:, :])]
        yT = spec0
        moe_back = [a[:, n * 1024:(n + 1) * 1024].rearrange("p (i k d) -> p i k d", k=2, d=D)
                    for a in (spec0, xT) for n in range(4)]
        pmf = part(8 * W)
        pm = pmf.rearrange("p (a j w) -> p a j w", a=2, w=W)
        prod = pmf.rearrange("p (n a w) -> p n a w", n=4, w=W)
        ej = part(4 * W, "p (s x w) -> p s x w", s=2, w=W)
        uv = part(4 * W, "p (s a w) -> p s a w", s=2, w=W)

        S = [ps(f"psS{n}", [P, 2, 512]) for n in range(2)]
        TP = [ps(f"psT{n}", [P, 512]) for n in range(2)]
        O = [ps(f"psO{n}", [P, 512]) for n in range(2)]
        SB = [S[0][:, 0, :], S[0][:, 1, :], S[1][:, 0, :], S[1][:, 1, :]]
        TO = [TP[0][:, :], TP[1][:, :], O[0][:, :], O[1][:, :]]

        def col(name, shape=None, **kw):
            a = cst[:, CONST[name][0]:CONST[name][1]]
            return a.rearrange(shape, **kw) if shape else a

        def ei(a):
            return a[:, :, :].rearrange("p e i -> p i e")

        def flat(a):
            return a[:, :, :].rearrange("p e i -> p (e i)")

        def over_e(a):
            return a[:, :].unsqueeze(1).to_broadcast([P, E, NT])

        ident = col("ident")

        x_loaded = [sem(f"x_loaded{g}") for g in range(B)]
        cst_loaded = sem("cst_loaded")
        w_a_loaded = sem("w_a_loaded")
        filt_loaded = sem("filt_loaded")
        fw_loaded = sem("fw_loaded")
        rope_loaded = sem("rope_loaded")
        moe0_w_loaded = sem("moe0_w_loaded")
        l1_w_loaded = sem("l1_w_loaded")
        b2_loaded = sem("b2_loaded")
        iv_loaded = [sem(f"iv_loaded{c}") for c in range(NC)]
        fill_ready = sem("fill_ready")
        prefilled = sem("prefilled")
        casts_done = sem("casts_done")
        ones_done = sem("ones_done")
        ids_done = sem("ids_done")
        stats_done = sem("stats_done")
        aggr_done = sem("aggr_done")
        veps_done = sem("veps_done")
        rstd_done = sem("rstd_done")
        xn_done = sem("xn_done")
        tr_full = sem("tr_full")
        tr_free = sem("tr_free")
        vg_full = sem("vg_full")
        vg_free = sem("vg_free")
        f_full = sem("f_full")
        f_act = sem("f_act")
        f_dve = sem("f_dve")
        fs_full = sem("fs_full")
        fs_free = sem("fs_free")
        hspec_done = sem("hspec_done")
        rt = sem("rt")
        rt_exp = sem("rt_exp")
        rt_mm = sem("rt_mm")
        slot0_ready = sem("slot0_ready")
        sent0 = sem("sent0")
        pr_full = sem("pr_full")
        rope_mul = sem("rope_mul")
        rope_done = sem("rope_done")
        s_full = sem("s_full")
        max_done = sem("max_done")
        exp_done = sem("exp_done")
        bias_done = sem("bias_done")
        pt_full = sem("pt_full")
        pt_act = sem("pt_act")
        pt_dve = sem("pt_dve")
        o_full = sem("o_full")
        rrec_done = sem("rrec_done")
        o_done = sem("o_done")
        xs_loaded = [[sem(f"xs_loaded{l}_{m}") for m in range(UNROLL)] for l in range(2)]
        sent_back = [[sem(f"sent_back{l}_{m}") for m in range(UNROLL)] for l in range(2)]
        e_t = [sem(f"e_t{l}") for l in range(2)]
        e_xT = [sem(f"e_xT{l}") for l in range(2)]
        e_y = [sem(f"e_y{l}") for l in range(2)]
        e_ys = [sem(f"e_ys{l}") for l in range(2)]
        e_w1 = sem("e_w1")
        e_h = sem("e_h")
        e_ha = sem("e_ha")
        e_hd = sem("e_hd")
        y0_loaded = sem("y0_loaded")
        y0_used = sem("y0_used")
        uvg_full = sem("uvg_full")
        v_done = sem("v_done")
        u_done = sem("u_done")
        g_full = sem("g_full")
        lg1_done = sem("lg1_done")
        bo_done = sem("bo_done")
        slot1_ready = sem("slot1_ready")
        expert_ready = sem("expert_ready")
        sent1 = [sem(f"sent1_{n}") for n in range(4)]
        ids2_done = sem("ids2_done")
        rad = sem("rad")
        x_full = sem("x_full")
        pmul = sem("pmul")
        x_free = sem("x_free")
        y_ready = sem("y_ready")
        b_full = sem("b_full")
        b_free = sem("b_free")
        conv_done = sem("conv_done")
        yt_full = sem("yt_full")
        yt_free = sem("yt_free")
        wo_full = sem("wo_full")
        wo_done = sem("wo_done")
        back_loaded = [sem(f"back_loaded{n}") for n in range(NT // 4)]
        gated2 = sem("gated2")
        out_a = sem("out_a")
        out_ready = sem("out_ready")
        stored = sem("stored")

        T_USES, O_USES = [], []
        for n in range(NT):
            T_USES += [("p", n, c) for c in range((n % J + 4) // 4)]
            if n:
                O_USES.append(("o", n - 1))
            T_USES += [("x", k) for k in moe0_tiles(n)]
            O_USES += [("y", k) for k in moe0_tiles(n)]
        O_USES.append(("o", NT - 1))
        T_AT = {use: u for u, use in enumerate(T_USES)}
        O_AT = {use: u for u, use in enumerate(O_USES)}
        SECOND = [n for n in range(NT) if n % J >= 4]

        def t_bank(*use):
            return TP[T_AT[use] % 2]

        def o_bank(*use):
            return O[O_AT[use] % 2]

        def pt_full_at(n, c):
            return sum(use[0] == "p" for use in T_USES[:T_AT[("p", n, c)] + 1])

        def wait_emptied(eng, uses, u):
            if u < 2:
                return
            kind, n, *c = uses[u - 2]
            if kind == "p":
                eng.wait_ge(*((pt_dve, SECOND.index(n) + 1) if c[0] else (pt_act, n + 1)))
            else:
                eng.wait_ge({"x": e_xT[0], "o": o_done, "y": e_ys[0]}[kind], n + 1)

        C_USES = [("inv", v) for v in range(NC, 2 * NC)]
        for h in range(HALF):
            for q in range(4 * h, 4 * h + 4):
                C_USES += [("yt", q)] + ([("wo", q - 1)] if q > 4 * h else [])
            C_USES.append(("wo", 4 * h + 3))
        C_AT = {use: u for u, use in enumerate(C_USES)}

        def c_bank(*use):
            return SB[2 + C_AT[use] % 2]

        def wait_c_emptied(eng, *use):
            if C_AT[use] >= 2:
                kind, n = C_USES[C_AT[use] - 2]
                eng.wait_ge({"inv": b_free, "yt": yt_free, "wo": wo_done}[kind], n + 1)

        S_USES = [("pr", u) for u in range(4)] + [("s", 0)]
        for n in range(NT):
            if n % J == 4 and n // J + 1 < B:
                S_USES += [("pr", 4 * (n // J + 1) + u) for u in range(4)]
            if n + 1 < NT:
                S_USES.append(("s", n + 1))
        LAST_S, seen = {}, {}
        for use in S_USES:
            slot = use[1] % 2 if use[0] == "s" else (use[1] + 1) % 2
            LAST_S[use] = seen.get(slot)
            seen[slot] = use

        def wait_hidden(eng, n):
            eng.wait_ge(e_hd if n % 2 else e_ha, n // 2 + 1)

        block = ctx.enter_context(nc.Block())

        @block.sync
        def _(sp):
            xv = x_in.rearrange("b (j p) d -> b p j d", p=P)
            for g in range(B):
                sp.dma_start(xres[:, J * g:J * (g + 1), :], xv[g]).then_inc(x_loaded[g], 16)
                if g == 0:
                    sp.dma_start(cst[:, :], cst_in).then_inc(cst_loaded, 16)
                    sp.dma_start(wvg, wvg_in).then_inc(w_a_loaded, 16)
            for a, b in ((pe_sb[0:FO, :], pe_in), (f1w, f1w_in), (f1b, f1b_in), (f2w, f2w_in),
                         (f2b, f2b_in), (f3w, f3_in)):
                sp.dma_start(a, b).then_inc(filt_loaded, 16)
            sp.dma_start(mats[:, :, :, :], fw_in).then_inc(fw_loaded, 16)
            sp.dma_start(wqk, wqk_in).then_inc(rope_loaded, 16)
            sp.dma_start(rope, rope_in).then_inc(rope_loaded, 16)
            sp.dma_start(w0[:, :, :], w0_in).then_inc(moe0_w_loaded, 16)
            sp.dma_start(bmoe[:, :, :], b0_in.rearrange("e d -> (e d)").partition_broadcast(P)).then_inc(moe0_w_loaded, 16)
            sp.wait_ge(fill_ready, 2)
            for dst, n in ((slots0, TILES0), (slots1, TILES1)):
                for i in range(0, n, 8):
                    sp.dma_start(dst[i * P:(i + 8) * P, :].rearrange("(i p) w -> p i w", p=P),
                                 xs[:, :, :]).then_inc(prefilled, 16)
            for i in range(0, NT, 8):
                sp.dma_start(moe0[i * P:(i + 8) * P, :].rearrange("(i p) w -> p i w", p=P),
                             xs[:, :, 0:D]).then_inc(prefilled, 16)
            for a, b in ((w1[:, :, 0:H1], w1_in.rearrange("e d h -> d e h")), (w1[:, :, H1:H1 + 2], b1_in),
                         (w2[:, :, :].rearrange("p e (f o) -> p e f o", f=2), w2_in.rearrange("e (f p) o -> p e f o", p=P)),
                         (wv[:, :], wv_in), (wu[:, :], wu_in), (wg1[:, :], wg1_in), (wo[:, :], wo_in),
                         (bu[:, :], bu_in.partition_broadcast(P)), (bv[:, :], bv_in.partition_broadcast(P)),
                         (bo[:, :], bo_in.partition_broadcast(P))):
                for e in (range(E) if b.ndim == 4 else [None]):
                    sp.dma_start(a if e is None else a[:, e], b if e is None else b[:, e]).then_inc(l1_w_loaded, 16)

            def expert_rows(l, src, n_iter):
                for m in range(UNROLL):
                    sp.dma_start(xs[:, m, :], src[m * P:(m + 1) * P, :]).then_inc(xs_loaded[l][m], 16)
                with sp.Fori(1, n_iter) as it:
                    for m in range(UNROLL):
                        sp.wait_ge(sent_back[l][m], it * 16)
                        n = it * UNROLL + m
                        sp.dma_start(xs[:, m, :], src[bass.ds(n * P, P), :]).then_inc(xs_loaded[l][m], 16)

            sp.wait_ge(prefilled, 16 * N_FILL)
            sp.wait_ge(sent0, 16 * NT)
            expert_rows(0, slots0, TILES0 // UNROLL)
            for m in range(UNROLL):
                sp.wait_ge(sent_back[0][m], 16 * (TILES0 // UNROLL))
            sp.dma_start(bmoe[:, :, :], b2_in.rearrange("e d -> (e d)").partition_broadcast(P)).then_inc(b2_loaded, 16)
            for g in range(B):
                if g:
                    sp.wait_ge(y0_used, J * g)
                sp.dma_start(y0, moe0[g * L:(g + 1) * L, :].rearrange("(j p) d -> p j d", p=P)).then_inc(y0_loaded, 16)
            for c in range(NC):
                sp.wait_ge(x_full, 2 * c + 2)
                sp.dma_start(mats[:, c, :, :], iv_in[:, c * 4 * P:(c + 1) * 4 * P]).then_inc(iv_loaded[c], 16)
            for s in sent1:
                sp.wait_ge(s, 16 * NT // 2)
            expert_rows(1, slots1, TILES1 // UNROLL)
            for m in range(UNROLL):
                sp.wait_ge(sent_back[1][m], 16 * (TILES1 // UNROLL))
            sp.wait_ge(wo_done, NT // 4)
            for q in range(NT // 4):
                sp.dma_start(moe_back[q], moe1[q * 1024:(q + 1) * 1024, :].rearrange(
                    "(i p k) d -> p i k d", p=P, k=2)).then_inc(back_loaded[q], 16)
            ov = out.rearrange("b (j p) d -> p (b j) d", p=P)
            for q in range(NT // 4):
                sp.wait_ge(out_ready, q + 1)
                sp.dma_start(ov[:, 4 * q:4 * q + 4, :], xres[:, 4 * q:4 * q + 4, :]).then_inc(stored, 16)
            sp.wait_ge(stored, 16 * (NT // 4))

        @block.gpsimd
        def _(pool):
            pool.memset(xs[:, :, 0:D], 0.0).then_inc(fill_ready, 1)
            pool.memset(xs[:, :, D:ROWW].bitcast(I32), 1 << 24).then_inc(fill_ready, 1)
            pool.memset(onesb[:, :], 1.0).then_inc(ones_done, 1)
            pool.memset(ones8[:, :], 1.0).then_inc(ones_done, 1)
            pool.wait_ge(cst_loaded, 16)
            ids = row[:, :, D:ROWW].rearrange("p i w -> p (i w)").bitcast(I32)
            pool.tensor_copy(ids, col("token").bitcast(I32)).then_inc(ids_done, 1)

            def inverse_std(k):
                g = slice(J * (k % B), J * (k % B) + J)
                pool.wait_ge(aggr_done, J * (k + 1))
                pool.tensor_scalar(veps[:, g], mv[:, g, 1], 1e-5, None, ALU.add).then_inc(veps_done, 1)
                pool.wait_ge(veps_done, k + 1)
                pool.tensor_tensor(rstd[:, g], veps[:, g], col("minus_half"), ALU.pow).then_inc(rstd_done, 1)

            def scatter_rows(dst, slots, bound, done, tiles=range(NT)):
                for i in tiles:
                    pool.indirect_dma_start(dst[:, :], bass.IndirectOffsetOnAxis(ap=slots[:, i:i + 1], axis=0),
                                            row[:, i, :], None, bounds_check=bound,
                                            oob_is_err=False).then_inc(done, 16)

            def rope_add(b):
                for u in range(4):
                    n = 4 * b + u
                    pool.wait_ge(rope_mul, 2 * (n + 1))
                    o = qk[b % 2][:, u % 2, 512 * (u // 2):512 * (u // 2) + 512]
                    pool.tensor_tensor(o, o, rtmp[:, n % 2, :], ALU.add).then_inc(rope_done, 1)

            def expert_back(l, dst, bound, n_iter):
                for n in range(UNROLL * n_iter):
                    m = n % UNROLL
                    pool.wait_ge(e_ys[l], n + 1)
                    pool.wait_ge(xs_loaded[l][m], (n // UNROLL) * 16 + 16)
                    pool.indirect_dma_start(
                        dst[:, :], bass.IndirectOffsetOnAxis(ap=xs[:, m, D:ROWW].bitcast(I32), axis=0),
                        ys[:, m, :], None, bounds_check=bound, oob_is_err=False).then_inc(sent_back[l][m], 16)

            for k in range(B):
                inverse_std(k)
            pool.wait_ge(xn_done, NT)
            pool.wait_ge(ids_done, 1)
            pool.wait_ge(prefilled, 16 * N_FILL)
            pool.wait_ge(slot0_ready, 1)
            rope_add(0)
            scatter_rows(slots0, slot0, SLOTS0 - 1, sent0, range(NT // 2))
            rope_add(1)
            scatter_rows(slots0, slot0, SLOTS0 - 1, sent0, range(NT // 2, NT))
            rope_add(2)
            expert_back(0, moe0, T - 1, TILES0 // UNROLL)
            rope_add(3)

            pool.wait_ge(sent0, 16 * NT)
            for k in range(B, 2 * B):
                inverse_std(k)
            pool.tensor_copy(ids, col("token2").bitcast(I32)).then_inc(ids_done, 1)
            pool.wait_ge(l1_w_loaded, 16 * N_L1W)
            for g in range(B):
                pool.wait_ge(xn_done, NT + J * (g + 1))
                r_ = xres[:, J * g:J * (g + 1), :]
                pool.tensor_tensor(r_, r_, bo[:, :].unsqueeze(1).to_broadcast([P, J, D]), ALU.add).then_inc(bo_done, 1)
            pool.wait_ge(ids_done, 2)
            pool.wait_ge(slot1_ready, 2)
            for h in range(2):
                scatter_rows(slots1, slot1, SLOTS1 - 1, sent1[h], range(h * NT // 2, (h + 1) * NT // 2))
            for h in range(2):
                pool.wait_ge(sent1[h], 16 * NT // 2)
                pool.tensor_copy(ids[:, h * NT // 2:(h + 1) * NT // 2],
                                 col("token2b").bitcast(I32)[:, h * NT // 2:(h + 1) * NT // 2]).then_inc(ids_done, 1)
                pool.wait_ge(ids_done, 3 + h)
                scatter_rows(slots1, slot2, SLOTS1 - 1, sent1[2 + h], range(h * NT // 2, (h + 1) * NT // 2))
            expert_back(1, moe1, 2 * T - 1, TILES1 // UNROLL)

        @block.scalar
        def _(act):
            act.wait_ge(cst_loaded, 16)
            for o, name in ((identb, "ident"), (beforeb, "before"), (maskb, "mask")):
                act.activation(o[:, :], col(name), ACT.Copy).then_inc(casts_done, 1)

            def take_transposes(k0):
                for u in range(2):
                    act.wait_ge(tr_full, k0 + u + 1)
                    act.activation(xT[:, 512 * ((k0 + u) % 8):512 * ((k0 + u) % 8) + 512], TP[u][:, :],
                                   ACT.Copy).then_inc(tr_free, 1)

            for g in range(B):
                take_transposes(2 * g)
                for u in range(4):
                    n = 4 * g + u
                    i = 2 * n
                    act.wait_ge(vg_full, n + 1)
                    pv = O[n % 2][:, 0:2 * VGW].rearrange("p (i w) -> p i w", w=VGW)
                    act.activation(vsb[:, i:i + 2, :], pv[:, :, 0:D], ACT.Copy)
                    act.activation(lg[:, :, i:i + 2].rearrange("p e i -> p i e"), pv[:, :, D:VGW],
                                   ACT.Copy).then_inc(vg_free, 1)

            for k, (fb, sc) in enumerate(((f1b, 1.0), (f2b, 0.5))):
                act.wait_ge(filt_loaded, 96)
                act.wait_ge(f_full, k + 1)
                act.activation(hx[0:FO, :], S[k][0:FO, :, :].rearrange("p a m -> p (a m)"), ACT.Identity,
                               bias=fb, scale=sc).then_inc(f_act, 1)
                act.wait_ge(f_dve, 4 * k + 3)
                act.activation(hg[0:FO, :], ht[0:FO, :], ACT.Tanh, scale=float(np.sqrt(2 / np.pi))).then_inc(f_act, 1)
                if k == 0:
                    act.wait_ge(rt, R0_REL)
                    act.activation(flat(expl), flat(rel), ACT.Exp).then_inc(rt_exp, 1)
            for u in range(4):
                act.wait_ge(fs_full, u + 1)
                act.activation(hspec[:, 2 * u:2 * u + 2, :, :].rearrange("p c a d -> p (c a d)"),
                               TO[u][:, :], ACT.Copy).then_inc(fs_free, 1)
            act.wait_ge(fs_free, 4)
            for a in range(2):
                act.activation(hspec0[:, a, :, :], hspec[:, 0, a, :].unsqueeze(1).to_broadcast([P, 2, D]),
                               ACT.Copy).then_inc(hspec_done, 1)
            act.wait_ge(hspec_done, 2)
            act.activation(hspec0[0:1, 0, 1, :], hspec[0:1, 0, 1, :], ACT.Copy).then_inc(hspec_done, 1)

            def exp_rows(n):
                i = n % J
                act.wait_ge(bias_done, n + 1)
                if n >= 2:
                    act.wait_ge(pt_full, pt_full_at(n - 2, (i - 2) % J // 4))
                act.activation(prob[n % 2][:, 0:(i + 1) * P],
                               S[n % 2][:, :, :].rearrange("p a m -> p (a m)")[:, 0:(i + 1) * P], ACT.Exp,
                               bias=negmax[:, n:n + 1], scale=SCALE,
                               accum_out=rsum[:, n:n + 1]).then_inc(exp_done, 1)

            def take_pt(n):
                act.wait_ge(pt_full, pt_full_at(n, 0))
                if n >= 2:
                    act.wait_ge(o_full, n - 1)
                k = min(4, n % J + 1)
                act.activation(pT[n % 2][:, 0:k, :].rearrange("p j q -> p (j q)"), t_bank("p", n, 0)[:, 0:k * P],
                               ACT.Copy).then_inc(pt_act, 1)

            exp_rows(0)
            for n in range(NT):
                take_pt(n)
                if n + 1 < NT:
                    exp_rows(n + 1)
                for k in moe0_tiles(n):
                    act.wait_ge(e_t[0], k + 1)
                    if k >= 2:
                        act.wait_ge(e_y[0], k - 1)
                    act.activation(xsT[:, k % 2, :], t_bank("x", k)[:, 0:P], ACT.Copy).then_inc(e_xT[0], 1)

            for g in range(B):
                take_transposes(2 * B + 2 * g)
            act.wait_ge(g_full, 1)
            act.activation(flat(lg), O[0][:, 0:E * NT].rearrange("p (i e) -> p e i", e=E), ACT.Copy).then_inc(lg1_done, 1)
            act.wait_ge(rt, R1_REL)
            act.activation(flat(expl), flat(rel), ACT.Exp).then_inc(rt_exp, 1)
            act.wait_ge(rt, R1_M2)
            act.activation(em2[:, :], m2[:, :], ACT.Exp).then_inc(rt_exp, 1)

            def take_inverse(v):
                act.wait_ge(b_full, v + 1)
                act.activation(spec[v // NC][:, v % NC, :, :].rearrange("p a w -> p (a w)"),
                               TO[v % 4] if v < NC else c_bank("inv", v), ACT.Copy).then_inc(b_free, 1)

            def take_y(q):
                act.wait_ge(yt_full, q + 1)
                act.activation(yT[:, 512 * q:512 * q + 512], c_bank("yt", q), ACT.Copy).then_inc(yt_free, 1)

            for v in range(NC):
                take_inverse(v)

            def copy_w1(n):
                e = act.value_load(expert[0:1, n:n + 1], min_val=0, max_val=E - 1)
                if n >= W1_RING:
                    act.wait_ge(e_h, n - W1_RING + 1)
                    wait_hidden(act, n - W1_RING)
                act.activation(w1r[:, n % W1_RING, :], w1[:, bass.ds(e, 1), :].rearrange("p e h -> p (e h)"),
                               ACT.Copy).then_inc(e_w1, 1)

            def take_rows(n):
                act.wait_ge(e_t[1], n + 1)
                if n >= 2:
                    act.wait_ge(e_h, n - 1)
                act.activation(xsT[:, n % 2, :], TP[n % 2][:, 0:P], ACT.Copy).then_inc(e_xT[1], 1)

            def hidden(n):
                act.wait_ge(e_h, n + 1)
                if n >= 2:
                    act.wait_ge(e_y[1], n - 1)
                for f in range(2):
                    last = act.activation(hT[:, n % 2, f, :], S[0][:, n % 2, f * P:(f + 1) * P], ACT.Relu,
                                          bias=w1r[:, n % W1_RING, H1 + f:H1 + f + 1])
                last.then_inc(e_ha, 1)

            act.wait_ge(expert_ready, 1)
            for n in range(-3, TILES1):
                if n + 3 < TILES1:
                    copy_w1(n + 3)
                if 0 <= n + 2 < TILES1:
                    take_rows(n + 2)
                if 0 <= n + 1 < TILES1 and n % 2:
                    hidden(n + 1)
                for kind, k in conv_pe_at(n):
                    if kind == "inv":
                        take_inverse(k)
                    if kind == "yt":
                        take_y(k)
            for q in range(NT // 4):
                act.wait_ge(back_loaded[q], 16)
                for t in range(4):
                    i = 4 * q + t
                    last = act.activation(moe_back[q][:, t, 1, :], moe_back[q][:, t, 1, :], ACT.Copy,
                                          scale=gate2[:, i:i + 1])
                last.then_inc(gated2, 1)

        @block.tensor
        def _(pe):
            def mm(o, lhsT, rhs, start=True, stop=True):
                return pe.matmul(o, lhsT, rhs, start=start, stop=stop)

            def transpose_tokens(k):
                for u in range(2):
                    n = 2 * k + u
                    if n >= 2:
                        pe.wait_ge(tr_free, n - 1)
                    for q in range(4):
                        i = 4 * (n % 8) + q
                        pe.wait_ge(xn_done, NT * (k // B) + i + 1)
                        last = pe.transpose(TP[u][:, q * P:(q + 1) * P], row[:, i, 0:D], ident)
                    last.then_inc(tr_full, 1)

            def values_and_gates(g):
                for u in range(4):
                    n = 4 * g + u
                    pe.wait_ge(tr_free, 2 * g + u // 2 + 1)
                    if n >= 2:
                        pe.wait_ge(vg_free, n - 1)
                    for q in range(2):
                        i = 2 * n + q
                        last = mm(O[n % 2][:, q * VGW:(q + 1) * VGW], xT[:, i * P:(i + 1) * P], wvg)
                    last.then_inc(vg_full, 1)

            def routing_counts(k):
                pe.wait_ge(rt, (R0_OH, R1_OH)[k])
                oh = ohb[:, :, :].rearrange("p e i -> p (e i)")
                mm(O[0][:, 0:E * NT], beforeb[:, :], oh)
                mm(O[0][:, E * NT:2 * E * NT], onesb[:, :], oh).then_inc(rt_mm, 1)

            def filter_network():
                pe.wait_ge(filt_loaded, 96)
                for k in range(2):
                    if k:
                        pe.wait_ge(f_dve, 4)
                    for h in range(2):
                        r = (pe_sb[0:FO, :], hg[0:FO, :])[k][:, 512 * h:512 * h + 512]
                        last = mm(S[k][0:FO, h, :], (f1w, f2w)[k], r)
                    last.then_inc(f_full, 1)
                    if k == 0:
                        routing_counts(0)
                pe.wait_ge(f_dve, 9)
                for j in range(J):
                    last = mm(S[0][:, j // 4, (j % 4) * P:(j % 4) * P + P], hg[0:FO + 1, j * P:(j + 1) * P], f3w)
                last.then_inc(f_full, 1)

            def dft(o, a, c, s):
                for n in range(2):
                    mm(o[n], mats[:, c, 2 * n, :], a[:, 0, :], stop=False)
                    last = mm(o[n], mats[:, c, 2 * n + 1, :], a[:, 1, :], start=False)
                last.then_inc(s, 1) if s else None

            def filter_spectrum():
                pe.wait_ge(fw_loaded, 16)
                pe.wait_ge(rad, RAD_F)
                for c in range(NC):
                    o = TO[c // 2][:, 256 * (c % 2):256 * (c % 2) + 256].rearrange("p (a w) -> p a w", a=2)
                    dft([o[:, 0, :], o[:, 1, :]], filt_spec[:, c, :, :], c, fs_full if c % 2 else None)

            def project(b):
                for u in range(4):
                    n = 4 * b + u
                    slot = S[(n + 1) % 2]
                    wait_scores_bank(("pr", n))
                    for a in range(2):
                        last = mm(slot[:, a, :], wqk[:, 2 * (u % 2) + a, :],
                                  xT[:, b * L + 512 * (u // 2):b * L + 512 * (u // 2) + 512])
                    last.then_inc(pr_full, 1)

            def scores(n):
                b, i = n // J, n % J
                wait_scores_bank(("s", n))
                pe.wait_ge(rope_done, 4 * b + (2 if i < 4 else 4))
                q = qk[b % 2][:, 0, i * P:(i + 1) * P]
                for c in range((i + 4) // 4):
                    w = min(512, (i + 1) * P - 512 * c)
                    diagonal = c == i // 4
                    last = mm(S[n % 2][:, c, 0:w], q, qk[b % 2][:, 1, 512 * c:512 * c + w], stop=not diagonal)
                    if diagonal:
                        last = mm(S[n % 2][:, c, w - P:w], identb[:, :], maskb[:, :], start=False)
                last.then_inc(s_full, 1)

            def wait_scores_bank(use):
                before = LAST_S[use]
                if before is not None:
                    kind, n = before
                    pe.wait_ge(*((rope_mul, 2 * n + 2) if kind == "pr" else (exp_done, n + 1)))

            def transpose_probs(n):
                i = n % J
                pe.wait_ge(exp_done, n + 1)
                for c in range((i + 4) // 4):
                    wait_emptied(pe, T_USES, T_AT[("p", n, c)])
                    for j in range(4 * c, min(4 * c + 4, i + 1)):
                        last = pe.transpose(t_bank("p", n, c)[:, (j - 4 * c) * P:(j - 4 * c + 1) * P],
                                            prob[n % 2][:, j * P:(j + 1) * P], ident)
                    last.then_inc(pt_full, 1)

            def weigh_values(n):
                b, i = n // J, n % J
                wait_emptied(pe, O_USES, O_AT[("o", n)])
                pe.wait_ge(pt_act, n + 1)
                for j in range(i + 1):
                    if j == 4:
                        pe.wait_ge(pt_dve, SECOND.index(n) + 1)
                    last = mm(o_bank("o", n)[:, 0:D], pT[n % 2][:, j, :], vsb[:, b * J + j, :], start=j == 0, stop=j == i)
                last.then_inc(o_full, 1)

            def expert0_rows(k):
                pe.wait_ge(xs_loaded[0][k % UNROLL], 16 * (k // UNROLL + 1))
                wait_emptied(pe, T_USES, T_AT[("x", k)])
                pe.transpose(t_bank("x", k)[:, 0:P], xs[:, k % UNROLL, 0:D], ident).then_inc(e_t[0], 1)

            def expert0_out(k):
                pe.wait_ge(e_xT[0], k + 1)
                wait_emptied(pe, O_USES, O_AT[("y", k)])
                mm(o_bank("y", k)[:, 0:D], xsT[:, k % 2, :], w0[:, k * P // CAP, :]).then_inc(e_y[0], 1)

            pe.wait_ge(cst_loaded, 16)
            pe.wait_ge(w_a_loaded, 16)
            for g in range(B):
                transpose_tokens(g)
                values_and_gates(g)
            pe.wait_ge(casts_done, 3)
            pe.wait_ge(ones_done, 2)
            pe.wait_ge(vg_free, 16)
            filter_network()
            pe.wait_ge(rt, R0_CUM)
            filter_spectrum()
            pe.wait_ge(fs_free, 4)
            pe.wait_ge(f_dve, 11)
            pe.wait_ge(rope_loaded, 32)
            project(0)
            scores(0)
            for n in range(NT):
                if n % J == 4 and n // J + 1 < B:
                    project(n // J + 1)
                if n + 1 < NT:
                    scores(n + 1)
                transpose_probs(n)
                if n:
                    weigh_values(n - 1)
                for k in moe0_tiles(n):
                    if k == 0:
                        pe.wait_ge(moe0_w_loaded, 32)
                    expert0_rows(k)
                    if k % MOE0_STEP:
                        expert0_out(k - 1)
                if moe0_tiles(n):
                    expert0_out(moe0_tiles(n)[-1])
            weigh_values(NT - 1)

            def gates(g):
                for i in range(J * g, J * g + J):
                    pe.wait_ge(tr_free, 2 * B + i // 4 + 1)
                    last = mm(O[0][:, i * E:(i + 1) * E], xT[:, i * P:(i + 1) * P], wg1[:, :])
                return last

            def project_vu(q):
                if q >= 2:
                    pe.wait_ge(v_done, q - 1)
                    pe.wait_ge(u_done, q - 1)
                for t in range(4):
                    i = 4 * q + t
                    xt = xT[:, i * P:(i + 1) * P]
                    mm(S[q % 2][:, 0, t * D:(t + 1) * D], xt, wv[:, :])
                    last = mm(S[q % 2][:, 1, t * D:(t + 1) * D], xt, wu[:, :])
                last.then_inc(uvg_full, 1)

            pe.wait_ge(pt_act, NT)
            pe.wait_ge(pt_dve, len(SECOND))
            pe.wait_ge(l1_w_loaded, 16 * N_L1W)
            for g in range(B):
                transpose_tokens(B + g)
                if g == 0:
                    pe.wait_ge(o_done, NT)
                elif g == B - 1:
                    project_vu(0)
                    project_vu(1)
                last = gates(g)
            last.then_inc(g_full, 1)
            routing_counts(1)
            for q in range(2, NT // 4):
                project_vu(q)
            pe.wait_ge(v_done, NT // 4)
            pe.wait_ge(u_done, NT // 4)

            def forward(u):
                if u < 2:
                    pe.wait_ge(rad, RAD_F * (u + 2))
                if u >= 4:
                    pe.wait_ge(x_free, u - 3)
                dft([SB[u % 4][:, 0:W], SB[u % 4][:, W:2 * W]], spec[u % 2][:, u // 2, :, :], u // 2, x_full)

            def inverse(v):
                hf, c = divmod(v, NC)
                pe.wait_ge(y_ready, 2 * c + hf + 1)
                pe.wait_ge(iv_loaded[c], 16)
                if v >= NC:
                    wait_c_emptied(pe, "inv", v)
                elif v >= 4:
                    pe.wait_ge(b_free, v - 3)
                o = TO[v % 4] if v < NC else c_bank("inv", v)
                dft([o[:, 0:W], o[:, W:2 * W]], spec[hf][:, c, :, :], c, b_full)

            LAG = 3
            for c in range(NC + LAG):
                if c < NC:
                    forward(2 * c)
                    forward(2 * c + 1)
                if c == LAG:
                    pe.wait_ge(rt, R1_CUM)
                if c >= LAG:
                    inverse(c - LAG)
            pe.wait_ge(x_free, 2 * NC)
            pe.wait_ge(b_free, NC)

            def transpose_y(q):
                if q % 4 == 0:
                    pe.wait_ge(conv_done, 2 * (q // 4) + 2)
                wait_c_emptied(pe, "yt", q)
                for t in range(4):
                    b, j = divmod(4 * q + t, J)
                    last = pe.transpose(c_bank("yt", q)[:, t * P:(t + 1) * P],
                                        vv[b // 2][:, j, (b % 2) * D:(b % 2 + 1) * D], ident)
                last.then_inc(yt_full, 1)

            def project_y(q):
                pe.wait_ge(yt_free, q + 1)
                wait_c_emptied(pe, "wo", q)
                for t in range(4):
                    i = 4 * q + t
                    last = mm(c_bank("wo", q)[:, t * D:(t + 1) * D], yT[:, i * P:(i + 1) * P], wo[:, :])
                last.then_inc(wo_full, 1)

            def expert_rows(n):
                pe.wait_ge(xs_loaded[1][n % UNROLL], 16 * (n // UNROLL + 1))
                if n >= 2:
                    pe.wait_ge(e_xT[1], n - 1)
                pe.transpose(TP[n % 2][:, 0:P], xs[:, n % UNROLL, 0:D], ident).then_inc(e_t[1], 1)

            def expert_hidden(n):
                pe.wait_ge(e_xT[1], n + 1)
                pe.wait_ge(e_w1, n + 1)
                if n >= 2:
                    wait_hidden(pe, n - 2)
                for f in range(2):
                    last = mm(S[0][:, n % 2, f * P:(f + 1) * P], w1r[:, n % W1_RING, f * P:(f + 1) * P], xsT[:, n % 2, :])
                last.then_inc(e_h, 1)

            def expert_out(n):
                e = pe.value_load(expert[0:1, n:n + 1], min_val=0, max_val=E - 1)
                we = w2[:, bass.ds(e, 1), :].rearrange("p e d -> p (e d)")
                if n >= 2:
                    pe.wait_ge(e_ys[1], n - 1)
                wait_hidden(pe, n)
                mm(O[n % 2][:, 0:D], hT[:, n % 2, 0, :], we[:, 0:D], stop=False)
                mm(O[n % 2][:, 0:D], hT[:, n % 2, 1, :], we[:, D:2 * D], start=False).then_inc(e_y[1], 1)

            pe.wait_ge(expert_ready, 1)
            for n in range(-2, TILES1):
                if n + 2 < TILES1:
                    expert_rows(n + 2)
                if 0 <= n + 1 < TILES1:
                    expert_hidden(n + 1)
                if 0 <= n:
                    expert_out(n)
                for kind, k in conv_pe_at(n):
                    {"inv": inverse, "yt": transpose_y, "wo": project_y}[kind](k)

        @block.vector
        def _(dve):
            tt, stt, ts = dve.tensor_tensor, dve.scalar_tensor_tensor, dve.tensor_scalar

            def norm_stats(k):
                g = k % B
                if k < B:
                    dve.wait_ge(x_loaded[g], 16)
                for i in range(J * g, J * g + J):
                    dve.bn_stats(stats[:, i, :], xres[:, i, :]).then_inc(stats_done, 1)
                dve.wait_ge(stats_done, J * (k + 1))
                for i in range(J * g, J * g + J):
                    dve.bn_aggr(mv[:, i, :], stats[:, i, :]).then_inc(aggr_done, 1)

            def norm_rows(k):
                g = k % B
                dve.wait_ge(rstd_done, k + 1)
                for i in range(J * g, J * g + J):
                    ts(row[:, i, 0:D], xres[:, i, :], mv[:, i, 0:1], rstd[:, i:i + 1], ALU.subtract,
                       ALU.mult).then_inc(xn_done, 1)

            def norms(k0):
                norm_stats(k0)
                for k in range(k0 + 1, k0 + B):
                    norm_stats(k)
                    norm_rows(k - 1)
                norm_rows(k0 + B - 1)

            n_rt = [0]

            def rstep(ins):
                ins.then_inc(rt, 1)
                n_rt[0] += 1
                dve.wait_ge(rt, n_rt[0])

            def best_expert(src, rel_out, top, onehot):
                rstep(dve.tensor_reduce(top[:, :], ei(src), X, ALU.max))
                rstep(tt(rel_out[:, :, :], src[:, :, :], over_e(top), ALU.subtract))
                rstep(stt(flat(score), flat(rel_out), 0.0, col("rank"), ALU.is_ge, ALU.mult))
                rstep(dve.tensor_reduce(best[:, :], ei(score), X, ALU.max))
                rstep(tt(onehot[:, :, :], score[:, :, :], over_e(best), ALU.is_equal))

            def inverse_sum(gate):
                rstep(dve.tensor_reduce(best[:, :], ei(expl), X, ALU.add))
                rstep(dve.reciprocal(gate[:, :], best[:, :]))

            def earlier_tokens(k):
                dve.wait_ge(rt_mm, k + 1)
                before, total = O[0][:, 0:E * NT], O[0][:, E * NT:2 * E * NT]
                rstep(dve.tensor_tensor_scan(flat(cum), col("carry"), total, 0.0, ALU.mult, ALU.add))
                rstep(tt(flat(score), flat(cum), total, ALU.subtract))
                rstep(tt(flat(score), flat(score), before, ALU.add))

            def filter_poly(k):
                dve.wait_ge(f_act, 2 * k + 1)
                h, t = hx[0:FO, :], ht[0:FO, :]
                tt(t, h, h, ALU.mult).then_inc(f_dve, 1)
                dve.wait_ge(f_dve, 4 * k + 1)
                ts(t, t, 0.044715, 1.0, ALU.mult, ALU.add).then_inc(f_dve, 1)
                dve.wait_ge(f_dve, 4 * k + 2)
                tt(t, t, h, ALU.mult).then_inc(f_dve, 1)

            def filter_gelu(k):
                dve.wait_ge(f_act, 2 * k + 2)
                stt(hg[0:FO, :], hg[0:FO, :], 1.0, hx[0:FO, :], ALU.add, ALU.mult).then_inc(f_dve, 1)

            n_rad = [0]

            def did(ins):
                ins.then_inc(rad, 1)
                n_rad[0] += 1
                return n_rad[0]

            def after(*steps):
                dve.wait_ge(rad, max(steps))

            def radix_forward(v, a, pm_, ej_, uv_):
                p_, m_ = pm_[:, 0], pm_[:, 1]
                after(n_rad[0])
                s1 = did(tt(p_, v[:, 0:4], v[:, 4:8], ALU.add))
                s2 = did(tt(m_, v[:, 0:4], v[:, 4:8], ALU.subtract))
                after(s1)
                did(tt(a[:, 1], p_[:, 0:2], p_[:, 2:4], ALU.subtract))
                s4 = did(tt(uv_[:, 0], p_[:, 0:2], p_[:, 2:4], ALU.add))
                after(s2)
                did(tt(uv_[:, 1, 0], m_[:, 1], m_[:, 3], ALU.subtract))
                s8 = did(tt(uv_[:, 1, 1], m_[:, 1], m_[:, 3], ALU.add))
                after(s4)
                did(tt(a[:, 0, 0], uv_[:, 0, 0], uv_[:, 0, 1], ALU.add))
                did(tt(a[:, 0, 1], uv_[:, 0, 0], uv_[:, 0, 1], ALU.subtract))
                s11 = did(stt(ej_[:, 0], m_[:, 2:4], RC, v[:, 0:2], ALU.mult, ALU.add))
                s12 = did(stt(ej_[:, 1], p_[:, 2:4], RC, v[:, 4:6], ALU.mult, ALU.add))
                after(s8)
                did(stt(a[:, 2], uv_[:, 1], RC, m_[:, 0:3:2], ALU.mult, ALU.add))
                s10 = did(stt(a[:, 3], uv_[:, 1], -RC, m_[:, 0:3:2], ALU.mult, ALU.add))
                after(s12)
                did(stt(v[:, 0:2], m_[:, 2:4], -RC, v[:, 0:2], ALU.mult, ALU.add))
                s14 = did(stt(v[:, 4:6], p_[:, 2:4], -RC, v[:, 4:6], ALU.mult, ALU.add))
                after(s10)
                did(stt(uv_[:, 0, 0], ej_[:, 1, 1], -TAU, ej_[:, 0, 1], ALU.mult, ALU.add))
                s16 = did(stt(uv_[:, 0, 1], ej_[:, 0, 1], TAU, ej_[:, 1, 1], ALU.mult, ALU.add))
                after(s14)
                did(stt(uv_[:, 1, 0], v[:, 1], -TAU, v[:, 5], ALU.mult, ALU.subtract))
                s18 = did(stt(uv_[:, 1, 1], v[:, 5], -TAU, v[:, 1], ALU.mult, ALU.add))
                after(s16)
                did(stt(a[:, 4], uv_[:, 0], TC, ej_[:, :, 0], ALU.mult, ALU.add))
                did(stt(a[:, 5], uv_[:, 0], -TC, ej_[:, :, 0], ALU.mult, ALU.add))
                after(s18)
                did(stt(a[:, 6], uv_[:, 1], TC, v[:, 0:5:4], ALU.mult, ALU.add))
                did(stt(a[:, 7], uv_[:, 1], -TC, v[:, 0:5:4], ALU.mult, ALU.add))

            def radix_inverse(a, v):
                p_, m_ = pm[:, 0], pm[:, 1]
                v01_45 = v.rearrange("p (s h x) w -> p s h x w", s=2, h=2)[:, :, 0]
                did(tt(ej[:, :, 0], a[:, 4], a[:, 5], ALU.add))
                yield
                s2 = did(tt(uv[:, :, 0], a[:, 6], a[:, 7], ALU.add))
                yield
                after(s2)
                did(tt(a[:, 5], a[:, 4], a[:, 5], ALU.subtract))
                yield
                s4 = did(tt(a[:, 7], a[:, 6], a[:, 7], ALU.subtract))
                yield
                after(s4)
                did(ts(a[:, 5], a[:, 5], TC, None, ALU.mult))
                yield
                s6 = did(ts(a[:, 7], a[:, 7], TC, None, ALU.mult))
                yield
                did(tt(m_[:, 0:3:2], a[:, 2], a[:, 3], ALU.add))
                yield
                s8 = did(tt(a[:, 3], a[:, 2], a[:, 3], ALU.subtract))
                yield
                after(s6)
                did(stt(ej[:, 0, 1], a[:, 5, 1], TAU, a[:, 5, 0], ALU.mult, ALU.add))
                yield
                did(stt(ej[:, 1, 1], a[:, 5, 0], -TAU, a[:, 5, 1], ALU.mult, ALU.add))
                yield
                did(stt(uv[:, 0, 1], a[:, 7, 0], -TAU, a[:, 7, 1], ALU.mult, ALU.add))
                yield
                s12 = did(stt(uv[:, 1, 1], a[:, 7, 1], -TAU, a[:, 7, 0], ALU.mult, ALU.subtract))
                yield
                did(tt(p_[:, 0], a[:, 0, 0], a[:, 0, 1], ALU.add))
                yield
                s14 = did(tt(p_[:, 1], a[:, 0, 0], a[:, 0, 1], ALU.subtract))
                yield
                after(s14)
                did(tt(v01_45, ej[:, :, :], uv[:, :, :], ALU.add))
                yield
                s16 = did(tt(ej[:, :, :], ej[:, :, :], uv[:, :, :], ALU.subtract))
                yield
                did(tt(m_[:, 1], a[:, 3, 0], a[:, 3, 1], ALU.add))
                yield
                s18 = did(tt(m_[:, 3], a[:, 3, 1], a[:, 3, 0], ALU.subtract))
                yield
                s19 = did(tt(p_[:, 2:4], p_[:, 0:2], a[:, 1], ALU.subtract))
                yield
                after(s19)
                did(tt(p_[:, 0:2], p_[:, 0:2], a[:, 1], ALU.add))
                yield
                s21 = did(tt(m_[:, 3], m_[:, 3], ej[:, 0, 1], ALU.add))
                yield
                did(stt(m_[:, 2], ej[:, 0, 0], RC, m_[:, 2], ALU.mult, ALU.add))
                yield
                s23 = did(stt(p_[:, 2:4], ej[:, 1], RC, p_[:, 2:4], ALU.mult, ALU.add))
                yield
                after(s21)
                s24 = did(ts(m_[:, 1:4:2], m_[:, 1:4:2], RC, None, ALU.mult))
                yield
                after(s24)
                did(tt(ej[:, 0], p_[:, 0:2], m_[:, 0:2], ALU.add))
                yield
                s26 = did(tt(ej[:, 1], p_[:, 0:2], m_[:, 0:2], ALU.subtract))
                yield
                did(tt(v[:, 2:4], p_[:, 2:4], m_[:, 2:4], ALU.add))
                yield
                did(tt(v[:, 6:8], p_[:, 2:4], m_[:, 2:4], ALU.subtract))
                yield
                after(s26)
                did(tt(v01_45, v01_45, ej[:, :, :], ALU.add))
                after(n_rad[0])
                yield

            norms(0)
            filter_poly(0)
            dve.wait_ge(vg_free, 16)
            dve.wait_ge(cst_loaded, 16)
            best_expert(lg, rel, m1, oh1)
            rstep(dve.tensor_copy(flat(ohb), flat(oh1)))
            assert n_rt[0] == R0_OH
            filter_gelu(0)
            dve.wait_ge(rt_exp, 1)
            inverse_sum(gate0)
            filter_poly(1)
            earlier_tokens(0)
            assert n_rt[0] == R0_CUM
            rstep(stt(flat(oh2), flat(score), float(CAP), flat(oh1), ALU.is_lt, ALU.mult))
            rstep(tt(flat(score), flat(score), col("e_cap"), ALU.add))
            rstep(stt(flat(score), flat(score), -FAR, flat(oh2), ALU.add, ALU.mult))
            rstep(dve.tensor_reduce(best[:, :], ei(score), X, ALU.add))
            ts(slot0[:, :], best[:, :], FAR, None, ALU.add).then_inc(slot0_ready, 1)
            filter_gelu(1)
            dve.memset(hg[FO:FO + 1, :], 2.0).then_inc(f_dve, 1)
            dve.wait_ge(f_full, 3)
            for h in range(2):
                tt(filt_v[:, 4 * h:4 * h + 4, :], S[0][:, h, :].rearrange("p (j w) -> p j w", w=D),
                   col("decay")[:, 4 * h:4 * h + 4].unsqueeze(2).to_broadcast([P, 4, D]), ALU.mult).then_inc(f_dve, 1)
            dve.wait_ge(f_dve, 11)
            radix_forward(filt_v, filt_spec, filt_pm, filt_ej, filt_uv)
            assert n_rad[0] == RAD_F
            dve.wait_ge(hspec_done, 2)
            dve.memset(hspec0[0:1, 1, :, :], 0.0).then_inc(hspec_done, 1)

            def rope_products(b):
                for u in range(4):
                    n = 4 * b + u
                    c = slice(512 * (u // 2), 512 * (u // 2) + 512)
                    if n >= 2:
                        dve.wait_ge(rope_done, n - 1)
                    dve.wait_ge(pr_full, n + 1)
                    slot = S[(n + 1) % 2]
                    tt(qk[b % 2][:, u % 2, c], slot[:, 0, :], rope[:, 0, c], ALU.mult).then_inc(rope_mul, 1)
                    tt(rtmp[:, n % 2, :], slot[:, 1, :], rope[:, 1, c], ALU.mult).then_inc(rope_mul, 1)

            def row_max(n):
                dve.wait_ge(s_full, n + 1)
                dve.tensor_reduce(negmax[:, n:n + 1],
                                  S[n % 2][:, :, :].rearrange("p a m -> p (a m)")[:, 0:(n % J + 1) * P], X, ALU.max,
                                  negate=True).then_inc(max_done, 1)
                dve.wait_ge(max_done, n + 1)
                ts(negmax[:, n:n + 1], negmax[:, n:n + 1], SCALE, None, ALU.mult).then_inc(bias_done, 1)

            def take_pt(n):
                if n not in SECOND:
                    return
                dve.wait_ge(pt_full, pt_full_at(n, 1))
                dve.wait_ge(o_full, n - 1)
                k = n % J + 1 - 4
                dve.tensor_copy(pT[n % 2][:, 4:4 + k, :].rearrange("p j q -> p (j q)"),
                                t_bank("p", n, 1)[:, 0:k * P]).then_inc(pt_dve, 1)

            def attention_row(n):
                dve.wait_ge(o_full, n + 1)
                dve.wait_ge(rrec_done, n + 1)
                stt(xres[:, n, :], o_bank("o", n)[:, 0:D], rrec[:, n:n + 1], xres[:, n, :], ALU.mult,
                    ALU.add).then_inc(o_done, 1)

            def expert0_bias(k):
                m = k % UNROLL
                if k >= UNROLL:
                    dve.wait_ge(sent_back[0][m], 16 * (k // UNROLL))
                dve.wait_ge(e_y[0], k + 1)
                tt(ys[:, m, :], o_bank("y", k)[:, 0:D], bmoe[:, k * P // CAP, :], ALU.add).then_inc(e_ys[0], 1)

            def add_experts(i):
                g, j = divmod(i, J)
                dve.wait_ge(y0_loaded, 16 * (g + 1))
                dve.wait_ge(o_done, i + 1)
                stt(xres[:, i, :], y0[:, j, :], gate0[:, i:i + 1], xres[:, i, :], ALU.mult, ALU.add).then_inc(y0_used, 1)

            def tile_stats(i):
                dve.wait_ge(y0_used, i + 1)
                dve.bn_stats(stats[:, i, :], xres[:, i, :]).then_inc(stats_done, 1)

            def tile_aggr(i):
                dve.wait_ge(stats_done, NT + i + 1)
                dve.bn_aggr(mv[:, i, :], stats[:, i, :]).then_inc(aggr_done, 1)

            dve.wait_ge(rope_loaded, 32)
            rope_products(0)
            row_max(0)
            for n in range(NT):
                if n % J == 4 and n // J + 1 < B:
                    rope_products(n // J + 1)
                if n + 1 < NT:
                    row_max(n + 1)
                dve.wait_ge(exp_done, n + 1)
                dve.reciprocal(rrec[:, n:n + 1], rsum[:, n:n + 1]).then_inc(rrec_done, 1)
                take_pt(n)
                if n:
                    attention_row(n - 1)
                for k in moe0_tiles(n):
                    if k == 0:
                        dve.wait_ge(moe0_w_loaded, 32)
                    expert0_bias(k)
                g, stage = divmod(n - ADD_AT, 3)
                if 0 <= g < B - 1:
                    tiles = range(J * g, J * g + J)
                    if stage < 2:
                        for i in tiles:
                            (add_experts, tile_stats)[stage](i)
                    else:
                        for i in tiles:
                            tile_aggr(i)
                        norm_rows(B + g)
            attention_row(NT - 1)
            for stage in (add_experts, tile_stats, tile_aggr):
                for i in range(NT - J, NT):
                    stage(i)

            norm_rows(2 * B - 1)
            dve.wait_ge(l1_w_loaded, 16 * N_L1W)

            def take_vu(q):
                b, j = divmod(4 * q, J)
                dve.wait_ge(uvg_full, q + 1)
                tt(vv[b // 2][:, j:j + 4, (b % 2) * D:(b % 2 + 1) * D],
                   S[q % 2][:, 0, :].rearrange("p (t d) -> p t d", d=D),
                   bv[:, :].unsqueeze(1).to_broadcast([P, 4, D]), ALU.add).then_inc(v_done, 1)
                tt(uu[:, 4 * q:4 * q + 4, :], S[q % 2][:, 1, :].rearrange("p (t d) -> p t d", d=D),
                   bu[:, :].unsqueeze(1).to_broadcast([P, 4, D]), ALU.add).then_inc(u_done, 1)

            take_vu(0)
            take_vu(1)
            dve.wait_ge(lg1_done, 1)
            n_rt[0] = 15
            best_expert(lg, rel, m1, oh1)
            rstep(stt(flat(score), flat(oh1), -1e30, flat(rel), ALU.mult, ALU.add))
            rstep(dve.tensor_reduce(m2[:, :], ei(score), X, ALU.max))
            rstep(tt(score[:, :, :], score[:, :, :], over_e(m2), ALU.subtract))
            rstep(stt(flat(score), flat(score), 0.0, col("rank"), ALU.is_ge, ALU.mult))
            rstep(dve.tensor_reduce(best[:, :], ei(score), X, ALU.max))
            rstep(tt(oh2[:, :, :], score[:, :, :], over_e(best), ALU.is_equal))
            rstep(tt(flat(ohb), flat(oh1), flat(oh2), ALU.add))
            assert n_rt[0] == R1_OH, n_rt
            dve.wait_ge(rt_exp, 3)
            inverse_sum(gate1)
            rstep(tt(gate2[:, :], em2[:, :], gate1[:, :], ALU.mult))
            earlier_tokens(1)
            assert n_rt[0] == R1_CUM, n_rt
            rstep(ts(cnt_i[:, :], cum[:, :, NT - 1], float(P - 1), None, ALU.add))
            rstep(ts(cnt_t[:, :], cnt_i[:, :], 7, None, ALU.arith_shift_right))
            rstep(dve.tensor_copy(ntile[:, :], cnt_t[:, :]))
            dve.wait_ge(ones_done, 2)
            rstep(dve.tensor_tensor_scan(ctile[:, :], ones8[:, :], ntile[:, :], 0.0, ALU.mult, ALU.add))
            rstep(tt(base[:, :], ctile[:, :], ntile[:, :], ALU.subtract))
            rstep(stt(score[:, :, :], base[:, :].unsqueeze(2).to_broadcast([P, E, NT]), float(P), score[:, :, :],
                      ALU.mult, ALU.add))
            for o, onehot, m in ((slot1, oh1, m1), (slot2, oh2, m2)):
                rstep(tt(flat(rel), flat(score), flat(onehot), ALU.mult))
                rstep(dve.tensor_reduce(m[:, :], ei(rel), X, ALU.add))
                dve.tensor_copy(o[:, :], m[:, :]).then_inc(slot1_ready, 1)
            rstep(tt(ecmp[:, :, :], ctile[0:1, :].unsqueeze(1).to_broadcast([1, TILES1, E]),
                     cst[0:1, CONST["tile_no"][0]:CONST["tile_no"][1]].rearrange("p (n e) -> p n e", e=E), ALU.is_le))
            rstep(dve.tensor_reduce(ecnt[:, :], ecmp[:, :, :], X, ALU.add))
            ts(expert[:, :], ecnt[:, :], float(E - 1), None, ALU.min).then_inc(expert_ready, 1)

            for q in range(2, NT // 4):
                take_vu(q)
            for hf in range(HALF):
                radix_forward(vv[hf], spec[hf], pm, ej, uv)
            dve.wait_ge(hspec_done, 4)
            for u in range(2 * NC):
                c, hf = divmod(u, 2)
                dve.wait_ge(x_full, u + 1)
                if u >= 2:
                    dve.wait_ge(y_ready, u - 1)
                t_ = [prod[:, 2 * (u % 2) + a] for a in range(2)]
                for a in range(2):
                    shape, x_ = ([P, 2, 2, D], "p (a b d) -> p a b d") if c == 0 else ([P, 4, D], "p (a d) -> p a d")
                    kw = dict(a=2, d=D) if c == 0 else dict(d=D)
                    h_ = hspec0[:, a, :, :].unsqueeze(2) if c == 0 else hspec[:, c, a, :].unsqueeze(1)
                    o_ = t_[a].rearrange("p a w -> p (a w)").rearrange(x_, **kw)
                    tt(o_, SB[u % 4].rearrange(x_, **kw), h_.to_broadcast(shape), ALU.mult).then_inc((pmul, x_free)[a], 1)
                dve.wait_ge(pmul, u + 1)
                dve.wait_ge(x_free, u + 1)
                y = spec[hf][:, c]
                tt(y[:, 0], t_[0][:, 0], t_[1][:, 1], ALU.subtract)
                tt(y[:, 1], t_[0][:, 1], t_[1][:, 0], ALU.add).then_inc(y_ready, 1)

            def convolution_back():
                dve.wait_ge(y_ready, 2 * NC)
                for hf in range(HALF):
                    dve.wait_ge(b_free, NC * (hf + 1))
                    yield from radix_inverse(spec[hf], vv[hf])
                    for b in range(2 * hf, 2 * hf + 2):
                        v_ = vv[hf][:, :, (b % 2) * D:(b % 2 + 1) * D]
                        tt(v_, v_, uu[:, J * b:J * b + J, :], ALU.mult).then_inc(conv_done, 1)
                        yield

            def add_y(q):
                dve.wait_ge(wo_full, q + 1)
                dve.wait_ge(bo_done, B)
                r_ = xres[:, 4 * q:4 * q + 4, :]
                tt(r_, c_bank("wo", q).rearrange("p (t d) -> p t d", d=D), r_, ALU.add).then_inc(wo_done, 1)

            def expert1_hidden(n):
                dve.wait_ge(e_h, n + 1)
                if n >= 2:
                    dve.wait_ge(e_y[1], n - 1)
                for f in range(2):
                    last = ts(hT[:, n % 2, f, :], S[0][:, n % 2, f * P:(f + 1) * P],
                              w1r[:, n % W1_RING, H1 + f:H1 + f + 1], 0.0, ALU.add, ALU.max)
                last.then_inc(e_hd, 1)

            def expert1_bias(n):
                m = n % UNROLL
                e = dve.value_load(expert[0:1, n:n + 1], min_val=0, max_val=E - 1)
                if n >= UNROLL:
                    dve.wait_ge(sent_back[1][m], 16 * (n // UNROLL))
                dve.wait_ge(e_y[1], n + 1)
                tt(ys[:, m, :], O[n % 2][:, 0:D], bmoe[:, bass.ds(e, 1), :].rearrange("p e d -> p (e d)"),
                   ALU.add).then_inc(e_ys[1], 1)

            dve.wait_ge(expert_ready, 1)
            dve.wait_ge(b2_loaded, 16)
            back = convolution_back()
            for n in range(-1, TILES1):
                if n + 1 < TILES1 and not n % 2:
                    expert1_hidden(n + 1)
                if n >= 0:
                    expert1_bias(n)
                for _ in range(conv_dve_at(n)):
                    next(back)
                for kind, k in conv_pe_at(n):
                    if kind == "wo":
                        add_y(k)
            assert next(back, None) is None
            for q in range(NT // 4):
                dve.wait_ge(back_loaded[q], 16)
                r_ = xres[:, 4 * q:4 * q + 4, :]
                for t in range(4):
                    i = 4 * q + t
                    last = stt(xres[:, i, :], moe_back[q][:, t, 0, :], gate1[:, i:i + 1], xres[:, i, :], ALU.mult, ALU.add)
                last.then_inc(out_a, 1)
                dve.wait_ge(out_a, q + 1)
                dve.wait_ge(gated2, q + 1)
                tt(r_, r_, moe_back[q][:, :, 1, :], ALU.add).then_inc(out_ready, 1)


def kernel(**inputs):
    import concourse.bacc as bacc
    from concourse.bass_utils import run_bass_kernel_spmd

    a = {k: np.asarray(v) for k, v in inputs.items()}
    fw, iv = dft_matrices()
    wq, wk = a["L0_attn_w_q"], a["L0_attn_w_k"]
    swap = np.arange(D) ^ 1
    args = {
        "x": a["L0_attn_x"],
        "cst": constants(),
        "rope": rope_tables(),
        "fw": fw,
        "iv": iv,
        "pe": position_table(),
        "wqk": np.concatenate([wq.T, wq[swap].T, wk.T, wk[swap].T], 1),
        "wvg": np.concatenate([a["L0_attn_w_v"].T, a["L0_ffn_wg"]], 1),
        "w0": a["L0_ffn_W"].transpose(2, 0, 1),
        "b0": a["L0_ffn_b"],
        "f1w": a["L1_attn_W1"],
        "f1b": a["L1_attn_b1"].reshape(FO, 1),
        "f2w": a["L1_attn_W2"],
        "f2b": a["L1_attn_b2"].reshape(FO, 1),
        "f3": np.concatenate([a["L1_attn_W3"], a["L1_attn_b3"][None]], 0),
        "wv": a["L1_attn_Wv"],
        "wu": a["L1_attn_Wu"],
        "wg1": a["L1_ffn_Wg"],
        "bu": a["L1_attn_bu"],
        "bv": a["L1_attn_bv"],
        "wo": a["L1_attn_Wo"],
        "bo": a["L1_attn_bo"],
        "w1": a["L1_ffn_W1"],
        "b1": a["L1_ffn_b1"].reshape(E, 2, P).transpose(2, 0, 1),
        "w2": a["L1_ffn_W2"],
        "b2": a["L1_ffn_b2"],
    }
    nc = bacc.Bacc("TRN2", target_bir_lowering=False, num_devices=1)
    arrays, aps = {}, []
    for name, v in args.items():
        v = np.ascontiguousarray(v)
        arrays[f"in_{name}"] = v
        aps.append(nc.dram_tensor(f"in_{name}", v.shape, mybir.dt.from_np(v.dtype), kind="ExternalInput").ap())
    aps.append(nc.dram_tensor("out", (B, L, D), F32, kind="ExternalOutput").ap())
    two_layer_kernel(nc, *aps)
    return run_bass_kernel_spmd(nc, [arrays], core_ids=[0]).results[0]["out"]
```

```python
from contextlib import ExitStack

import numpy as np

import concourse.bass as bass
from concourse import mybir

F32 = mybir.dt.float32
BF16 = mybir.dt.bfloat16
I32 = mybir.dt.int32
ALU = mybir.AluOpType
ACT = mybir.ActivationFunctionType
X = mybir.AxisListType.X

P = 128
D = 128
B, L = 4, 1024
T = B * L
NT = T // P
J = L // P
E = 8
CAP = T // E
GROUP = CAP // P
H1 = 256
ROWW = D + 1
SLOTS0 = E * CAP
TILES0 = SLOTS0 // P
UNROLL = 8
TILES1 = -(-(2 * T // P + E - 1) // UNROLL) * UNROLL
SLOTS1 = TILES1 * P
FAR = 65536.0
FO = 64
NFFT = 2 * L
KS = (0, 4, 2, 10, 1, 9, 5, 13)
NC = len(KS)
RC = float(np.sqrt(0.5))
TC = float(np.cos(np.pi / 8))
TAU = float(np.tan(np.pi / 8))
HALF = 2
W = (B // HALF) * D
VGW = D + E
SCALE = float(D) ** -0.5

CONST = {}


def _const_columns():
    at = 0
    for name, n in (("ident", P), ("before", P), ("mask", P), ("rank", E * NT), ("e_cap", E * NT),
                    ("carry", E * NT), ("decay", J), ("minus_half", J), ("tile_no", TILES1 * E),
                    ("token", NT), ("token2", NT), ("token2b", NT)):
        CONST[name] = (at, at + n)
        at += n
    return at


NCONST = _const_columns()


def dft_matrices():
    t = np.arange(P)
    fw = np.zeros((NC, 4, P, P))
    iv = np.zeros((NC, 4, P, P))
    for c, k1 in enumerate(KS):
        if c == 0:
            continue
        th = 2 * np.pi * ((t[:, None] * (k1 + 16 * t[None, :])) % NFFT) / NFFT
        co, si = np.cos(th), np.sin(th)
        fw[c] = co, -si, si, co
        iv[c] = co.T, si.T, -si.T, co.T
        iv[c] *= 2 / NFFT
    h = np.arange(P // 2)
    th0 = 2 * np.pi * ((t[:, None] * 16 * h[None, :]) % NFFT) / NFFT
    th8 = 2 * np.pi * ((t[:, None] * (8 + 16 * h[None, :])) % NFFT) / NFFT
    fw[0, 0, :, :64] = np.cos(th0)
    fw[0, 1, :, 64:] = np.cos(th8)
    fw[0, 2, :, :64] = np.sin(th0)
    fw[0, 2, :, 0] = (-1.0) ** t
    fw[0, 3, :, 64:] = np.sin(th8)
    iv[0, 0, :64] = 2 * np.cos(th0).T
    iv[0, 0, 0] = 1
    iv[0, 1, :64] = 2 * np.sin(th0).T
    iv[0, 1, 0] = (-1.0) ** t
    iv[0, 2, 64:] = 2 * np.cos(th8).T
    iv[0, 3, 64:] = 2 * np.sin(th8).T
    iv[0] /= NFFT
    lay = lambda m: np.ascontiguousarray(m.transpose(2, 0, 1, 3).reshape(P, -1), np.float32)
    return lay(fw), lay(iv)


def rope_tables():
    theta = np.float32(10000.0 ** (-2.0 * (np.arange(D // 2) - 1.0) / D))
    ang = np.arange(L, dtype=np.float32)[:, None] * theta.astype(np.float32)[None, :]
    ang = ang.astype(np.float64)
    co = np.repeat(np.cos(ang), 2, axis=1).T
    si = np.repeat(np.sin(ang), 2, axis=1).T * np.where(np.arange(D) % 2, -1.0, 1.0)[:, None]
    return np.ascontiguousarray(np.stack([co, si], 1).reshape(P, -1), np.float32)


def position_table():
    pos = np.arange(L, dtype=np.float32)[:, None]
    div = np.exp(np.arange(0, FO, 2, dtype=np.float32) * np.float32(-(np.log(np.float32(10000.0)) / np.float32(FO))),
                 dtype=np.float64).astype(np.float32)
    ang = (pos * div.astype(np.float32)).astype(np.float32).astype(np.float64)
    pe = np.zeros((L, FO), np.float32)
    pe[:, 0::2] = np.sin(ang)
    pe[:, 1::2] = np.cos(ang)
    return np.ascontiguousarray(pe.T)


def constants():
    c = np.zeros((P, NCONST), np.float32)
    p = np.arange(P)
    put = lambda name, v: c.__setitem__((slice(None), slice(*CONST[name])), np.broadcast_to(v, (P, CONST[name][1] - CONST[name][0])))
    put("ident", np.eye(P))
    put("before", (p[:, None] < p[None, :]))
    put("mask", np.where(p[None, :] > p[:, None], -1e38, 0.0))
    e = np.arange(E)
    put("rank", np.repeat(E - e, NT))
    put("e_cap", np.repeat(e * CAP, NT))
    put("carry", np.tile(np.arange(NT) > 0, E))
    t = np.arange(L, dtype=np.float32).reshape(J, P).T
    put("decay", 0.5 * np.exp(np.float32(-0.01) * t))
    put("minus_half", -0.5)
    put("tile_no", np.repeat(np.arange(TILES1), E))
    token = np.arange(T).reshape(NT, P).T
    c = c.view(np.int32)
    for name, v in (("token", token), ("token2", 2 * token), ("token2b", 2 * token + 1)):
        c[:, slice(*CONST[name])] = v
    return c.view(np.float32)


R0_REL, R0_OH, R0_CUM = 2, 6, 11
R1_REL, R1_M2, R1_OH, R1_CUM = 17, 22, 27, 33
R1_FIRST = 15
RAD_F = 22
N_FILL = (TILES0 + TILES1 + NT) // UNROLL
N_L1W = 2 + E + 4

FILT_RADIX_AT, FILT_DFT_AT = 3, 6
MOE0_FROM = 8
SPLIT_AT = 9
ADD_AT = 21
ROWS_AT = 22
GATES_AT = (27, 30, 31)

BV_AT, BU_AT, BO_AT = 0, D, 2 * D
NBIAS = 3 * D
PARTS = (slice(0, 96), slice(32, 64), slice(64, 96), slice(64, 96))

W_RING = 3
W_COLS = H1 + 2 + 2 * D
RING = (16, 12)
POOL_SUMS = (2, 5)
RADIX_PIECES = 8
INV_BEFORE = 12
N_BACK = 31

LAYER_TURNS = 16 * TILES0 // RING[0]


def turn(l, n):
    return 16 * (n // RING[l] + 1) + l * LAYER_TURNS


def projections_at(n):
    at = {1: [(0, 1)]}
    for b in range(1, B):
        at[J * b - 4] = [(b, 0)]
        at[J * b - 2] = [(b, 1)]
    return at.get(n, [])


def gates_at(n):
    return n in GATES_AT


def expert0_at(n):
    return [n - MOE0_FROM] if 0 <= n - MOE0_FROM < E else []


BV_AT, BU_AT, BO_AT = 0, D, 2 * D
NBIAS = 3 * D


RADIX_PIECES = 8
INV_BEFORE = 12
N_BACK = 31


def conv_dve_at(n):
    return 1 if 0 <= n < HALF * N_BACK else 0


def conv_pe_at(n):
    if 0 <= n < 2 * NC - INV_BEFORE:
        return [("inv", INV_BEFORE + n)]
    for h in range(HALF):
        k = n - (N_BACK * (h + 1) + 1)
        if 0 <= k <= 4:
            return ([("yt", 4 * h + k)] if k < 4 else []) + ([("wo", 4 * h + k - 1)] if k else [])
    return []


def two_layer_kernel(nc, x_in, cst_in, rope_in, fw_in, iv_in, pe_in, wqk_in, wvg_in, w0_in, b0_in,
                     fsmall_in, wv_in, wu_in, wg1_in, bvuo_in, wo_in,
                     w1_in, b1_in, w2_in, b2_in, out):
    ctx = ExitStack()
    with ctx:
        def sb(name, shape, dt=F32):
            return ctx.enter_context(nc.sbuf_tensor(name, shape, dt))

        def ps(name, shape):
            return ctx.enter_context(nc.psum_tensor(name, shape, F32))

        def sem(name):
            return ctx.enter_context(nc.semaphore(name))

        slots0 = nc.dram_tensor("slots0", (SLOTS0, ROWW), F32, kind="Internal").ap()
        slots1 = nc.dram_tensor("slots1", (SLOTS1, ROWW), F32, kind="Internal").ap()
        moe0 = nc.dram_tensor("moe0", (T, D), F32, kind="Internal").ap()
        moe1 = nc.dram_tensor("moe1", (2 * T, D), F32, kind="Internal").ap()

        xres = sb("xres", [P, NT, D])
        row = sb("row", [P, NT, ROWW])
        xT = sb("xT", [P, T])
        cst = sb("cst", [P, NCONST])
        identb = sb("identb", [P, P], BF16)
        beforeb = sb("beforeb", [P, P], BF16)
        maskb = sb("maskb", [P, P], BF16)
        onesb = sb("onesb", [P, P], BF16)
        w0 = sb("w0", [P, E, D])
        b2 = sb("b2", [P, E, D])
        bias = sb("bias", [P, NBIAS])
        biasb = sb("biasb", [P, NBIAS], BF16)
        pickb = sb("pickb", [P, P], BF16)
        w12 = sb("w12", [P, E, W_COLS])
        wv = sb("wv", [P, D])
        wu = sb("wu", [P, D])
        wg1 = sb("wg1", [P, E])
        wo = sb("wo", [P, D])
        mats = sb("mats", [P, NC, 4, P])
        hspec = sb("hspec", [P, NC, 2, D])
        hspec0 = sb("hspec0", [P, 2, 2, D])
        stats = sb("stats", [P, NT, 6])
        mv = sb("mv", [P, NT, 2])
        rstd = sb("rstd", [P, NT])
        veps = sb("veps", [P, NT])
        nbias = veps
        xs = sb("xs", [P, UNROLL, ROWW])
        ys = sb("ys", [P, UNROLL, D])
        xsT = sb("xsT", [P, 2, P])
        hT = sb("hT", [P, 2, 2, P])
        w12r = sb("w12r", [P, W_RING, W_COLS])
        late = sb("late", [P, TILES1 * E])
        ecmp = late[0:1, :].rearrange("p (n e) -> p n e", e=E)
        xsT0 = [hT[:, :, :, :].rearrange("p n f q -> p (n f q)"), late[:, 0:GROUP * P]]
        lg = sb("lg", [P, E, NT])
        rel = sb("rel", [P, E, NT])
        score = sb("score", [P, E, NT])
        expl = sb("expl", [P, E, NT])
        oh1 = sb("oh1", [P, E, NT])
        oh2 = sb("oh2", [P, E, NT])
        ohb = sb("ohb", [P, E, NT], BF16)
        cum = sb("cum", [P, E, NT])
        m1 = sb("m1", [P, NT])
        m2 = sb("m2", [P, NT])
        best = sb("best", [P, NT])
        gate0 = sb("gate0", [P, NT])
        gate1 = sb("gate1", [P, NT])
        gate2 = sb("gate2", [P, NT])
        em2 = sb("em2", [P, NT])
        slot0 = sb("slot0", [P, NT], I32)
        slot1 = sb("slot1", [P, NT], I32)
        slot2 = sb("slot2", [P, NT], I32)
        cnt_i = sb("cnt_i", [P, E], I32)
        cnt_t = sb("cnt_t", [P, E], I32)
        ntile = sb("ntile", [P, E])
        ctile = sb("ctile", [P, E])
        base = sb("base", [P, E])
        ones8 = sb("ones8", [P, E])
        ecnt = sb("ecnt", [1, TILES1])
        expert = sb("expert", [1, TILES1], I32)

        WORK = 17200
        work = sb("work", [P, WORK])
        place = [0]

        def part(n, shape=None, **kw):
            a = work[:, place[0]:place[0] + n]
            place[0] += n
            assert place[0] <= WORK
            return a.rearrange(shape, **kw) if shape else a

        rope = part(2 * L, "p (a m) -> p a m", a=2)
        wqk = part(4 * D, "p (a e) -> p a e", a=4)
        wvg = part(VGW)
        vsb = part(NT * D, "p (i d) -> p i d", d=D)
        negmax = part(NT)
        rsum = part(NT)
        rrec = part(NT)
        y0 = part(J * D, "p (j d) -> p j d", d=D)
        qk = [part(2 * L, "p (a m) -> p a m", a=2) for _ in range(2)]
        rtmp = part(2 * 512, "p (a m) -> p a m", a=2)
        prob = [part(L) for _ in range(2)]
        pT = [part(L, "p (j q) -> p j q", q=P) for _ in range(2)]
        hx, ht, hg, pe_sb = (w12[:, :, :].rearrange("p e h -> p (e h)")[:, n * L:(n + 1) * L] for n in range(4))
        fw_small = w12r[:, :, :].rearrange("p n h -> p (n h)")[:, 0:2 * FO + D + 2]
        filt_v, filt_spec = ys, hspec
        filt_pm = hx.rearrange("p (a j w) -> p a j w", a=2, w=D)
        filt_ej = ht[:, 0:4 * D].rearrange("p (s x w) -> p s x w", s=2, w=D)
        filt_uv = hg[:, 0:4 * D].rearrange("p (s a w) -> p s a w", s=2, w=D)
        f1w, f2w = fw_small[0:FO, 0:FO], fw_small[0:FO, FO:2 * FO]
        f3w = fw_small[0:FO + 1, 2 * FO:2 * FO + D]
        f1b, f2b = fw_small[0:FO, 2 * FO + D:2 * FO + D + 1], fw_small[0:FO, 2 * FO + D + 1:2 * FO + D + 2]
        place[0] = 0
        uu = part(NT * D, "p (i d) -> p i d", d=D)
        vv = [part(J * W, "p (j w) -> p j w", w=W) for _ in range(HALF)]
        spec0 = part(NC * 2 * W)
        spec = [a.rearrange("p (c a w) -> p c a w", a=2, w=W) for a in (spec0, xT[:, :])]
        yT = spec0
        moe_back = [a[:, n * 1024:(n + 1) * 1024].rearrange("p (i k d) -> p i k d", k=2, d=D)
                    for a in (spec0, xT) for n in range(4)]
        pmf = part(8 * W)
        pm = pmf.rearrange("p (a j w) -> p a j w", a=2, w=W)
        prod = [[a.rearrange("p (a w) -> p a w", w=W) for a in pair] for pair in (
            (ys[:, 0:4, :].rearrange("p m d -> p (m d)"), ys[:, 4:8, :].rearrange("p m d -> p (m d)")), xsT0)]
        ej = part(4 * W, "p (s x w) -> p s x w", s=2, w=W)
        uv = part(4 * W, "p (s a w) -> p s a w", s=2, w=W)

        w12r_rows = w12r[:, :, :].rearrange("p n h -> p (n h)")[:, 0:8 * ROWW].rearrange("p (n w) -> p n w", w=ROWW)
        w0_rows = w0[:, :, :].rearrange("p e d -> p (e d)")[:, 0:4 * ROWW].rearrange("p (n w) -> p n w", w=ROWW)
        row_slots = [[xs[:, m, :] for m in range(UNROLL)] + [a[:, m, :] for m in range(RING[l] - UNROLL)]
                     for l, a in enumerate((w12r_rows, w0_rows))]

        S = [ps(f"psS{n}", [P, 2, 512]) for n in range(2)]
        TP = [ps(f"psT{n}", [P, 512]) for n in range(2)]
        O = [ps(f"psO{n}", [P, 512]) for n in range(2)]
        SB = [S[0][:, 0, :], S[0][:, 1, :], S[1][:, 0, :], S[1][:, 1, :]]
        TO = [TP[0][:, :], TP[1][:, :], O[0][:, :], O[1][:, :]]

        def col(name, shape=None, **kw):
            a = cst[:, CONST[name][0]:CONST[name][1]]
            return a.rearrange(shape, **kw) if shape else a

        def ei(a):
            return a[:, :, :].rearrange("p e i -> p i e")

        def flat(a):
            return a[:, :, :].rearrange("p e i -> p (e i)")

        def over_e(a):
            return a[:, :].unsqueeze(1).to_broadcast([P, E, NT])

        ident = col("ident")

        x_loaded = [sem(f"x_loaded{g}") for g in range(B)]
        cst_loaded = sem("cst_loaded")
        w_a_loaded = sem("w_a_loaded")
        filt_loaded = sem("filt_loaded")
        fw_loaded = sem("fw_loaded")
        rope_loaded = sem("rope_loaded")
        moe0_w_loaded = sem("moe0_w_loaded")
        l1_w_loaded = sem("l1_w_loaded")
        b2_loaded = sem("b2_loaded")
        iv_loaded = [sem(f"iv_loaded{c}") for c in range(NC)]
        fill_ready = sem("fill_ready")
        prefilled = sem("prefilled")
        casts_done = sem("casts_done")
        ones_done = sem("ones_done")
        ids_done = sem("ids_done")
        stats_done = sem("stats_done")
        aggr_done = sem("aggr_done")
        veps_done = sem("veps_done")
        rstd_done = sem("rstd_done")
        neg_done = sem("neg_done")
        nbias_done = sem("nbias_done")
        xn_done = sem("xn_done")
        tr_full = sem("tr_full")
        tr_free = sem("tr_free")
        vg_full = sem("vg_full")
        vg_free = sem("vg_free")
        f_full = sem("f_full")
        f_act = sem("f_act")
        f_pool = sem("f_pool")
        filt_v_done = sem("filt_v_done")
        twos_done = sem("twos_done")
        pick_done = sem("pick_done")
        split_done = sem("split_done")
        split_sub = sem("split_sub")
        rad_f = sem("rad_f")
        fs_full = sem("fs_full")
        fs_free = sem("fs_free")
        hspec_done = sem("hspec_done")
        rt = sem("rt")
        rt_exp = sem("rt_exp")
        rt_mm = sem("rt_mm")
        slot0_ready = sem("slot0_ready")
        sent0 = sem("sent0")
        pr_full = sem("pr_full")
        rope_mul = sem("rope_mul")
        rope_done = sem("rope_done")
        s_full = sem("s_full")
        max_done = sem("max_done")
        exp_done = sem("exp_done")
        bias_done = sem("bias_done")
        pt_full = sem("pt_full")
        pt_act = sem("pt_act")
        pt_dve = sem("pt_dve")
        o_full = sem("o_full")
        rrec_done = sem("rrec_done")
        o_done = sem("o_done")
        xs_loaded = [sem(f"xs_loaded{m}") for m in range(RING[0])]
        sent_back = [sem(f"sent_back{m}") for m in range(RING[0])]
        e_t = [sem(f"e_t{l}") for l in range(2)]
        e_xT = [sem(f"e_xT{l}") for l in range(2)]
        e_y = [sem(f"e_y{l}") for l in range(2)]
        e_ys = [sem(f"e_ys{l}") for l in range(2)]
        e_w1 = sem("e_w1")
        e_h = sem("e_h")
        e_ha = sem("e_ha")
        e_hd = sem("e_hd")
        y0_loaded = sem("y0_loaded")
        y0_used = sem("y0_used")
        y0_gated = sem("y0_gated")
        uvg_full = sem("uvg_full")
        uv_taken = sem("uv_taken")
        g_full = sem("g_full")
        lg1_done = sem("lg1_done")
        slot1_ready = sem("slot1_ready")
        expert_ready = sem("expert_ready")
        sent1 = [sem(f"sent1_{n}") for n in range(4)]
        rad = sem("rad")
        x_full = sem("x_full")
        pmul = sem("pmul")
        x_free = sem("x_free")
        y_ready = sem("y_ready")
        b_full = sem("b_full")
        b_free = sem("b_free")
        conv_done = sem("conv_done")
        yt_full = sem("yt_full")
        yt_free = sem("yt_free")
        wo_full = sem("wo_full")
        wo_done = sem("wo_done")
        back_loaded = [sem(f"back_loaded{n}") for n in range(NT // 4)]
        gated2 = sem("gated2")
        out_a = sem("out_a")
        out_ready = sem("out_ready")
        pool_gated = sem("pool_gated")
        pool_added = sem("pool_added")
        out_ready_pool = sem("out_ready_pool")
        stored = sem("stored")

        T_USES, O_USES = [], []
        for n in range(NT):
            T_USES += [("p", n, c) for c in range((n % J + 4) // 4)]
            if n == FILT_RADIX_AT - 1:
                T_USES += [("h", 0), ("h", 1)]
            if n in (FILT_DFT_AT, FILT_DFT_AT + 1):
                T_USES += [("f", 2 * (n - FILT_DFT_AT) + u) for u in range(2)]
            if n:
                O_USES.append(("o", n - 1))
            T_USES += [("x", e) for e in expert0_at(n)]
            O_USES += [("y", e) for e in expert0_at(n - 1)]
            if gates_at(n):
                g = GATES_AT.index(n)
                T_USES += [("t", 2 * g), ("t", 2 * g + 1)]
                O_USES.append(("g", g))
        T_USES += [("t", 2 * B - 2), ("t", 2 * B - 1)]
        O_USES += [("o", NT - 1), ("g", B - 1)]
        T_AT = {use: u for u, use in enumerate(T_USES)}
        O_AT = {use: u for u, use in enumerate(O_USES)}
        SECOND = [n for n in range(NT) if n % J >= 4]

        def t_bank(*use):
            return TP[T_AT[use] % 2]

        def o_bank(*use):
            return O[O_AT[use] % 2]

        def pt_full_at(n, c):
            return sum(use[0] == "p" for use in T_USES[:T_AT[("p", n, c)] + 1])

        def wait_emptied(eng, uses, u):
            if u < 2:
                return
            kind, n, *c = uses[u - 2]
            if kind == "p":
                eng.wait_ge(*((pt_dve, SECOND.index(n) + 1) if c[0] else (pt_act, n + 1)))
            else:
                if kind == "t":
                    n += 2 * B
                if kind == "h":
                    n = 4 * n + 3
                eng.wait_ge({"h": filt_v_done, "x": e_xT[0], "f": fs_free, "t": tr_free, "g": lg1_done,
                             "o": o_done, "y": e_ys[0]}[kind], n + 1)

        C_USES = [("inv", v) for v in range(INV_BEFORE, 2 * NC)]
        for h in range(HALF):
            for q in range(4 * h, 4 * h + 4):
                C_USES += [("yt", q)] + ([("wo", q - 1)] if q > 4 * h else [])
            C_USES.append(("wo", 4 * h + 3))
        C_AT = {use: u for u, use in enumerate(C_USES)}

        def c_bank(*use):
            return SB[2 + C_AT[use] % 2]

        def wait_c_emptied(eng, *use):
            if C_AT[use] >= 2:
                kind, n = C_USES[C_AT[use] - 2]
                eng.wait_ge({"inv": b_free, "yt": yt_free, "wo": wo_done}[kind], n + 1)

        S_USES = [("pr", 0), ("pr", 1), ("s", 0)]
        for n in range(NT):
            for b, h in projections_at(n):
                S_USES += [("pr", 4 * b + 2 * h + u) for u in range(2)]
            if n + 1 < NT:
                S_USES.append(("s", n + 1))
        LAST_S, seen = {}, {}
        for use in S_USES:
            slot = use[1] % 2 if use[0] == "s" else (use[1] + 1) % 2
            LAST_S[use] = seen.get(slot)
            seen[slot] = use

        def wait_sent_back(eng, l, n):
            eng.wait_ge(sent_back[n % RING[l]], turn(l, n))

        def wait_hidden(eng, n):
            eng.wait_ge(e_hd if n % 2 else e_ha, n // 2 + 1)

        def radix_forward(eng, steps, count, v, a, pm_, ej_, uv_):
            tt, stt = eng.tensor_tensor, eng.scalar_tensor_tensor

            def did(ins):
                ins.then_inc(steps, 1)
                count[0] += 1
                return count[0]

            def after(step):
                eng.wait_ge(steps, step)

            p_, m_ = pm_[:, 0], pm_[:, 1]
            if count[0]:
                after(count[0])
            s1 = did(tt(p_, v[:, 0:4], v[:, 4:8], ALU.add))
            yield
            s2 = did(tt(m_, v[:, 0:4], v[:, 4:8], ALU.subtract))
            yield
            after(s1)
            did(tt(a[:, 1], p_[:, 0:2], p_[:, 2:4], ALU.subtract))
            yield
            s4 = did(tt(uv_[:, 0], p_[:, 0:2], p_[:, 2:4], ALU.add))
            yield
            after(s2)
            did(tt(uv_[:, 1, 0], m_[:, 1], m_[:, 3], ALU.subtract))
            yield
            s8 = did(tt(uv_[:, 1, 1], m_[:, 1], m_[:, 3], ALU.add))
            yield
            after(s4)
            did(tt(a[:, 0, 0], uv_[:, 0, 0], uv_[:, 0, 1], ALU.add))
            yield
            did(tt(a[:, 0, 1], uv_[:, 0, 0], uv_[:, 0, 1], ALU.subtract))
            yield
            s11 = did(stt(ej_[:, 0], m_[:, 2:4], RC, v[:, 0:2], ALU.mult, ALU.add))
            yield
            s12 = did(stt(ej_[:, 1], p_[:, 2:4], RC, v[:, 4:6], ALU.mult, ALU.add))
            yield
            after(s8)
            did(stt(a[:, 2], uv_[:, 1], RC, m_[:, 0:3:2], ALU.mult, ALU.add))
            yield
            s10 = did(stt(a[:, 3], uv_[:, 1], -RC, m_[:, 0:3:2], ALU.mult, ALU.add))
            yield
            after(s12)
            did(stt(v[:, 0:2], m_[:, 2:4], -RC, v[:, 0:2], ALU.mult, ALU.add))
            yield
            s14 = did(stt(v[:, 4:6], p_[:, 2:4], -RC, v[:, 4:6], ALU.mult, ALU.add))
            yield
            after(s10)
            did(stt(uv_[:, 0, 0], ej_[:, 1, 1], -TAU, ej_[:, 0, 1], ALU.mult, ALU.add))
            yield
            s16 = did(stt(uv_[:, 0, 1], ej_[:, 0, 1], TAU, ej_[:, 1, 1], ALU.mult, ALU.add))
            yield
            after(s14)
            did(stt(uv_[:, 1, 0], v[:, 1], -TAU, v[:, 5], ALU.mult, ALU.subtract))
            yield
            s18 = did(stt(uv_[:, 1, 1], v[:, 5], -TAU, v[:, 1], ALU.mult, ALU.add))
            yield
            after(s16)
            did(stt(a[:, 4], uv_[:, 0], TC, ej_[:, :, 0], ALU.mult, ALU.add))
            yield
            did(stt(a[:, 5], uv_[:, 0], -TC, ej_[:, :, 0], ALU.mult, ALU.add))
            yield
            after(s18)
            did(stt(a[:, 6], uv_[:, 1], TC, v[:, 0:5:4], ALU.mult, ALU.add))
            yield
            did(stt(a[:, 7], uv_[:, 1], -TC, v[:, 0:5:4], ALU.mult, ALU.add))
            yield

        block = ctx.enter_context(nc.Block())

        @block.sync
        def _(sp):
            xv = x_in.rearrange("b (j p) d -> b p j d", p=P)
            for g in range(B):
                sp.dma_start(xres[:, J * g:J * (g + 1), :], xv[g]).then_inc(x_loaded[g], 16)
                if g == 0:
                    sp.dma_start(cst[:, :], cst_in).then_inc(cst_loaded, 16)
                    sp.dma_start(wvg, wvg_in).then_inc(w_a_loaded, 16)
            sp.dma_start(mats[:, :, :, :], fw_in).then_inc(fw_loaded, 16)
            sp.dma_start(wqk, wqk_in).then_inc(rope_loaded, 16)
            sp.dma_start(rope, rope_in).then_inc(rope_loaded, 16)
            sp.dma_start(w0[:, :, :], w0_in).then_inc(moe0_w_loaded, 16)
            sp.dma_start(y0.rearrange("p j d -> p (j d)"), b0_in.rearrange("e d -> (e d)").partition_broadcast(P)).then_inc(moe0_w_loaded, 16)
            sp.dma_start(b2[:, :, :].rearrange("p e d -> p (e d)"), b2_in.rearrange("e d -> (e d)").partition_broadcast(P)).then_inc(b2_loaded, 16)
            sp.dma_start(bias[:, :], bvuo_in.partition_broadcast(P)).then_inc(b2_loaded, 16)
            sp.wait_ge(fill_ready, 2)
            for dst, n in ((slots0, TILES0), (slots1, TILES1)):
                for i in range(0, n, 8):
                    sp.dma_start(dst[i * P:(i + 8) * P, :].rearrange("(i p) w -> p i w", p=P),
                                 xs[:, :, :]).then_inc(prefilled, 16)
            for i in range(0, NT, 8):
                sp.dma_start(moe0[i * P:(i + 8) * P, :].rearrange("(i p) w -> p i w", p=P),
                             xs[:, :, 0:D]).then_inc(prefilled, 16)

            def expert_rows(l, src, n_tiles):
                for m, slot in enumerate(row_slots[l]):
                    sp.dma_start(slot, src[m * P:(m + 1) * P, :]).then_inc(xs_loaded[m], 16)
                with sp.Fori(1, n_tiles // RING[l]) as it:
                    for m, slot in enumerate(row_slots[l]):
                        sp.wait_ge(sent_back[m], it * 16 + l * LAYER_TURNS)
                        n = it * RING[l] + m
                        sp.dma_start(slot, src[bass.ds(n * P, P), :]).then_inc(xs_loaded[m], 16)

            sp.wait_ge(rad_f, RAD_F)
            for a, b in ((w12[:, :, 0:H1], w1_in.rearrange("e d h -> d e h")), (w12[:, :, H1:H1 + 2], b1_in),
                         (w12[:, :, H1 + 2:W_COLS].rearrange("p e (f o) -> p e f o", f=2), w2_in.rearrange("e (f p) o -> p e f o", p=P)),
                         (wv[:, :], wv_in), (wu[:, :], wu_in), (wg1[:, :], wg1_in), (wo[:, :], wo_in)):
                for e in (range(E) if b.ndim == 4 else [None]):
                    sp.dma_start(a if e is None else a[:, e], b if e is None else b[:, e]).then_inc(l1_w_loaded, 16)

            sp.wait_ge(prefilled, 16 * N_FILL)
            sp.wait_ge(sent0, 16 * NT)
            expert_rows(0, slots0, TILES0)
            for m in range(RING[0]):
                sp.wait_ge(sent_back[m], LAYER_TURNS)
            for g in range(B):
                if g:
                    sp.wait_ge(y0_used, J * g)
                sp.dma_start(y0, moe0[g * L:(g + 1) * L, :].rearrange("(j p) d -> p j d", p=P)).then_inc(y0_loaded, 16)
            for c in range(NC):
                sp.wait_ge(x_full, NC + c + 1)
                sp.dma_start(mats[:, c, :, :], iv_in[:, c * 4 * P:(c + 1) * 4 * P]).then_inc(iv_loaded[c], 16)
            for s in sent1:
                sp.wait_ge(s, 16 * NT // 2)
            expert_rows(1, slots1, TILES1)
            for m in range(RING[1]):
                sp.wait_ge(sent_back[m], LAYER_TURNS + 16 * (TILES1 // RING[1]))
            sp.wait_ge(wo_done, NT // 4)
            for q in range(NT // 4):
                sp.dma_start(moe_back[q], moe1[q * 1024:(q + 1) * 1024, :].rearrange(
                    "(i p k) d -> p i k d", p=P, k=2)).then_inc(back_loaded[q], 16)
            ov = out.rearrange("b (j p) d -> p (b j) d", p=P)
            for q in range(NT // 4):
                if q in POOL_SUMS:
                    sp.wait_ge(out_ready_pool, POOL_SUMS.index(q) + 1)
                else:
                    sp.wait_ge(out_ready, q - sum(r < q for r in POOL_SUMS) + 1)
                sp.dma_start(ov[:, 4 * q:4 * q + 4, :], xres[:, 4 * q:4 * q + 4, :]).then_inc(stored, 16)
            sp.wait_ge(stored, 16 * (NT // 4))

        @block.gpsimd
        def _(pool):
            pool.memset(xs[:, :, 0:D], 0.0).then_inc(fill_ready, 1)
            pool.memset(xs[:, :, D:ROWW].bitcast(I32), 1 << 24).then_inc(fill_ready, 1)
            pool.memset(onesb[:, :], 1.0).then_inc(ones_done, 1)
            pool.memset(ones8[:, :], 1.0).then_inc(ones_done, 1)
            pool.wait_ge(cst_loaded, 16)
            ids = row[:, :, D:ROWW].rearrange("p i w -> p (i w)").bitcast(I32)
            pool.tensor_copy(ids, col("token").bitcast(I32)).then_inc(ids_done, 1)

            def inverse_std(k, a=0, n=J):
                g = slice(J * (k % B) + a, J * (k % B) + a + n)
                pool.wait_ge(aggr_done, J * k + a + n)
                pool.tensor_scalar(veps[:, g], mv[:, g, 1], 1e-5, None, ALU.add).then_inc(veps_done, n)
                pool.wait_ge(veps_done, J * k + a + n)
                pool.tensor_tensor(rstd[:, g], veps[:, g], col("minus_half")[:, 0:n], ALU.pow).then_inc(rstd_done, n)

            def scatter_rows(dst, slots, bound, done, tiles=range(NT)):
                for i in tiles:
                    pool.indirect_dma_start(dst[:, :], bass.IndirectOffsetOnAxis(ap=slots[:, i:i + 1], axis=0),
                                            row[:, i, :], None, bounds_check=bound,
                                            oob_is_err=False).then_inc(done, 16)

            def send_back(l, n, dst, bound):
                m = n % RING[l]
                pool.wait_ge(e_ys[l], n + 1 if l else n // GROUP + 1)
                pool.wait_ge(xs_loaded[m], turn(l, n))
                pool.indirect_dma_start(
                    dst[:, :], bass.IndirectOffsetOnAxis(ap=row_slots[l][m][:, D:ROWW].bitcast(I32), axis=0),
                    ys[:, n % UNROLL, :], None, bounds_check=bound, oob_is_err=False).then_inc(sent_back[m], 16)

            n_pool = [0]

            def times_x_plus_x(t):
                for op in (ALU.mult, ALU.add):
                    pool.tensor_tensor(t[0:FO, :], t[0:FO, :], hx[0:FO, :], op).then_inc(f_pool, 1)
                    n_pool[0] += 1
                    if op == ALU.mult:
                        pool.wait_ge(f_pool, n_pool[0])

            def filter_cubic(k):
                pool.wait_ge(f_act, 3 * k + 2)
                times_x_plus_x(ht)

            def filter_gelu(k):
                pool.wait_ge(f_act, 3 * k + 3)
                times_x_plus_x(hg)

            inverse_std(0)
            inverse_std(1)
            filter_cubic(0)
            inverse_std(2)
            inverse_std(3)
            filter_gelu(0)
            filter_cubic(1)
            filter_gelu(1)
            pool.wait_ge(xn_done, NT)
            pool.wait_ge(ids_done, 1)
            pool.wait_ge(prefilled, 16 * N_FILL)
            pool.wait_ge(slot0_ready, 1)
            scatter_rows(slots0, slot0, SLOTS0 - 1, sent0)
            for k in range(TILES0):
                send_back(0, k, moe0, T - 1)

            pool.wait_ge(sent0, 16 * NT)
            for g in range(B - 1):
                tiles = slice(J * g, J * g + J)
                pool.wait_ge(y0_loaded, 16 * (g + 1))
                for j in range(J):
                    i = J * g + j
                    pool.tensor_scalar(y0[:, j, :], y0[:, j, :], gate0[:, i:i + 1], None, ALU.mult).then_inc(y0_gated, 1)
                pool.wait_ge(y0_gated, J * (g + 1))
                pool.wait_ge(o_done, J * (g + 1))
                pool.tensor_tensor(xres[:, tiles, :], xres[:, tiles, :], y0, ALU.add).then_inc(y0_used, J)
                inverse_std(B + g)
                pool.wait_ge(rstd_done, J * (B + g + 1))
                pool.tensor_tensor(nbias[:, tiles], mv[:, tiles, 0], rstd[:, tiles], ALU.mult).then_inc(neg_done, 1)
                pool.wait_ge(neg_done, g + 1)
                pool.tensor_scalar(nbias[:, tiles], nbias[:, tiles], -1.0, None, ALU.mult).then_inc(nbias_done, 1)
            for a in (0, J // 2):
                inverse_std(2 * B - 1, a, J // 2)
            pool.tensor_copy(ids, col("token2").bitcast(I32)).then_inc(ids_done, 1)
            pool.wait_ge(ids_done, 2)
            pool.wait_ge(xn_done, 2 * NT)
            pool.wait_ge(slot1_ready, 1)
            for h in range(2):
                scatter_rows(slots1, slot1, SLOTS1 - 1, sent1[h], range(h * NT // 2, (h + 1) * NT // 2))
            for h in range(2):
                pool.wait_ge(slot1_ready, 2)
                pool.wait_ge(sent1[h], 16 * NT // 2)
                pool.tensor_copy(ids[:, h * NT // 2:(h + 1) * NT // 2],
                                 col("token2b").bitcast(I32)[:, h * NT // 2:(h + 1) * NT // 2]).then_inc(ids_done, 1)
                pool.wait_ge(ids_done, 3 + h)
                scatter_rows(slots1, slot2, SLOTS1 - 1, sent1[2 + h], range(h * NT // 2, (h + 1) * NT // 2))
            for n in range(TILES1):
                send_back(1, n, moe1, 2 * T - 1)
            for r, q in enumerate(POOL_SUMS):
                x_, y_ = xres[:, 4 * q:4 * q + 4, :], moe_back[q]
                pool.wait_ge(back_loaded[q], 16)
                for t in range(4):
                    pool.tensor_scalar(y_[:, t, 0, :], y_[:, t, 0, :], gate1[:, 4 * q + t:4 * q + t + 1], None,
                                       ALU.mult).then_inc(pool_gated, 1)
                pool.wait_ge(pool_gated, 4 * (r + 1))
                pool.tensor_tensor(x_, x_, y_[:, :, 0, :], ALU.add).then_inc(pool_added, 1)
                pool.wait_ge(pool_added, r + 1)
                pool.wait_ge(gated2, q + 1)
                pool.tensor_tensor(x_, x_, y_[:, :, 1, :], ALU.add).then_inc(out_ready_pool, 1)

        @block.scalar
        def _(act):
            act.dma_start(fw_small[0:FO + 1, :], fsmall_in).then_inc(filt_loaded, 16)
            act.dma_start(pe_sb[0:FO, :], pe_in).then_inc(filt_loaded, 16)
            act.wait_ge(cst_loaded, 16)
            for o, name in ((identb, "ident"), (beforeb, "before"), (maskb, "mask")):
                act.activation(o[:, :], col(name), ACT.Copy).then_inc(casts_done, 1)

            def take_transposes(k0):
                for u in range(2):
                    act.wait_ge(tr_full, k0 + u + 1)
                    act.activation(xT[:, 512 * ((k0 + u) % 8):512 * ((k0 + u) % 8) + 512], TP[u][:, :],
                                   ACT.Copy).then_inc(tr_free, 1)

            def take_values(g):
                take_transposes(2 * g)
                for u in range(4):
                    n = 4 * g + u
                    i = 2 * n
                    act.wait_ge(vg_full, n + 1)
                    pv = O[n % 2][:, 0:2 * VGW].rearrange("p (i w) -> p i w", w=VGW)
                    act.activation(vsb[:, i:i + 2, :], pv[:, :, 0:D], ACT.Copy)
                    act.activation(lg[:, :, i:i + 2].rearrange("p e i -> p i e"), pv[:, :, D:VGW],
                                   ACT.Copy).then_inc(vg_free, 1)

            def filter_layer(k):
                act.wait_ge(f_full, k + 1)
                act.activation(hx[0:FO, :], S[k][0:FO, :, :].rearrange("p a m -> p (a m)"), ACT.Identity,
                               bias=(f1b, f2b)[k], scale=(1.0, 0.5)[k]).then_inc(f_act, 1)
                act.wait_ge(f_act, 3 * k + 1)
                act.activation(ht[0:FO, :], hx[0:FO, :], ACT.Square, scale=float(np.sqrt(0.044715))).then_inc(f_act, 1)

            def filter_tanh(k):
                act.wait_ge(f_pool, 4 * k + 2)
                act.activation(hg[0:FO, :], ht[0:FO, :], ACT.Tanh, scale=float(np.sqrt(2 / np.pi))).then_inc(f_act, 1)

            act.wait_ge(filt_loaded, 32)
            filter_layer(0)
            filter_tanh(0)
            for g in range(B):
                take_values(g)
            filter_layer(1)
            act.wait_ge(rt, R0_REL)
            act.activation(flat(expl), flat(rel), ACT.Exp).then_inc(rt_exp, 1)
            filter_tanh(1)

            def filter_values():
                act.wait_ge(f_full, 3)
                for j in range(J):
                    act.activation(filt_v[:, j, :], t_bank("h", j // 4)[:, (j % 4) * D:(j % 4) * D + D], ACT.Copy,
                                   scale=col("decay")[:, j:j + 1]).then_inc(filt_v_done, 1)

            def filter_spectrum(u):
                act.wait_ge(fs_full, u + 1)
                act.activation(hspec[:, 2 * u:2 * u + 2, :, :].rearrange("p c a d -> p (c a d)"),
                               t_bank("f", u)[:, :], ACT.Copy).then_inc(fs_free, 1)

            def filter_class0():
                act.wait_ge(fs_free, 4)
                for a in range(2):
                    act.activation(hspec0[:, a, :, :], hspec[:, 0, a, :].unsqueeze(1).to_broadcast([P, 2, D]),
                                   ACT.Copy).then_inc(hspec_done, 1)
                act.wait_ge(hspec_done, 2)
                act.activation(hspec0[0:1, 1, :, :], hspec0[0:1, 1, :, :], ACT.Copy, scale=0.0).then_inc(hspec_done, 1)
                act.activation(hspec0[0:1, 0, 1, :], hspec[0:1, 0, 1, :], ACT.Copy).then_inc(hspec_done, 1)

            def split_bias(k):
                act.wait_ge(b2_loaded, 32)
                if k:
                    act.wait_ge(split_sub, k)
                act.activation(biasb[PARTS[k], :], bias[PARTS[k], :], ACT.Copy).then_inc(split_done, 1)

            def exp_rows(n):
                i = n % J
                act.wait_ge(bias_done, n + 1)
                if n >= 2:
                    act.wait_ge(pt_full, pt_full_at(n - 2, (i - 2) % J // 4))
                act.activation(prob[n % 2][:, 0:(i + 1) * P],
                               S[n % 2][:, :, :].rearrange("p a m -> p (a m)")[:, 0:(i + 1) * P], ACT.Exp,
                               bias=negmax[:, n:n + 1], scale=SCALE,
                               accum_out=rsum[:, n:n + 1]).then_inc(exp_done, 1)

            def take_pt(n):
                act.wait_ge(pt_full, pt_full_at(n, 0))
                if n >= 2:
                    act.wait_ge(o_full, n - 1)
                k = min(4, n % J + 1)
                act.activation(pT[n % 2][:, 0:k, :].rearrange("p j q -> p (j q)"), t_bank("p", n, 0)[:, 0:k * P],
                               ACT.Copy).then_inc(pt_act, 1)

            def norm_rows(g, third):
                act.wait_ge(nbias_done, g + 1)
                for i in range(J * g + 3 * third, J * g + min(3 * third + 3, J)):
                    act.activation(row[:, i, 0:D], xres[:, i, :], ACT.Identity, bias=nbias[:, i:i + 1],
                                   scale=rstd[:, i:i + 1]).then_inc(xn_done, 1)

            def take_gates(g):
                for u in (2 * g, 2 * g + 1):
                    act.wait_ge(tr_full, 2 * B + u + 1)
                    act.activation(xT[:, 512 * u:512 * u + 512], t_bank("t", u)[:, :], ACT.Copy).then_inc(tr_free, 1)
                act.wait_ge(g_full, g + 1)
                act.activation(lg[:, :, J * g:J * g + J].rearrange("p e i -> p i e"),
                               o_bank("g", g)[:, 0:J * E].rearrange("p (i e) -> p i e", e=E), ACT.Copy).then_inc(lg1_done, 1)

            exp_rows(0)
            for n in range(NT):
                take_pt(n)
                if n + 1 < NT:
                    exp_rows(n + 1)
                if n == FILT_RADIX_AT - 1:
                    filter_values()
                if n in (FILT_DFT_AT, FILT_DFT_AT + 1):
                    for u in range(2):
                        filter_spectrum(2 * (n - FILT_DFT_AT) + u)
                if n == FILT_DFT_AT + 2:
                    filter_class0()
                if 0 <= n - SPLIT_AT < 2 * len(PARTS) and (n - SPLIT_AT) % 2 == 0:
                    split_bias((n - SPLIT_AT) // 2)
                if ROWS_AT <= n < ROWS_AT + 3 * (B - 1):
                    norm_rows(*divmod(n - ROWS_AT, 3))
                if gates_at(n):
                    take_gates(GATES_AT.index(n))
                for e in expert0_at(n):
                    act.wait_ge(e_t[0], e + 1)
                    if e >= 2:
                        act.wait_ge(e_y[0], e - 1)
                    act.activation(xsT0[e % 2], t_bank("x", e)[:, :], ACT.Copy).then_inc(e_xT[0], 1)

            def take_projection(u):
                act.wait_ge(uvg_full, u + 1)
                q = u % 8
                b, j = divmod(4 * q, J)
                o = vv[b // 2][:, j:j + 4, (b % 2) * D:(b % 2 + 1) * D] if u < 8 else uu[:, 4 * q:4 * q + 4, :]
                act.activation(o, SB[u % 4].rearrange("p (t d) -> p t d", d=D), ACT.Copy).then_inc(uv_taken, 1)

            take_projection(0)
            take_projection(1)
            take_gates(B - 1)
            take_projection(2)
            act.wait_ge(rt, R1_REL)
            act.activation(flat(expl), flat(rel), ACT.Exp).then_inc(rt_exp, 1)
            take_projection(3)
            act.wait_ge(rt, R1_M2)
            act.activation(em2[:, :], m2[:, :], ACT.Exp).then_inc(rt_exp, 1)
            for u in range(4, 16):
                take_projection(u)

            def take_inverse(v):
                act.wait_ge(b_full, v + 1)
                act.activation(spec[v // NC][:, v % NC, :, :].rearrange("p a w -> p (a w)"),
                               TO[v % 4] if v < INV_BEFORE else c_bank("inv", v), ACT.Copy).then_inc(b_free, 1)

            def take_y(q):
                act.wait_ge(yt_full, q + 1)
                act.activation(yT[:, 512 * q:512 * q + 512], c_bank("yt", q), ACT.Copy).then_inc(yt_free, 1)

            for v in range(INV_BEFORE):
                take_inverse(v)

            def copy_weights(n):
                e = act.value_load(expert[0:1, n:n + 1], min_val=0, max_val=E - 1)
                if n >= W_RING:
                    act.wait_ge(e_y[1], n - W_RING + 1)
                act.activation(w12r[:, n % W_RING, :], w12[:, bass.ds(e, 1), :].rearrange("p e h -> p (e h)"),
                               ACT.Copy).then_inc(e_w1, 1)

            def take_rows(n):
                act.wait_ge(e_t[1], n + 1)
                if n >= 2:
                    act.wait_ge(e_h, n - 1)
                act.activation(xsT[:, n % 2, :], TP[n % 2][:, 0:P], ACT.Copy).then_inc(e_xT[1], 1)

            def hidden(n):
                act.wait_ge(e_h, n + 1)
                if n >= 2:
                    act.wait_ge(e_y[1], n - 1)
                for f in range(2):
                    last = act.activation(hT[:, n % 2, f, :], S[0][:, n % 2, f * P:(f + 1) * P], ACT.Relu,
                                          bias=w12r[:, n % W_RING, H1 + f:H1 + f + 1])
                last.then_inc(e_ha, 1)

            act.wait_ge(expert_ready, 1)
            act.wait_ge(y_ready, 2 * NC)
            for n in range(-2, TILES1):
                if n + 2 < TILES1:
                    copy_weights(n + 2)
                    take_rows(n + 2)
                if 0 <= n + 1 < TILES1 and n % 2:
                    hidden(n + 1)
                for kind, k in conv_pe_at(n):
                    if kind == "inv":
                        take_inverse(k)
                    if kind == "yt":
                        take_y(k)
            for q in range(NT // 4):
                act.wait_ge(back_loaded[q], 16)
                for t in range(4):
                    i = 4 * q + t
                    last = act.activation(moe_back[q][:, t, 1, :], moe_back[q][:, t, 1, :], ACT.Copy,
                                          scale=gate2[:, i:i + 1])
                last.then_inc(gated2, 1)

        @block.tensor
        def _(pe):
            def mm(o, lhsT, rhs, start=True, stop=True):
                return pe.matmul(o, lhsT, rhs, start=start, stop=stop)

            def transpose_tokens(k):
                for u in range(2):
                    n = 2 * k + u
                    if n >= 2:
                        pe.wait_ge(tr_free, n - 1)
                    for q in range(4):
                        i = 4 * n + q
                        pe.wait_ge(xn_done, i + 1)
                        last = pe.transpose(TP[u][:, q * P:(q + 1) * P], row[:, i, 0:D], ident)
                    last.then_inc(tr_full, 1)

            def values_and_gates(g):
                for u in range(4):
                    n = 4 * g + u
                    pe.wait_ge(tr_free, 2 * g + u // 2 + 1)
                    if n >= 2:
                        pe.wait_ge(vg_free, n - 1)
                    for q in range(2):
                        i = 2 * n + q
                        last = mm(O[n % 2][:, q * VGW:(q + 1) * VGW], xT[:, i * P:(i + 1) * P], wvg)
                    last.then_inc(vg_full, 1)

            def routing_counts(k):
                pe.wait_ge(rt, (R0_OH, R1_OH)[k])
                if k:
                    pe.wait_ge(lg1_done, B)
                    pe.wait_ge(o_done, NT)
                oh = ohb[:, :, :].rearrange("p e i -> p (e i)")
                mm(O[0][:, 0:E * NT], beforeb[:, :], oh)
                mm(O[0][:, E * NT:2 * E * NT], onesb[:, :], oh).then_inc(rt_mm, 1)

            def filter_layer(k):
                if k:
                    pe.wait_ge(f_pool, 4 * k)
                if k < 2:
                    for h in range(2):
                        r = (pe_sb[0:FO, :], hg[0:FO, :])[k][:, 512 * h:512 * h + 512]
                        last = mm(S[k][0:FO, h, :], (f1w, f2w)[k], r)
                else:
                    pe.wait_ge(twos_done, 1)
                    for j in range(J):
                        if j % 4 == 0:
                            wait_emptied(pe, T_USES, T_AT[("h", j // 4)])
                        last = mm(t_bank("h", j // 4)[:, (j % 4) * P:(j % 4) * P + P], hg[0:FO + 1, j * P:(j + 1) * P], f3w)
                last.then_inc(f_full, 1)

            def dft(o, a, c, s):
                for n in range(2):
                    mm(o[n], mats[:, c, 2 * n, :], a[:, 0, :], stop=False)
                    last = mm(o[n], mats[:, c, 2 * n + 1, :], a[:, 1, :], start=False)
                last.then_inc(s, 1) if s else None

            def filter_spectrum(u):
                pe.wait_ge(fw_loaded, 16)
                pe.wait_ge(rad_f, RAD_F)
                wait_emptied(pe, T_USES, T_AT[("f", u)])
                for c in (2 * u, 2 * u + 1):
                    o = t_bank("f", u)[:, 256 * (c % 2):256 * (c % 2) + 256].rearrange("p (a w) -> p a w", a=2)
                    dft([o[:, 0, :], o[:, 1, :]], filt_spec[:, c, :, :], c, fs_full if c % 2 else None)

            def project(b, h):
                for u in (2 * h, 2 * h + 1):
                    n = 4 * b + u
                    slot = S[(n + 1) % 2]
                    wait_scores_bank(("pr", n))
                    for a in range(2):
                        last = mm(slot[:, a, :], wqk[:, 2 * (u % 2) + a, :],
                                  xT[:, b * L + 512 * (u // 2):b * L + 512 * (u // 2) + 512])
                    last.then_inc(pr_full, 1)

            def scores(n):
                b, i = n // J, n % J
                wait_scores_bank(("s", n))
                pe.wait_ge(rope_done, 4 * b + (2 if i < 4 else 4))
                q = qk[b % 2][:, 0, i * P:(i + 1) * P]
                for c in range((i + 4) // 4):
                    w = min(512, (i + 1) * P - 512 * c)
                    diagonal = c == i // 4
                    last = mm(S[n % 2][:, c, 0:w], q, qk[b % 2][:, 1, 512 * c:512 * c + w], stop=not diagonal)
                    if diagonal:
                        last = mm(S[n % 2][:, c, w - P:w], identb[:, :], maskb[:, :], start=False)
                last.then_inc(s_full, 1)

            def wait_scores_bank(use):
                before = LAST_S[use]
                if before is not None:
                    kind, n = before
                    pe.wait_ge(*((rope_mul, 2 * n + 2) if kind == "pr" else (exp_done, n + 1)))

            def transpose_probs(n):
                i = n % J
                pe.wait_ge(exp_done, n + 1)
                for c in range((i + 4) // 4):
                    wait_emptied(pe, T_USES, T_AT[("p", n, c)])
                    for j in range(4 * c, min(4 * c + 4, i + 1)):
                        last = pe.transpose(t_bank("p", n, c)[:, (j - 4 * c) * P:(j - 4 * c + 1) * P],
                                            prob[n % 2][:, j * P:(j + 1) * P], ident)
                    last.then_inc(pt_full, 1)

            def weigh_values(n):
                b, i = n // J, n % J
                wait_emptied(pe, O_USES, O_AT[("o", n)])
                pe.wait_ge(pt_act, n + 1)
                for j in range(i + 1):
                    if j == 4:
                        pe.wait_ge(pt_dve, SECOND.index(n) + 1)
                    last = mm(o_bank("o", n)[:, 0:D], pT[n % 2][:, j, :], vsb[:, b * J + j, :], start=j == 0, stop=j == i)
                last.then_inc(o_full, 1)

            def gates(g):
                for u in (2 * g, 2 * g + 1):
                    wait_emptied(pe, T_USES, T_AT[("t", u)])
                    for q in range(4):
                        pe.wait_ge(xn_done, NT + 4 * u + q + 1)
                        last = pe.transpose(t_bank("t", u)[:, q * P:(q + 1) * P], row[:, 4 * u + q, 0:D], ident)
                    last.then_inc(tr_full, 1)
                pe.wait_ge(l1_w_loaded, 16 * N_L1W)
                wait_emptied(pe, O_USES, O_AT[("g", g)])
                for i in range(J * g, J * g + J):
                    pe.wait_ge(tr_free, 2 * B + i // 4 + 1)
                    last = mm(o_bank("g", g)[:, (i % J) * E:(i % J) * E + E], xT[:, i * P:(i + 1) * P], wg1[:, :])
                last.then_inc(g_full, 1)

            def expert0_rows(e):
                wait_emptied(pe, T_USES, T_AT[("x", e)])
                for t in range(GROUP):
                    k = GROUP * e + t
                    pe.wait_ge(xs_loaded[k % RING[0]], turn(0, k))
                    last = pe.transpose(t_bank("x", e)[:, t * P:(t + 1) * P], row_slots[0][k % RING[0]][:, 0:D], ident)
                last.then_inc(e_t[0], 1)

            def expert0_out(e):
                pe.wait_ge(moe0_w_loaded, 32)
                pe.wait_ge(e_xT[0], e + 1)
                wait_emptied(pe, O_USES, O_AT[("y", e)])
                for t in range(GROUP):
                    last = mm(o_bank("y", e)[:, t * D:(t + 1) * D], xsT0[e % 2][:, t * P:(t + 1) * P], w0[:, e, :])
                last.then_inc(e_y[0], 1)

            pe.wait_ge(filt_loaded, 32)
            filter_layer(0)
            pe.wait_ge(cst_loaded, 16)
            pe.wait_ge(w_a_loaded, 16)
            for g in range(B):
                transpose_tokens(g)
                values_and_gates(g)
            pe.wait_ge(casts_done, 3)
            pe.wait_ge(ones_done, 2)
            filter_layer(1)
            pe.wait_ge(vg_free, 16)
            routing_counts(0)
            pe.wait_ge(rope_loaded, 32)
            pe.wait_ge(f_act, 4)
            project(0, 0)
            pe.wait_ge(rt, R0_CUM)
            scores(0)
            for n in range(NT):
                for b, h in projections_at(n):
                    project(b, h)
                if n + 1 < NT:
                    scores(n + 1)
                transpose_probs(n)
                if n == FILT_RADIX_AT - 1:
                    filter_layer(2)
                if n in (FILT_DFT_AT, FILT_DFT_AT + 1):
                    for u in range(2):
                        filter_spectrum(2 * (n - FILT_DFT_AT) + u)
                if n:
                    weigh_values(n - 1)
                for e in expert0_at(n):
                    expert0_rows(e)
                for e in expert0_at(n - 1):
                    expert0_out(e)
                if gates_at(n):
                    gates(GATES_AT.index(n))
            weigh_values(NT - 1)

            def project_vu(u):
                if u >= 4:
                    pe.wait_ge(uv_taken, u - 3)
                o = SB[u % 4]
                for t in range(4):
                    i = 4 * (u % 8) + t
                    mm(o[:, t * D:(t + 1) * D], pickb[0:96, :], biasb[0:96, (BV_AT, BU_AT)[u // 8]:(BV_AT, BU_AT)[u // 8] + D],
                       stop=False)
                    last = mm(o[:, t * D:(t + 1) * D], xT[:, i * P:(i + 1) * P], (wv, wu)[u // 8][:, :], start=False)
                last.then_inc(uvg_full, 1)

            pe.wait_ge(exp_done, NT)
            pe.wait_ge(split_done, len(PARTS))
            pe.wait_ge(pick_done, 4)
            for u in range(4):
                project_vu(u)
            gates(B - 1)
            routing_counts(1)
            for u in range(4, 16):
                project_vu(u)
            pe.wait_ge(uv_taken, 16)

            def forward(u):
                if u % NC == 0:
                    pe.wait_ge(rad, RAD_F * (u // NC + 1))
                if u >= 4:
                    pe.wait_ge(x_free, u - 3)
                dft([SB[u % 4][:, 0:W], SB[u % 4][:, W:2 * W]], spec[u // NC][:, u % NC, :, :], u % NC, x_full)

            def inverse(v):
                hf, c = divmod(v, NC)
                pe.wait_ge(y_ready, v + 1)
                pe.wait_ge(iv_loaded[c], 16)
                if v >= INV_BEFORE:
                    wait_c_emptied(pe, "inv", v)
                elif v >= 4:
                    pe.wait_ge(b_free, v - 3)
                o = TO[v % 4] if v < INV_BEFORE else c_bank("inv", v)
                dft([o[:, 0:W], o[:, W:2 * W]], spec[hf][:, c, :, :], c, b_full)

            LAG = 3
            for c in range(NC):
                forward(c)
            pe.wait_ge(rt, R1_CUM)
            for v in range(INV_BEFORE + LAG):
                if v < NC:
                    forward(NC + v)
                if v >= LAG:
                    inverse(v - LAG)
            pe.wait_ge(x_free, 2 * NC)
            pe.wait_ge(b_free, INV_BEFORE)

            def transpose_y(q):
                if q % 4 == 0:
                    pe.wait_ge(conv_done, 2 * (q // 4) + 2)
                wait_c_emptied(pe, "yt", q)
                for t in range(4):
                    b, j = divmod(4 * q + t, J)
                    last = pe.transpose(c_bank("yt", q)[:, t * P:(t + 1) * P],
                                        vv[b // 2][:, j, (b % 2) * D:(b % 2 + 1) * D], ident)
                last.then_inc(yt_full, 1)

            def project_y(q):
                pe.wait_ge(yt_free, q + 1)
                wait_c_emptied(pe, "wo", q)
                for t in range(4):
                    i = 4 * q + t
                    o = c_bank("wo", q)[:, t * D:(t + 1) * D]
                    mm(o, pickb[0:96, :], biasb[0:96, BO_AT:BO_AT + D], stop=False)
                    last = mm(o, yT[:, i * P:(i + 1) * P], wo[:, :], start=False)
                last.then_inc(wo_full, 1)

            def expert_rows(n):
                pe.wait_ge(xs_loaded[n % RING[1]], turn(1, n))
                if n >= 2:
                    pe.wait_ge(e_xT[1], n - 1)
                pe.transpose(TP[n % 2][:, 0:P], row_slots[1][n % RING[1]][:, 0:D], ident).then_inc(e_t[1], 1)

            def expert_hidden(n):
                pe.wait_ge(e_xT[1], n + 1)
                pe.wait_ge(e_w1, n + 1)
                if n >= 2:
                    wait_hidden(pe, n - 2)
                for f in range(2):
                    last = mm(S[0][:, n % 2, f * P:(f + 1) * P], w12r[:, n % W_RING, f * P:(f + 1) * P], xsT[:, n % 2, :])
                last.then_inc(e_h, 1)

            def expert_out(n):
                we = w12r[:, n % W_RING, H1 + 2:W_COLS]
                if n >= 2:
                    pe.wait_ge(e_ys[1], n - 1)
                wait_hidden(pe, n)
                mm(O[n % 2][:, 0:D], hT[:, n % 2, 0, :], we[:, 0:D], stop=False)
                mm(O[n % 2][:, 0:D], hT[:, n % 2, 1, :], we[:, D:2 * D], start=False).then_inc(e_y[1], 1)

            pe.wait_ge(expert_ready, 1)
            for n in range(-2, TILES1):
                if n + 2 < TILES1:
                    expert_rows(n + 2)
                if 0 <= n + 1 < TILES1:
                    expert_hidden(n + 1)
                if 0 <= n:
                    expert_out(n)
                for kind, k in conv_pe_at(n):
                    {"inv": inverse, "yt": transpose_y, "wo": project_y}[kind](k)

        @block.vector
        def _(dve):
            tt, stt, ts = dve.tensor_tensor, dve.scalar_tensor_tensor, dve.tensor_scalar

            def norm_stats(g):
                dve.wait_ge(x_loaded[g], 16)
                for i in range(J * g, J * g + J):
                    dve.bn_stats(stats[:, i, :], xres[:, i, :]).then_inc(stats_done, 1)
                dve.wait_ge(stats_done, J * (g + 1))
                for i in range(J * g, J * g + J):
                    dve.bn_aggr(mv[:, i, :], stats[:, i, :]).then_inc(aggr_done, 1)

            def norm_rows(k, a=0, n=J):
                g = k % B
                dve.wait_ge(rstd_done, J * k + a + n)
                for i in range(J * g + a, J * g + a + n):
                    ts(row[:, i, 0:D], xres[:, i, :], mv[:, i, 0:1], rstd[:, i:i + 1], ALU.subtract,
                       ALU.mult).then_inc(xn_done, 1)

            def norms():
                norm_stats(0)
                for k in range(1, B):
                    norm_stats(k)
                    norm_rows(k - 1)
                norm_rows(B - 1)

            n_rt = [0]

            def rstep(ins):
                ins.then_inc(rt, 1)
                n_rt[0] += 1
                dve.wait_ge(rt, n_rt[0])

            def best_expert(src, rel_out, top, onehot):
                rstep(dve.tensor_reduce(top[:, :], ei(src), X, ALU.max))
                rstep(tt(rel_out[:, :, :], src[:, :, :], over_e(top), ALU.subtract))
                rstep(stt(flat(score), flat(rel_out), 0.0, col("rank"), ALU.is_ge, ALU.mult))
                rstep(dve.tensor_reduce(best[:, :], ei(score), X, ALU.max))
                rstep(tt(onehot[:, :, :], score[:, :, :], over_e(best), ALU.is_equal))

            def inverse_sum(gate):
                rstep(dve.tensor_reduce(best[:, :], ei(expl), X, ALU.add))
                rstep(dve.reciprocal(gate[:, :], best[:, :]))

            def earlier_tokens(k):
                dve.wait_ge(rt_mm, k + 1)
                before, total = O[0][:, 0:E * NT], O[0][:, E * NT:2 * E * NT]
                rstep(dve.tensor_tensor_scan(flat(cum), col("carry"), total, 0.0, ALU.mult, ALU.add))
                rstep(tt(flat(score), flat(cum), total, ALU.subtract))
                rstep(tt(flat(score), flat(score), before, ALU.add))

            n_rad = [0]

            def did(ins):
                ins.then_inc(rad, 1)
                n_rad[0] += 1
                return n_rad[0]

            def after(step):
                dve.wait_ge(rad, step)

            def radix_inverse(a, v):
                p_, m_ = pm[:, 0], pm[:, 1]
                v01_45 = v.rearrange("p (s h x) w -> p s h x w", s=2, h=2)[:, :, 0]
                did(tt(ej[:, :, 0], a[:, 4], a[:, 5], ALU.add))
                yield
                s2 = did(tt(uv[:, :, 0], a[:, 6], a[:, 7], ALU.add))
                yield
                after(s2)
                did(tt(a[:, 5], a[:, 4], a[:, 5], ALU.subtract))
                yield
                s4 = did(tt(a[:, 7], a[:, 6], a[:, 7], ALU.subtract))
                yield
                after(s4)
                did(ts(a[:, 5], a[:, 5], TC, None, ALU.mult))
                yield
                s6 = did(ts(a[:, 7], a[:, 7], TC, None, ALU.mult))
                yield
                did(tt(m_[:, 0:3:2], a[:, 2], a[:, 3], ALU.add))
                yield
                s8 = did(tt(a[:, 3], a[:, 2], a[:, 3], ALU.subtract))
                yield
                after(s6)
                did(stt(ej[:, 0, 1], a[:, 5, 1], TAU, a[:, 5, 0], ALU.mult, ALU.add))
                yield
                did(stt(ej[:, 1, 1], a[:, 5, 0], -TAU, a[:, 5, 1], ALU.mult, ALU.add))
                yield
                did(stt(uv[:, 0, 1], a[:, 7, 0], -TAU, a[:, 7, 1], ALU.mult, ALU.add))
                yield
                s12 = did(stt(uv[:, 1, 1], a[:, 7, 1], -TAU, a[:, 7, 0], ALU.mult, ALU.subtract))
                yield
                did(tt(p_[:, 0], a[:, 0, 0], a[:, 0, 1], ALU.add))
                yield
                s14 = did(tt(p_[:, 1], a[:, 0, 0], a[:, 0, 1], ALU.subtract))
                yield
                after(s14)
                did(tt(v01_45, ej[:, :, :], uv[:, :, :], ALU.add))
                yield
                s16 = did(tt(ej[:, :, :], ej[:, :, :], uv[:, :, :], ALU.subtract))
                yield
                did(tt(m_[:, 1], a[:, 3, 0], a[:, 3, 1], ALU.add))
                yield
                s18 = did(tt(m_[:, 3], a[:, 3, 1], a[:, 3, 0], ALU.subtract))
                yield
                s19 = did(tt(p_[:, 2:4], p_[:, 0:2], a[:, 1], ALU.subtract))
                yield
                after(s19)
                did(tt(p_[:, 0:2], p_[:, 0:2], a[:, 1], ALU.add))
                yield
                s21 = did(tt(m_[:, 3], m_[:, 3], ej[:, 0, 1], ALU.add))
                yield
                did(stt(m_[:, 2], ej[:, 0, 0], RC, m_[:, 2], ALU.mult, ALU.add))
                yield
                s23 = did(stt(p_[:, 2:4], ej[:, 1], RC, p_[:, 2:4], ALU.mult, ALU.add))
                yield
                after(s21)
                s24 = did(ts(m_[:, 1:4:2], m_[:, 1:4:2], RC, None, ALU.mult))
                yield
                after(s24)
                did(tt(ej[:, 0], p_[:, 0:2], m_[:, 0:2], ALU.add))
                yield
                s26 = did(tt(ej[:, 1], p_[:, 0:2], m_[:, 0:2], ALU.subtract))
                yield
                did(tt(v[:, 2:4], p_[:, 2:4], m_[:, 2:4], ALU.add))
                yield
                did(tt(v[:, 6:8], p_[:, 2:4], m_[:, 2:4], ALU.subtract))
                yield
                after(s26)
                did(tt(v01_45, v01_45, ej[:, :, :], ALU.add))
                after(n_rad[0])
                yield

            dve.memset(hg[FO:FO + 1, :], 2.0).then_inc(twos_done, 1)
            dve.memset(pickb[:, :], 0.0).then_inc(pick_done, 1)
            dve.wait_ge(pick_done, 1)
            for r in (0, 32, 64):
                dve.memset(pickb[r:r + 1, :], 1.0).then_inc(pick_done, 1)

            norms()
            dve.wait_ge(vg_free, 16)
            dve.wait_ge(cst_loaded, 16)
            best_expert(lg, rel, m1, oh1)
            rstep(dve.tensor_copy(flat(ohb), flat(oh1)))
            assert n_rt[0] == R0_OH
            dve.wait_ge(rt_exp, 1)
            inverse_sum(gate0)
            earlier_tokens(0)
            assert n_rt[0] == R0_CUM
            rstep(stt(flat(oh2), flat(score), float(CAP), flat(oh1), ALU.is_lt, ALU.mult))
            rstep(tt(flat(score), flat(score), col("e_cap"), ALU.add))
            rstep(stt(flat(score), flat(score), -FAR, flat(oh2), ALU.add, ALU.mult))
            rstep(dve.tensor_reduce(best[:, :], ei(score), X, ALU.add))
            ts(slot0[:, :], best[:, :], FAR, None, ALU.add).then_inc(slot0_ready, 1)
            def rotate(b, h):
                def add(n):
                    u = n % 4
                    dve.wait_ge(rope_mul, 2 * (n + 1))
                    o = qk[b % 2][:, u % 2, 512 * (u // 2):512 * (u // 2) + 512]
                    tt(o, o, rtmp[:, n % 2, :], ALU.add).then_inc(rope_done, 1)

                for u in (2 * h, 2 * h + 1):
                    n = 4 * b + u
                    c = slice(512 * (u // 2), 512 * (u // 2) + 512)
                    dve.wait_ge(pr_full, n + 1)
                    if n >= 2:
                        dve.wait_ge(rope_done, n - 1)
                    slot = S[(n + 1) % 2]
                    tt(qk[b % 2][:, u % 2, c], slot[:, 0, :], rope[:, 0, c], ALU.mult).then_inc(rope_mul, 1)
                    tt(rtmp[:, n % 2, :], slot[:, 1, :], rope[:, 1, c], ALU.mult).then_inc(rope_mul, 1)
                    if u % 2:
                        add(n - 1)
                add(4 * b + 2 * h + 1)

            def row_max(n):
                dve.wait_ge(s_full, n + 1)
                dve.tensor_reduce(negmax[:, n:n + 1],
                                  S[n % 2][:, :, :].rearrange("p a m -> p (a m)")[:, 0:(n % J + 1) * P], X, ALU.max,
                                  negate=True).then_inc(max_done, 1)
                dve.wait_ge(max_done, n + 1)
                ts(negmax[:, n:n + 1], negmax[:, n:n + 1], SCALE, None, ALU.mult).then_inc(bias_done, 1)

            def take_pt(n):
                if n not in SECOND:
                    return
                dve.wait_ge(pt_full, pt_full_at(n, 1))
                dve.wait_ge(o_full, n - 1)
                k = n % J + 1 - 4
                dve.tensor_copy(pT[n % 2][:, 4:4 + k, :].rearrange("p j q -> p (j q)"),
                                t_bank("p", n, 1)[:, 0:k * P]).then_inc(pt_dve, 1)

            def attention_row(n):
                dve.wait_ge(o_full, n + 1)
                dve.wait_ge(rrec_done, n + 1)
                stt(xres[:, n, :], o_bank("o", n)[:, 0:D], rrec[:, n:n + 1], xres[:, n, :], ALU.mult,
                    ALU.add).then_inc(o_done, 1)

            def expert0_bias(e):
                if e >= 2:
                    for k in range(GROUP * (e - 2), GROUP * (e - 1)):
                        wait_sent_back(dve, 0, k)
                dve.wait_ge(e_y[0], e + 1)
                tt(ys[:, GROUP * (e % 2):GROUP * (e % 2 + 1), :], o_bank("y", e)[:, :].rearrange("p (t d) -> p t d", d=D),
                   y0[:, e, :].unsqueeze(1).to_broadcast([P, GROUP, D]), ALU.add).then_inc(e_ys[0], 1)

            def add_experts(i):
                g, j = divmod(i, J)
                dve.wait_ge(y0_loaded, 16 * (g + 1))
                dve.wait_ge(o_done, i + 1)
                stt(xres[:, i, :], y0[:, j, :], gate0[:, i:i + 1], xres[:, i, :], ALU.mult, ALU.add).then_inc(y0_used, 1)

            def tile_stats(i):
                dve.wait_ge(y0_used, i + 1)
                dve.bn_stats(stats[:, i, :], xres[:, i, :]).then_inc(stats_done, 1)

            def tile_aggr(i):
                dve.wait_ge(stats_done, NT + i + 1)
                dve.bn_aggr(mv[:, i, :], stats[:, i, :]).then_inc(aggr_done, 1)

            dve.wait_ge(rope_loaded, 32)
            rotate(0, 0)
            filter_radix = radix_forward(dve, rad_f, [0], filt_v, filt_spec, filt_pm, filt_ej, filt_uv)
            row_max(0)
            for n in range(NT):
                for b, h in projections_at(n):
                    rotate(b, h)
                if n == FILT_RADIX_AT:
                    dve.wait_ge(filt_v_done, J)
                if n + 1 < NT:
                    row_max(n + 1)
                dve.wait_ge(exp_done, n + 1)
                dve.reciprocal(rrec[:, n:n + 1], rsum[:, n:n + 1]).then_inc(rrec_done, 1)
                take_pt(n)
                if n:
                    attention_row(n - 1)
                if FILT_RADIX_AT <= n < FILT_DFT_AT:
                    for _ in range(RAD_F // (FILT_DFT_AT - FILT_RADIX_AT) + 1):
                        next(filter_radix, None)
                if 0 <= n - SPLIT_AT < 2 * len(PARTS) - 1 and (n - SPLIT_AT) % 2:
                    k = (n - SPLIT_AT + 1) // 2
                    dve.wait_ge(split_done, k)
                    tt(bias[PARTS[k], :], bias[PARTS[k], :], biasb[PARTS[k], :], ALU.subtract).then_inc(split_sub, 1)
                for e in expert0_at(n - 1):
                    dve.wait_ge(moe0_w_loaded, 32)
                    expert0_bias(e)
                if n >= ADD_AT and (n - ADD_AT) % 3 == 0 and (n - ADD_AT) // 3 < B - 1:
                    g = (n - ADD_AT) // 3
                    for i in range(J * g, J * g + J):
                        tile_stats(i)
                    for i in range(J * g, J * g + J):
                        tile_aggr(i)
                if n == NT - 4:
                    for stage in (add_experts, tile_stats):
                        for i in range(NT - 8, NT - 4):
                            stage(i)
                if n == NT - 3:
                    for i in range(NT - 8, NT - 4):
                        tile_aggr(i)
                if n == NT - 1:
                    norm_rows(2 * B - 1, 0, J // 2)
                    for i in range(NT - 4, NT - 1):
                        add_experts(i)
            attention_row(NT - 1)
            add_experts(NT - 1)
            for stage in (tile_stats, tile_aggr):
                for i in range(NT - 4, NT):
                    stage(i)
            norm_rows(2 * B - 1, J // 2, J // 2)

            dve.wait_ge(lg1_done, B)
            assert n_rt[0] == R1_FIRST
            best_expert(lg, rel, m1, oh1)
            rstep(stt(flat(score), flat(oh1), -1e30, flat(rel), ALU.mult, ALU.add))
            rstep(dve.tensor_reduce(m2[:, :], ei(score), X, ALU.max))
            rstep(tt(score[:, :, :], score[:, :, :], over_e(m2), ALU.subtract))
            rstep(stt(flat(score), flat(score), 0.0, col("rank"), ALU.is_ge, ALU.mult))
            rstep(dve.tensor_reduce(best[:, :], ei(score), X, ALU.max))
            rstep(tt(oh2[:, :, :], score[:, :, :], over_e(best), ALU.is_equal))
            rstep(tt(flat(ohb), flat(oh1), flat(oh2), ALU.add))
            assert n_rt[0] == R1_OH, n_rt
            dve.wait_ge(rt_exp, 3)
            inverse_sum(gate1)
            rstep(tt(gate2[:, :], em2[:, :], gate1[:, :], ALU.mult))
            earlier_tokens(1)
            assert n_rt[0] == R1_CUM, n_rt
            rstep(ts(cnt_i[:, :], cum[:, :, NT - 1], float(P - 1), None, ALU.add))
            rstep(ts(cnt_t[:, :], cnt_i[:, :], 7, None, ALU.arith_shift_right))
            rstep(dve.tensor_copy(ntile[:, :], cnt_t[:, :]))
            dve.wait_ge(ones_done, 2)
            rstep(dve.tensor_tensor_scan(ctile[:, :], ones8[:, :], ntile[:, :], 0.0, ALU.mult, ALU.add))
            rstep(tt(base[:, :], ctile[:, :], ntile[:, :], ALU.subtract))
            rstep(stt(score[:, :, :], base[:, :].unsqueeze(2).to_broadcast([P, E, NT]), float(P), score[:, :, :],
                      ALU.mult, ALU.add))
            for o, onehot, m in ((slot1, oh1, m1), (slot2, oh2, m2)):
                rstep(tt(flat(rel), flat(score), flat(onehot), ALU.mult))
                rstep(dve.tensor_reduce(m[:, :], ei(rel), X, ALU.add))
                dve.tensor_copy(o[:, :], m[:, :]).then_inc(slot1_ready, 1)
            rstep(tt(ecmp[:, :, :], ctile[0:1, :].unsqueeze(1).to_broadcast([1, TILES1, E]),
                     cst[0:1, CONST["tile_no"][0]:CONST["tile_no"][1]].rearrange("p (n e) -> p n e", e=E), ALU.is_le))
            rstep(dve.tensor_reduce(ecnt[:, :], ecmp[:, :, :], X, ALU.add))
            ts(expert[:, :], ecnt[:, :], float(E - 1), None, ALU.min).then_inc(expert_ready, 1)

            def product(u):
                hf, c = divmod(u, NC)
                dve.wait_ge(x_full, u + 1)
                if u >= 2:
                    dve.wait_ge(y_ready, u - 1)
                t_ = prod[u % 2]
                for a in range(2):
                    shape, x_ = ([P, 2, 2, D], "p (a b d) -> p a b d") if c == 0 else ([P, 4, D], "p (a d) -> p a d")
                    kw = dict(a=2, d=D) if c == 0 else dict(d=D)
                    h_ = hspec0[:, a, :, :].unsqueeze(2) if c == 0 else hspec[:, c, a, :].unsqueeze(1)
                    o_ = t_[a].rearrange("p a w -> p (a w)").rearrange(x_, **kw)
                    tt(o_, SB[u % 4].rearrange(x_, **kw), h_.to_broadcast(shape), ALU.mult).then_inc((pmul, x_free)[a], 1)
                dve.wait_ge(pmul, u + 1)
                dve.wait_ge(x_free, u + 1)
                y = spec[hf][:, c]
                tt(y[:, 0], t_[0][:, 0], t_[1][:, 1], ALU.subtract)
                tt(y[:, 1], t_[0][:, 1], t_[1][:, 0], ALU.add).then_inc(y_ready, 1)

            dve.wait_ge(uv_taken, 4)
            for _ in radix_forward(dve, rad, n_rad, vv[0], spec[0], pm, ej, uv):
                pass
            dve.wait_ge(hspec_done, 4)
            dve.wait_ge(uv_taken, 16)
            second = radix_forward(dve, rad, n_rad, vv[1], spec[1], pm, ej, uv)
            for u in range(2 * NC):
                product(u)
                for _ in range(RADIX_PIECES):
                    next(second, None)

            def convolution_back():
                dve.wait_ge(y_ready, 2 * NC)
                for hf in range(HALF):
                    dve.wait_ge(b_free, NC * (hf + 1))
                    yield from radix_inverse(spec[hf], vv[hf])
                    for b in range(2 * hf, 2 * hf + 2):
                        v_ = vv[hf][:, :, (b % 2) * D:(b % 2 + 1) * D]
                        tt(v_, v_, uu[:, J * b:J * b + J, :], ALU.mult).then_inc(conv_done, 1)
                        yield

            def add_y(q):
                dve.wait_ge(wo_full, q + 1)
                r_ = xres[:, 4 * q:4 * q + 4, :]
                tt(r_, c_bank("wo", q).rearrange("p (t d) -> p t d", d=D), r_, ALU.add).then_inc(wo_done, 1)

            def expert1_hidden(n):
                dve.wait_ge(e_h, n + 1)
                if n >= 2:
                    dve.wait_ge(e_y[1], n - 1)
                for f in range(2):
                    last = ts(hT[:, n % 2, f, :], S[0][:, n % 2, f * P:(f + 1) * P],
                              w12r[:, n % W_RING, H1 + f:H1 + f + 1], 0.0, ALU.add, ALU.max)
                last.then_inc(e_hd, 1)

            def expert1_out(n):
                m = n % UNROLL
                e = dve.value_load(expert[0:1, n:n + 1], min_val=0, max_val=E - 1)
                if n >= UNROLL:
                    wait_sent_back(dve, 1, n - UNROLL)
                dve.wait_ge(e_y[1], n + 1)
                tt(ys[:, m, :], O[n % 2][:, 0:D], b2[:, bass.ds(e, 1), :].rearrange("p e d -> p (e d)"),
                   ALU.add).then_inc(e_ys[1], 1)

            dve.wait_ge(expert_ready, 1)
            dve.wait_ge(b2_loaded, 32)
            back = convolution_back()
            for n in range(-1, TILES1):
                if n + 1 < TILES1 and not n % 2:
                    expert1_hidden(n + 1)
                if n >= 0:
                    expert1_out(n)
                for _ in range(conv_dve_at(n)):
                    next(back)
                for kind, k in conv_pe_at(n):
                    if kind == "wo":
                        add_y(k)
            assert next(back, None) is None
            for m, q in enumerate(q for q in range(NT // 4) if q not in POOL_SUMS):
                dve.wait_ge(back_loaded[q], 16)
                r_ = xres[:, 4 * q:4 * q + 4, :]
                for t in range(4):
                    i = 4 * q + t
                    last = stt(xres[:, i, :], moe_back[q][:, t, 0, :], gate1[:, i:i + 1], xres[:, i, :], ALU.mult, ALU.add)
                last.then_inc(out_a, 1)
                dve.wait_ge(out_a, m + 1)
                dve.wait_ge(gated2, q + 1)
                tt(r_, r_, moe_back[q][:, :, 1, :], ALU.add).then_inc(out_ready, 1)


def kernel(**inputs):
    import concourse.bacc as bacc
    from concourse.bass_utils import run_bass_kernel_spmd

    a = {k: np.asarray(v) for k, v in inputs.items()}
    fw, iv = dft_matrices()
    wq, wk = a["L0_attn_w_q"], a["L0_attn_w_k"]
    swap = np.arange(D) ^ 1
    args = {
        "x": a["L0_attn_x"],
        "cst": constants(),
        "rope": rope_tables(),
        "fw": fw,
        "iv": iv,
        "pe": position_table(),
        "wqk": np.concatenate([wq.T, wq[swap].T, wk.T, wk[swap].T], 1),
        "wvg": np.concatenate([a["L0_attn_w_v"].T, a["L0_ffn_wg"]], 1),
        "w0": a["L0_ffn_W"].transpose(2, 0, 1),
        "b0": a["L0_ffn_b"],
        "fsmall": np.concatenate([
            np.pad(np.concatenate([a["L1_attn_W1"], a["L1_attn_W2"]], 1), ((0, 1), (0, 0))),
            np.concatenate([a["L1_attn_W3"], a["L1_attn_b3"][None]], 0),
            np.pad(np.stack([a["L1_attn_b1"], a["L1_attn_b2"]], 1), ((0, 1), (0, 0)))], 1),
        "wv": a["L1_attn_Wv"],
        "wu": a["L1_attn_Wu"],
        "wg1": a["L1_ffn_Wg"],
        "bvuo": np.concatenate([a["L1_attn_bv"], a["L1_attn_bu"], a["L1_attn_bo"]]),
        "wo": a["L1_attn_Wo"],
        "w1": a["L1_ffn_W1"],
        "b1": a["L1_ffn_b1"].reshape(E, 2, P).transpose(2, 0, 1),
        "w2": a["L1_ffn_W2"],
        "b2": a["L1_ffn_b2"],
    }
    nc = bacc.Bacc("TRN2", target_bir_lowering=False, num_devices=1)
    arrays, aps = {}, []
    for name, v in args.items():
        v = np.ascontiguousarray(v)
        arrays[f"in_{name}"] = v
        aps.append(nc.dram_tensor(f"in_{name}", v.shape, mybir.dt.from_np(v.dtype), kind="ExternalInput").ap())
    aps.append(nc.dram_tensor("out", (B, L, D), F32, kind="ExternalOutput").ap())
    two_layer_kernel(nc, *aps)
    return run_bass_kernel_spmd(nc, [arrays], core_ids=[0]).results[0]["out"]
```
